# Optimizing a Trainium2 kernel written in Bass

```python
import numpy as np
import jax
import jax.numpy as jnp

def _softmax(x, axis=-1):
    return jax.nn.softmax(x, axis=axis)

def _gelu(x):
    return jax.nn.gelu(x, approximate=True)

def _silu(x):
    return jax.nn.silu(x)

def _sigmoid(x):
    return jax.nn.sigmoid(x)

def _layernorm(x, axis=-1, eps=1e-05):
    m = jnp.mean(x, axis=axis, keepdims=True)
    v = jnp.var(x, axis=axis, keepdims=True)
    return (x - m) / jnp.sqrt(v + eps)

def _scatter_add(tgt, idx, src, axis=0):
    return tgt.at[idx].add(src)

def _segment_sum(src, seg, n):
    return jax.ops.segment_sum(src, seg, n)
kernel_name = 'mk_gps_d2_gnn_r32_278173'

def setup_inputs(seed: int=0):
    np.random.seed(seed)
    _w = jnp.asarray

    def _rec_inputs():
        import jax
        import jax.numpy as jnp
        _gk = jax.random.key(seed)
        x = -0.0002117 + 1 * jax.random.normal(jax.random.fold_in(_gk, 1), (3125, 256), jnp.float32)
        _s = jax.random.randint(jax.random.fold_in(_gk, 2), (25000,), 0, 3125, jnp.int32)
        _d = jax.random.randint(jax.random.fold_in(_gk, 3), (25000,), 0, 3125, jnp.int32)
        _loop = jnp.arange(3125, dtype=jnp.int32)
        src = jnp.concatenate([_s, _d, _loop])
        dst = jnp.concatenate([_d, _s, _loop])
        _o = jnp.argsort(dst, stable=True)
        src = src[_o]
        dst = dst[_o]
        edge_weight = jax.random.uniform(jax.random.fold_in(_gk, 13), (53125,), jnp.float32, 0.0, 1)
        return (x, src, dst, edge_weight)
    x, src, dst, edge_weight = _rec_inputs()

    def _L0_gnn_setup():
        import jax, jax.numpy as jnp
        import numpy as np
        N_NODES = 3125
        N_EDGES = 100000
        D_IN = 256
        D_OUT = 256
        key = jax.random.key(seed)
        k1, k2, k3, k4, k5, k6 = jax.random.split(key, 6)
        X = jax.random.normal(k1, (N_NODES, D_IN), dtype=jnp.float32)
        edge_src = jax.random.randint(k2, (N_EDGES,), 0, N_NODES, dtype=jnp.int32)
        edge_dst = jax.random.randint(k3, (N_EDGES,), 0, N_NODES, dtype=jnp.int32)
        edge_vals = jax.random.uniform(k4, (N_EDGES,), dtype=jnp.float32)
        W = jax.random.normal(k5, (D_IN, D_OUT), dtype=jnp.float32) * (1.0 / np.sqrt(D_IN))
        b = jax.random.normal(k6, (D_OUT,), dtype=jnp.float32) * 0.01
        return {'X': X, 'edge_src': edge_src, 'edge_dst': edge_dst, 'edge_vals': edge_vals, 'W': W, 'b': b}
    _L0_gnn_all = _L0_gnn_setup()
    _L0_gnn_in = {k: v for k, v in _L0_gnn_all.items() if k in ('W', 'b')}
    del _L0_gnn_all

    def _L0_mix_setup():
        import jax, jax.numpy as jnp
        import numpy as np
        DIM = 256
        HEADS = 4
        DIM_HEAD = 32
        NUM_MEM = 4
        HIDDEN = HEADS * DIM_HEAD
        SCALE = DIM_HEAD ** (-0.5)

        def rmsnorm(x, g):
            n = jnp.linalg.norm(x, axis=-1, keepdims=True)
            return x / jnp.maximum(n, 1e-12) * g * x.shape[-1] ** 0.5
        key = jax.random.key(seed)
        ks = jax.random.split(key, 8)
        B, N = (4, 512)
        return {'x': jax.random.normal(ks[0], (B, N, DIM), jnp.float32), 't': jax.random.normal(ks[1], (B,), jnp.float32), 'w_qkv': jax.random.normal(ks[2], (DIM, 3 * HIDDEN), jnp.float32) * 0.02, 'mem_kv': jax.random.normal(ks[3], (2, HEADS, DIM_HEAD, NUM_MEM), jnp.float32), 'w_out': jax.random.normal(ks[4], (HIDDEN, DIM), jnp.float32) * 0.02, 'b_out': jnp.zeros((DIM,), jnp.float32), 'g_out': jnp.ones((DIM,), jnp.float32), 'g_pre': jnp.ones((DIM,), jnp.float32)}
    _L0_mix_all = _L0_mix_setup()
    _L0_mix_in = {k: v for k, v in _L0_mix_all.items() if k in ('t', 'w_qkv', 'mem_kv', 'w_out', 'b_out', 'g_out', 'g_pre')}
    del _L0_mix_all

    def _L0_ffn_setup():
        import jax, jax.numpy as jnp
        import numpy as np
        NUM_EXPERTS = 8
        TOP_K = 2
        B, S, D = (8, 256, 256)

        def _moe(tokens, router_w, w1, b1, w2, b2):
            N = tokens.shape[0]
            E = router_w.shape[0]
            logits = tokens.astype(jnp.float32) @ router_w.astype(jnp.float32).T
            probs = jax.nn.softmax(logits, axis=-1)
            rw, re = jax.lax.top_k(probs, TOP_K)
            if TOP_K > 1:
                rw = rw / jnp.maximum(rw.sum(-1, keepdims=True), 1e-12)
            rw = rw.astype(tokens.dtype)
            combine = jnp.zeros((N, E), tokens.dtype).at[jnp.arange(N)[:, None], re].set(rw)
            out = tokens
            for e in range(E):
                h = jax.nn.gelu(tokens @ w1[e] + b1[e], approximate=False)
                y = h @ w2[e] + b2[e]
                out = out + combine[:, e:e + 1] * y
            return out
        key = jax.random.key(seed)
        ks = jax.random.split(key, 4)
        scale = 1.0 / np.sqrt(D).astype(np.float32)
        return {'input_embeddings': jax.random.normal(ks[0], (B, S, D), jnp.float32), 'router_w': jax.random.normal(ks[1], (NUM_EXPERTS, D), jnp.float32) * scale, 'w1': jax.random.normal(ks[2], (NUM_EXPERTS, D, D), jnp.float32) * scale, 'b1': jnp.zeros((NUM_EXPERTS, D), jnp.float32), 'w2': jax.random.normal(ks[3], (NUM_EXPERTS, D, D), jnp.float32) * scale, 'b2': jnp.zeros((NUM_EXPERTS, D), jnp.float32)}
    _L0_ffn_all = _L0_ffn_setup()
    _L0_ffn_in = {k: v for k, v in _L0_ffn_all.items() if k in ('router_w', 'w1', 'b1', 'w2', 'b2')}
    del _L0_ffn_all

    def _L1_gnn_setup():
        import jax, jax.numpy as jnp
        import numpy as np
        N_NODES = 50000
        N_EDGES = 10000
        D_IN = 256
        D_OUT = 256
        key = jax.random.key(seed)
        k1, k2, k3, k4, k5, k6, k7 = jax.random.split(key, 7)
        s = 1.0 / np.sqrt(D_IN)
        return {'node_features': jax.random.normal(k1, (N_NODES, D_IN), dtype=jnp.float32), 'edge_index': jax.random.randint(k2, (2, N_EDGES), 0, N_NODES, dtype=jnp.int64), 'w1': jax.random.uniform(k3, (D_OUT, D_IN), jnp.float32, -s, s), 'w2': jax.random.uniform(k4, (D_OUT, D_IN), jnp.float32, -s, s), 'w3': jax.random.uniform(k5, (D_OUT, D_IN), jnp.float32, -s, s), 'b3': jax.random.uniform(k6, (D_OUT,), jnp.float32, -s, s)}
    _L1_gnn_all = _L1_gnn_setup()
    _L1_gnn_in = {k: v for k, v in _L1_gnn_all.items() if k in ('w1', 'w2', 'w3', 'b3')}
    del _L1_gnn_all

    def _L1_mix_setup():
        import jax, jax.numpy as jnp
        import numpy as np
        B, N, C = (8, 256, 256)
        H, D, S = (8, 32, 32)
        HID = 4 * C

        def layernorm(x, w, b, eps=1e-05):
            mu = jnp.mean(x, axis=-1, keepdims=True)
            var = jnp.mean(jnp.square(x - mu), axis=-1, keepdims=True)
            return (x - mu) * jax.lax.rsqrt(var + eps) * w + b

        def linear_no_attn(x, Wx, bx, Wq, Wk, Wv, Wo, bo):
            x_mid = x @ Wx.T + bx
            x_mid = x_mid.reshape(x.shape[0], x.shape[1], H, D).transpose(0, 2, 1, 3)
            q = jax.nn.softmax(x_mid @ Wq.T, axis=-1)
            k = jax.nn.softmax(x_mid @ Wk.T, axis=-2)
            v = x_mid @ Wv.T
            kv = jnp.einsum('bhns,bhnd->bhsd', k, v)
            qkv = jnp.einsum('bhns,bhsd->bhnd', q, kv)
            qkv = qkv.transpose(0, 2, 1, 3).reshape(x.shape[0], x.shape[1], H * D)
            return qkv @ Wo.T + bo
        key = jax.random.key(seed)
        ks = jax.random.split(key, 16)
        s = lambda fan: 1.0 / np.sqrt(fan)
        return {'fx': jax.random.normal(ks[0], (B, N, C), jnp.float32), 'ln1_w': jnp.ones((C,), jnp.float32), 'ln1_b': jnp.zeros((C,), jnp.float32), 'Wx': jax.random.uniform(ks[1], (C, C), jnp.float32, -s(C), s(C)), 'bx': jax.random.uniform(ks[2], (C,), jnp.float32, -s(C), s(C)), 'Wq': jax.random.uniform(ks[3], (S, D), jnp.float32, -s(D), s(D)), 'Wk': jax.random.uniform(ks[4], (S, D), jnp.float32, -s(D), s(D)), 'Wv': jax.random.uniform(ks[5], (D, D), jnp.float32, -s(D), s(D)), 'Wo': jax.random.uniform(ks[6], (C, C), jnp.float32, -s(C), s(C)), 'bo': jax.random.uniform(ks[7], (C,), jnp.float32, -s(C), s(C)), 'ln2_w': jnp.ones((C,), jnp.float32), 'ln2_b': jnp.zeros((C,), jnp.float32), 'W1': jax.random.uniform(ks[8], (HID, C), jnp.float32, -s(C), s(C)), 'b1': jax.random.uniform(ks[9], (HID,), jnp.float32, -s(C), s(C)), 'W2': jax.random.uniform(ks[10], (C, HID), jnp.float32, -s(HID), s(HID)), 'b2': jax.random.uniform(ks[11], (C,), jnp.float32, -s(HID), s(HID))}
    _L1_mix_all = _L1_mix_setup()
    _L1_mix_in = {k: v for k, v in _L1_mix_all.items() if k in ('ln1_w', 'ln1_b', 'Wx', 'bx', 'Wq', 'Wk', 'Wv', 'Wo', 'bo', 'ln2_w', 'ln2_b', 'W1', 'b1', 'W2', 'b2')}
    del _L1_mix_all

    def _L1_ffn_setup():
        import jax, jax.numpy as jnp
        import numpy as np
        DIM = 256
        H = 8
        D = 64
        G = 64
        INNER = H * D
        SCALE = D ** (-0.5)
        key = jax.random.key(seed)
        ks = jax.random.split(key, 12)
        B, N = (4, 512)
        x = jax.random.normal(ks[0], (B, N, DIM), dtype=jnp.float32)
        s = lambda fan_in: 1.0 / np.sqrt(fan_in)
        W_fx = jax.random.normal(ks[1], (DIM, INNER), dtype=jnp.float32) * s(DIM)
        b_fx = jnp.zeros((INNER,), dtype=jnp.float32)
        W_x = jax.random.normal(ks[2], (DIM, INNER), dtype=jnp.float32) * s(DIM)
        b_x = jnp.zeros((INNER,), dtype=jnp.float32)
        A = jax.random.normal(ks[3], (G, D), dtype=jnp.float32)
        Q, _ = jnp.linalg.qr(A.T)
        W_slice = Q[:, :G].astype(jnp.float32)
        b_slice = jnp.zeros((G,), dtype=jnp.float32)
        W_q = jax.random.normal(ks[4], (D, D), dtype=jnp.float32) * s(D)
        W_k = jax.random.normal(ks[5], (D, D), dtype=jnp.float32) * s(D)
        W_v = jax.random.normal(ks[6], (D, D), dtype=jnp.float32) * s(D)
        W_out = jax.random.normal(ks[7], (INNER, DIM), dtype=jnp.float32) * s(INNER)
        b_out = jnp.zeros((DIM,), dtype=jnp.float32)
        temperature = jnp.ones((1, H, 1, 1), dtype=jnp.float32) * 0.5
        return {'x': x, 'W_fx': W_fx, 'b_fx': b_fx, 'W_x': W_x, 'b_x': b_x, 'W_slice': W_slice, 'b_slice': b_slice, 'W_q': W_q, 'W_k': W_k, 'W_v': W_v, 'W_out': W_out, 'b_out': b_out, 'temperature': temperature}
    _L1_ffn_all = _L1_ffn_setup()
    _L1_ffn_in = {k: v for k, v in _L1_ffn_all.items() if k in ('W_fx', 'b_fx', 'W_x', 'b_x', 'W_slice', 'b_slice', 'W_q', 'W_k', 'W_v', 'W_out', 'b_out', 'temperature')}
    del _L1_ffn_all
    return {'x': x, 'src': src, 'dst': dst, 'edge_weight': edge_weight, 'L0_gnn_W': _L0_gnn_in['W'], 'L0_gnn_b': _L0_gnn_in['b'], 'L0_mix_t': _L0_mix_in['t'], 'L0_mix_w_qkv': _L0_mix_in['w_qkv'], 'L0_mix_mem_kv': _L0_mix_in['mem_kv'], 'L0_mix_w_out': _L0_mix_in['w_out'], 'L0_mix_b_out': _L0_mix_in['b_out'], 'L0_mix_g_out': _L0_mix_in['g_out'], 'L0_mix_g_pre': _L0_mix_in['g_pre'], 'L0_ffn_router_w': _L0_ffn_in['router_w'], 'L0_ffn_w1': _L0_ffn_in['w1'], 'L0_ffn_b1': _L0_ffn_in['b1'], 'L0_ffn_w2': _L0_ffn_in['w2'], 'L0_ffn_b2': _L0_ffn_in['b2'], 'L1_gnn_w1': _L1_gnn_in['w1'], 'L1_gnn_w2': _L1_gnn_in['w2'], 'L1_gnn_w3': _L1_gnn_in['w3'], 'L1_gnn_b3': _L1_gnn_in['b3'], 'L1_mix_ln1_w': _L1_mix_in['ln1_w'], 'L1_mix_ln1_b': _L1_mix_in['ln1_b'], 'L1_mix_Wx': _L1_mix_in['Wx'], 'L1_mix_bx': _L1_mix_in['bx'], 'L1_mix_Wq': _L1_mix_in['Wq'], 'L1_mix_Wk': _L1_mix_in['Wk'], 'L1_mix_Wv': _L1_mix_in['Wv'], 'L1_mix_Wo': _L1_mix_in['Wo'], 'L1_mix_bo': _L1_mix_in['bo'], 'L1_mix_ln2_w': _L1_mix_in['ln2_w'], 'L1_mix_ln2_b': _L1_mix_in['ln2_b'], 'L1_mix_W1': _L1_mix_in['W1'], 'L1_mix_b1': _L1_mix_in['b1'], 'L1_mix_W2': _L1_mix_in['W2'], 'L1_mix_b2': _L1_mix_in['b2'], 'L1_ffn_W_fx': _L1_ffn_in['W_fx'], 'L1_ffn_b_fx': _L1_ffn_in['b_fx'], 'L1_ffn_W_x': _L1_ffn_in['W_x'], 'L1_ffn_b_x': _L1_ffn_in['b_x'], 'L1_ffn_W_slice': _L1_ffn_in['W_slice'], 'L1_ffn_b_slice': _L1_ffn_in['b_slice'], 'L1_ffn_W_q': _L1_ffn_in['W_q'], 'L1_ffn_W_k': _L1_ffn_in['W_k'], 'L1_ffn_W_v': _L1_ffn_in['W_v'], 'L1_ffn_W_out': _L1_ffn_in['W_out'], 'L1_ffn_b_out': _L1_ffn_in['b_out'], 'L1_ffn_temperature': _L1_ffn_in['temperature']}

def reference(x, src, dst, edge_weight, L0_gnn_W, L0_gnn_b, L0_mix_t, L0_mix_w_qkv, L0_mix_mem_kv, L0_mix_w_out, L0_mix_b_out, L0_mix_g_out, L0_mix_g_pre, L0_ffn_router_w, L0_ffn_w1, L0_ffn_b1, L0_ffn_w2, L0_ffn_b2, L1_gnn_w1, L1_gnn_w2, L1_gnn_w3, L1_gnn_b3, L1_mix_ln1_w, L1_mix_ln1_b, L1_mix_Wx, L1_mix_bx, L1_mix_Wq, L1_mix_Wk, L1_mix_Wv, L1_mix_Wo, L1_mix_bo, L1_mix_ln2_w, L1_mix_ln2_b, L1_mix_W1, L1_mix_b1, L1_mix_W2, L1_mix_b2, L1_ffn_W_fx, L1_ffn_b_fx, L1_ffn_W_x, L1_ffn_b_x, L1_ffn_W_slice, L1_ffn_b_slice, L1_ffn_W_q, L1_ffn_W_k, L1_ffn_W_v, L1_ffn_W_out, L1_ffn_b_out, L1_ffn_temperature):
    import jax
    import jax.numpy as jnp

    def _L0_gnn_ref(X, edge_src, edge_dst, edge_vals, W, b):
        import jax, jax.numpy as jnp
        import numpy as np
        N_NODES = 3125
        N_EDGES = 100000
        D_IN = 256
        D_OUT = 256
        msgs = edge_vals[:, None] * X[edge_src]
        H = jax.ops.segment_sum(msgs, edge_dst, num_segments=N_NODES)
        H = jnp.dot(H, W) + b
        return jax.nn.relu(H)

    def _L0_mix_ref(x, t, w_qkv, mem_kv, w_out, b_out, g_out, g_pre):
        import jax, jax.numpy as jnp
        import numpy as np
        DIM = 256
        HEADS = 4
        DIM_HEAD = 32
        NUM_MEM = 4
        HIDDEN = HEADS * DIM_HEAD
        SCALE = DIM_HEAD ** (-0.5)

        def rmsnorm(x, g):
            n = jnp.linalg.norm(x, axis=-1, keepdims=True)
            return x / jnp.maximum(n, 1e-12) * g * x.shape[-1] ** 0.5
        b, n, c = x.shape
        xn = rmsnorm(x, g_pre)
        qkv = xn @ w_qkv
        q, k, v = jnp.split(qkv, 3, axis=-1)

        def to_heads(z):
            return z.reshape(b, n, HEADS, DIM_HEAD).transpose(0, 2, 3, 1)
        q, k, v = map(to_heads, (q, k, v))
        mk = jnp.broadcast_to(mem_kv[0], (b, HEADS, DIM_HEAD, NUM_MEM))
        mv = jnp.broadcast_to(mem_kv[1], (b, HEADS, DIM_HEAD, NUM_MEM))
        k = jnp.concatenate([mk, k], axis=-1)
        v = jnp.concatenate([mv, v], axis=-1)
        q = jax.nn.softmax(q, axis=-2) * SCALE
        k = jax.nn.softmax(k, axis=-1)
        context = jnp.einsum('bhdn,bhen->bhde', k, v)
        out = jnp.einsum('bhde,bhdn->bhen', context, q)
        out = out.transpose(0, 3, 1, 2).reshape(b, n, HIDDEN)
        out = rmsnorm(out @ w_out + b_out, g_out)
        return out + x

    def _L0_ffn_ref(input_embeddings, router_w, w1, b1, w2, b2):
        import jax, jax.numpy as jnp
        import numpy as np
        NUM_EXPERTS = 8
        TOP_K = 2
        B, S, D = (8, 256, 256)

        def _moe(tokens, router_w, w1, b1, w2, b2):
            N = tokens.shape[0]
            E = router_w.shape[0]
            logits = tokens.astype(jnp.float32) @ router_w.astype(jnp.float32).T
            probs = jax.nn.softmax(logits, axis=-1)
            rw, re = jax.lax.top_k(probs, TOP_K)
            if TOP_K > 1:
                rw = rw / jnp.maximum(rw.sum(-1, keepdims=True), 1e-12)
            rw = rw.astype(tokens.dtype)
            combine = jnp.zeros((N, E), tokens.dtype).at[jnp.arange(N)[:, None], re].set(rw)
            out = tokens
            for e in range(E):
                h = jax.nn.gelu(tokens @ w1[e] + b1[e], approximate=False)
                y = h @ w2[e] + b2[e]
                out = out + combine[:, e:e + 1] * y
            return out
        b, s, d = input_embeddings.shape
        tokens = input_embeddings.reshape(b * s, d)
        return _moe(tokens, router_w, w1, b1, w2, b2).reshape(b, s, d)

    def _L1_gnn_ref(node_features, edge_index, w1, w2, w3, b3):
        import jax, jax.numpy as jnp
        import numpy as np
        N_NODES = 50000
        N_EDGES = 10000
        D_IN = 256
        D_OUT = 256
        n = node_features.shape[0]
        proj = node_features @ w3.T + b3
        msgs = proj[edge_index[0]]
        agg = jax.ops.segment_sum(msgs, edge_index[1], num_segments=n)
        out = node_features @ w1.T + agg @ w2.T
        return out

    def _L1_mix_ref(fx, ln1_w, ln1_b, Wx, bx, Wq, Wk, Wv, Wo, bo, ln2_w, ln2_b, W1, b1, W2, b2):
        import jax, jax.numpy as jnp
        import numpy as np
        B, N, C = (8, 256, 256)
        H, D, S = (8, 32, 32)
        HID = 4 * C

        def layernorm(x, w, b, eps=1e-05):
            mu = jnp.mean(x, axis=-1, keepdims=True)
            var = jnp.mean(jnp.square(x - mu), axis=-1, keepdims=True)
            return (x - mu) * jax.lax.rsqrt(var + eps) * w + b

        def linear_no_attn(x, Wx, bx, Wq, Wk, Wv, Wo, bo):
            x_mid = x @ Wx.T + bx
            x_mid = x_mid.reshape(x.shape[0], x.shape[1], H, D).transpose(0, 2, 1, 3)
            q = jax.nn.softmax(x_mid @ Wq.T, axis=-1)
            k = jax.nn.softmax(x_mid @ Wk.T, axis=-2)
            v = x_mid @ Wv.T
            kv = jnp.einsum('bhns,bhnd->bhsd', k, v)
            qkv = jnp.einsum('bhns,bhsd->bhnd', q, kv)
            qkv = qkv.transpose(0, 2, 1, 3).reshape(x.shape[0], x.shape[1], H * D)
            return qkv @ Wo.T + bo
        h = linear_no_attn(layernorm(fx, ln1_w, ln1_b), Wx, bx, Wq, Wk, Wv, Wo, bo) + fx
        y = layernorm(h, ln2_w, ln2_b)
        y = jax.nn.gelu(y @ W1.T + b1, approximate=False)
        y = y @ W2.T + b2
        return y + h

    def _L1_ffn_ref(x, W_fx, b_fx, W_x, b_x, W_slice, b_slice, W_q, W_k, W_v, W_out, b_out, temperature):
        import jax, jax.numpy as jnp
        import numpy as np
        DIM = 256
        H = 8
        D = 64
        G = 64
        INNER = H * D
        SCALE = D ** (-0.5)
        B, N, _ = x.shape
        fx_mid = (x @ W_fx + b_fx).reshape(B, N, H, D).transpose(0, 2, 1, 3)
        x_mid = (x @ W_x + b_x).reshape(B, N, H, D).transpose(0, 2, 1, 3)
        temp = jnp.clip(temperature, 0.1, 5.0)
        slice_weights = jax.nn.softmax((x_mid @ W_slice + b_slice) / temp, axis=-1)
        slice_norm = slice_weights.sum(axis=2)
        slice_token = jnp.einsum('bhnc,bhng->bhgc', fx_mid, slice_weights)
        slice_token = slice_token / (slice_norm[..., None] + 1e-05)
        q = slice_token @ W_q
        k = slice_token @ W_k
        v = slice_token @ W_v
        attn = jax.nn.softmax(jnp.einsum('bhgc,bhkc->bhgk', q, k) * SCALE, axis=-1)
        out_slice = jnp.einsum('bhgk,bhkc->bhgc', attn, v)
        out_x = jnp.einsum('bhgc,bhng->bhnc', out_slice, slice_weights)
        out_x = out_x.transpose(0, 2, 1, 3).reshape(B, N, INNER)
        return out_x @ W_out + b_out
    edge_index = jnp.stack([src, dst])
    xn = _layernorm(x, axis=-1)
    x = x + _L0_gnn_ref(xn, src, dst, edge_weight, L0_gnn_W, L0_gnn_b) + _L0_mix_ref(xn[None], L0_mix_t, L0_mix_w_qkv, L0_mix_mem_kv, L0_mix_w_out, L0_mix_b_out, L0_mix_g_out, L0_mix_g_pre)[0]
    x = x + _L0_ffn_ref(_layernorm(x, axis=-1)[None], L0_ffn_router_w, L0_ffn_w1, L0_ffn_b1, L0_ffn_w2, L0_ffn_b2)[0]
    xn = _layernorm(x, axis=-1)
    x = x + _L1_gnn_ref(xn, edge_index, L1_gnn_w1, L1_gnn_w2, L1_gnn_w3, L1_gnn_b3) + _L1_mix_ref(xn[None], L1_mix_ln1_w, L1_mix_ln1_b, L1_mix_Wx, L1_mix_bx, L1_mix_Wq, L1_mix_Wk, L1_mix_Wv, L1_mix_Wo, L1_mix_bo, L1_mix_ln2_w, L1_mix_ln2_b, L1_mix_W1, L1_mix_b1, L1_mix_W2, L1_mix_b2)[0]
    x = x + _L1_ffn_ref(_layernorm(x, axis=-1)[None], L1_ffn_W_fx, L1_ffn_b_fx, L1_ffn_W_x, L1_ffn_b_x, L1_ffn_W_slice, L1_ffn_b_slice, L1_ffn_W_q, L1_ffn_W_k, L1_ffn_W_v, L1_ffn_W_out, L1_ffn_b_out, L1_ffn_temperature)[0]
    return x

_drawn_inputs = setup_inputs


def setup_inputs(seed=0):
    import zlib

    import numpy as np

    out = dict(_drawn_inputs(seed))
    spreads = {'L0_mix_b_out': (0.0, 0.1),
     'L0_mix_g_out': (1.0, 0.2),
     'L0_mix_g_pre': (1.0, 0.6),
     'L0_ffn_b1': (0.0, 0.593),
     'L0_ffn_b2': (0.0, 0.384),
     'L1_mix_ln1_w': (1.0, 0.6),
     'L1_mix_ln1_b': (0.0, 0.8),
     'L1_mix_ln2_w': (1.0, 0.6),
     'L1_mix_ln2_b': (0.0, 2.0),
     'L1_ffn_b_fx': (0.0, 1.352),
     'L1_ffn_b_x': (0.0, 2.0),
     'L1_ffn_b_slice': (0.0, 2.0),
     'L1_ffn_b_out': (0.0, 2.0),
     'L1_ffn_temperature': (0.5, 0.6)}
    factors = {'L0_gnn_b': 8.0,
     'L0_mix_w_qkv': 8.0,
     'L0_mix_mem_kv': 8.0,
     'L0_mix_w_out': 8.0,
     'L1_mix_Wx': 3.887,
     'L1_mix_bx': 8.0,
     'L1_mix_Wq': 8.0,
     'L1_mix_Wk': 8.0,
     'L1_mix_Wv': 3.66,
     'L1_mix_Wo': 3.996,
     'L1_mix_bo': 37.668,
     'L1_mix_b1': 64.0,
     'L1_mix_b2': 64.0,
     'L1_ffn_W_x': 8.0,
     'L1_ffn_W_slice': 8.0,
     'L1_ffn_W_q': 8.0,
     'L1_ffn_W_k': 8.0,
     'L1_gnn_b3': 3.651,
     'L1_mix_W1': 4.045,
     'L1_mix_W2': 3.482}
    for name, (base, spread) in spreads.items():
        noise = np.random.default_rng([zlib.crc32(name.encode()), seed]).standard_normal(out[name].shape)
        drawn = base * np.exp(spread * noise) if base else spread * noise
        out[name] = jnp.asarray(drawn.astype(out[name].dtype))
    for name, factor in factors.items():
        out[name] = (out[name] * factor).astype(out[name].dtype)
    return out
```

```python
from contextlib import ExitStack

import concourse.bass as bass
from concourse import mybir

F32 = mybir.dt.float32
I32 = mybir.dt.int32
ALU = mybir.AluOpType
ACT = mybir.ActivationFunctionType
AX = mybir.AxisListType.X

N = 3125
D = 256
TK = 125
T = N // TK
C = D // 128
E = 53125
NCH = E // TK
GK = 5
NG = NCH // GK
W = 128
HTW = N + W
BT = 5
NB = T // BT
NE = 8
NM = 4
NHID = 8
H1 = 8
HS = 8
INNER = 512
PITCH = D + 1
EPS = 1e-5


class Steps:

    def __init__(self, eng, sem, per, passed):
        self.eng, self.sem, self.per, self.passed, self.k = eng, sem, per, passed, 0

    def tile(self, t):
        self.base, self.k = t * self.per, 0

    def done(self, ins, plain=False):
        self.k += 1
        ins.then_inc(self.sem, 1)
        self.eng.wait_ge(self.sem, self.base + self.k)
        if plain:
            self.eng.sem_inc(self.passed, 1)

    def end(self):
        assert self.k == self.per, (self.k, self.per)


def build(nc, x, src, dst, edge_weight, W0g, b0g, wqkv, mem_kv, wout0, bout0, gout0, gpre, router, we1, be1,
          we2, be2, g1w1, g1w2, g1w3, g1b3, ln1w, ln1b, Wx, bx, Wq, Wk, Wv, Wo, bo, ln2w, ln2b, Wm1, bm1, Wm2, bm2,
          Wfx, bfx, Wsx, bsx, Wsl, bsl, Wsq, Wsk, Wsv, Wout, bout, temp, out):
    table = [nc.dram_tensor(f"table{i}", (N, D), F32, kind="Internal").ap() for i in range(2)]
    with ExitStack() as ctx:
        def sb(name, shape, dt=F32):
            return ctx.enter_context(nc.sbuf_tensor(name, shape, dt))

        def sem(name):
            return ctx.enter_context(nc.semaphore(name))

        X = sb("X", [TK, T, D])
        XN = sb("XN", [TK, T, D])
        KQ = sb("KQ", [128, 4, N])
        HT = sb("HT", [128, C, HTW])
        big = sb("big", [128, 8192])
        stg = sb("stg", [128, 2848])
        onehot = sb("onehot", [TK, 2, GK, W])
        src_i = sb("src_i", [TK, NCH], I32)
        dst_r = sb("dst_r", [TK, NCH])
        w_e = sb("w_e", [TK, NCH])
        idx = sb("idx", [TK, 2, GK], I32)
        base = sb("base", [1, NG], I32)
        iota = sb("iota", [TK, W])
        ident = sb("ident", [128, 128])
        mask32 = sb("mask32", [128, 128])
        WA = sb("WA", [128, C, 2 * D])
        WB = sb("WB", [128, C, 2 * D])
        WV = sb("WV", [128, C, D])
        WoT = sb("WoT", [128, C, D])
        M = sb("M", [128, C, D])
        rT = sb("rT", [128, C, NE])
        vecs = sb("vecs", [48, 128])
        vT = sb("vT", [128, 48])
        b2row = sb("b2row", [NE, D])
        rows = sb("rows", [TK, 4, D])
        bqk = sb("bqk", [TK, 2 * D])
        bvc = sb("bvc", [128, C])
        rr = sb("rr", [TK, T])
        mu = sb("mu", [TK, T])
        kmax = sb("kmax", [128, C])
        ksum = sb("ksum", [128, C, NB])
        small = sb("small", [128, 64])
        MV = sb("MV", [TK, T, 2])
        st = sb("st", [TK, 2, 10])
        st2 = sb("st2", [TK, 2, 10])
        qst = sb("qst", [TK, 2, 3 * H1])
        fsx = sb("fsx", [128, 4, D])
        rt = sb("rt", [TK, 2, 48])
        rt2 = sb("rt2", [TK, 14])
        cT = sb("cT", [NE, TK])
        eps = sb("eps", [TK, 1])
        neghalf = sb("neghalf", [TK, T])
        pb = ctx.enter_context(nc.psum_tensor("pb", [128, 8, 512], F32))

        V_GPRE, V_B1, V_LN1W, V_BX, V_LN2W, V_BM1, V_B3, V_BSX = 0, 2, 18, 20, 22, 24, 32, 34
        NV = 38
        VECS = ((gpre, V_GPRE), (be1, V_B1), (ln1w, V_LN1W), (bx, V_BX), (ln2w, V_LN2W), (bm1, V_BM1),
                (g1b3, V_B3), (bsx, V_BSX))

        def part(buf, at, shape):
            n = 1
            for s in shape[1:]:
                n *= s
            v = buf[0:shape[0], at:at + n]
            if len(shape) == 3:
                v = v.rearrange("p (a b) -> p a b", b=shape[2])
            if len(shape) == 4:
                v = v.rearrange("p (a b c) -> p a b c", b=shape[2], c=shape[3])
            return v

        ring = part(big, 4096, [TK, 2, GK, D])
        w1 = part(big, 0, [128, NE, C, D])
        w2 = part(big, 4096, [128, NE, C, D])
        w1T = part(big, 0, [128, C, NHID * 128])
        w2T = part(big, 2048, [128, NHID, D])
        W0, Wg, wo0 = part(big, 6656, [128, C, D]), part(big, 7168, [128, C, 384]), part(big, 7936, [128, D])

        def bank(i, p, n, at=0):
            return pb[0:p, i, at:at + n]

        class Signal:

            def __init__(self, name, free=0, unit=1, sem=None, after=0):
                self.s = ctx.enter_context(nc.semaphore(name)) if sem is None else sem
                self.credit, self.unit, self.after = free * unit, unit, after

            def done(self, k):
                return self.s, (k + self.after) * self.unit + self.credit

            def free(self, k):
                return self.s, (k + self.after + 1) * self.unit

            def next(self, n):
                return Signal(None, self.credit // self.unit, self.unit, self.s, self.after + n)

        def in_turn(name, *counts):
            s, after, made = ctx.enter_context(nc.semaphore(name)), 0, []
            for n in counts:
                made.append(Signal(None, sem=s, after=after))
                after += n
            return made

        s_in = Signal("s_in", unit=16)
        s_x = Signal("s_x", unit=16)
        s_w = Signal("s_w", unit=16)
        s_w12 = Signal("s_w12", unit=16)
        l_raw = Signal("l_loaded", unit=16)
        l_row = Signal("l_rows_loaded", unit=16)
        f_w = Signal("f_loaded", unit=16)
        phase = ctx.enter_context(nc.semaphore("phase_ended"))
        ENDS = (4, 3, 3, 3, 3, 4, 3, 3, 3, 3, 4)

        def ended(i):
            return phase, sum(ENDS[:i + 1])

        s_const, a_rr, f_one = in_turn("pool_once", 6, 2, 1)
        (s_tT, s_vT, w_T, w_P, o_mT, o_pe0, l_T, o_pe1, f_T, f_P, g_T, g_tok, g_qkv, g_sc, g_aT, g_M) = in_turn(
            "pe_once", 3, 1, 1, 1, 1, 3, 2 * NHID, 3 * C, 1, 1, 1, 1, 1, 1, 1, 1)
        o_pe = (o_pe0, o_pe1)
        w_Tc, w_Pc, o_mTc, o_gTc0, o_gTc1, f_Tc, g_Tc, g_qkvc, g_vw, g_ex = in_turn(
            "act_once", 4, 1, 1, 1, C, 2, 3, 2, 2, 1)
        o_gTc = (o_gTc0, o_gTc1)
        (s_rel, s_tab, s_vTc, w_blk, w_b, c_max0, o_mem, o_v0, l_b, c_max1, o_v1, f_blk, f_ready, g_s, g_tokc,
         g_kc, g_mx, g_at, g_aTc, g_Mc) = in_turn(
            "dve_once", 2, 3, 3, 3, 1, 1, 1, 3, NHID, 1, 3 * C, 1, 1, 4, 4, 1, 2, 2, 1, 2)
        c_max, o_v = (c_max0, c_max1), (o_v0, o_v1)
        passed = ctx.enter_context(nc.semaphore("dve_passed"))
        dve_steps = ctx.enter_context(nc.semaphore("dve_steps"))
        g_idx, g_oh = Signal("g_staged"), Signal("g_onehot")
        g_agg, g_acc = Signal("g_summed", 2), Signal("g_added", 2)
        g_got = [Signal(f"g_got{b}", unit=16 * GK) for b in range(2)]
        g_idx, g_oh, g_agg, g_acc = ((s, s.next(NG)) for s in (g_idx, g_oh, g_agg, g_acc))
        g_got = (g_got, [g_got[0].next(NG // 2 + 1), g_got[1].next(NG // 2)])
        a_dve = ctx.enter_context(nc.semaphore("a_dve"))
        a_var, a_rstd = Signal("a_variance"), Signal("a_rstd")
        a_xs = Signal("a_normed")
        a_T = Signal("a_transposed")
        a_xT = Signal("a_xT", 2)
        a_sq = Signal("a_squared", 2)
        a_kept = Signal("a_kept", 2)
        a_p = Signal("a_projected")
        a_pr = Signal("a_rows", 2)
        a_st = [Signal(f"a_stored{u}", 1, 16) for u in range(2)]
        k_ys = Signal("k_scaled")
        k_T = Signal("k_transposed")
        k_yT = Signal("k_yT", 2)
        k_L = Signal("k_logits")
        k_k = Signal("k_keys", 2)
        k_sub = Signal("k_shifted", 2)
        k_exp = Signal("k_exp")
        k_dve = ctx.enter_context(nc.semaphore("k_dve"))
        k_q = Signal("k_queries")
        k_KT = Signal("k_kq_transposed")
        k_KQ = Signal("k_kq_out", 2)
        c_es, c_T, c_er, c_G = (Signal("c_exp"), Signal("c_transposed", 1), Signal("c_rows", 1),
                                Signal("c_summed", 1))
        c_es, c_T, c_er, c_G = ((s, s.next(NB)) for s in (c_es, c_T, c_er, c_G))
        c_hh = Signal("c_normed")
        m_hs = Signal("m_staged")
        m_o = Signal("m_out_rows", 2)
        m_bo = Signal("m_biased")
        m_ss = Signal("m_norm")
        m_dve = ctx.enter_context(nc.semaphore("m_dve"))
        m_sq, m_rn = Signal("m_norm_bounded"), Signal("m_norm_inverse")
        m_var, m_rstd = Signal("m_variance"), Signal("m_rstd")
        m_xs = Signal("m_normed")
        m_T = Signal("m_transposed")
        m_xT = Signal("m_xT")
        m_r = Signal("m_router")
        m_mx = Signal("m_router_max")
        m_ex = Signal("m_router_exp")
        m_c = Signal("m_weights")
        m_cT = Signal("m_weights_transposed")
        m_cTc = Signal("m_weights_out")
        m_b = Signal("m_bias")
        m_x = Signal("m_started", 1)
        m_h = Signal("m_hidden")
        m_g = Signal("m_gelu", 2)
        m_y = Signal("m_out", 2)
        m_acc = Signal("m_added", 2)
        t_dve = ctx.enter_context(nc.semaphore("t_dve"))
        t_var, t_rstd = Signal("t_variance"), Signal("t_rstd")
        t_fs = Signal("t_normed")
        t_kept = Signal("t_kept", 1)
        t_hh = Signal("t_normed_twice")
        t_T = Signal("t_transposed", 2)
        t_Tc = Signal("t_transposed_out")
        t_A = Signal("t_messages")
        t_B = Signal("t_logits")
        t_pr = Signal("t_rows")
        t_st = [Signal(f"t_stored{u}", 1, 16) for u in range(2)]
        t_sub = Signal("t_shifted")
        t_exp = Signal("t_exp")
        t_q = Signal("t_queries")
        t_K = Signal("t_kq_transposed", 1)
        t_KQ = Signal("t_kq_out", 1)
        l_ev = Signal("l_transposed_out", 4)
        e_qs = Signal("e_staged")
        e_o = Signal("e_mixed", 2)
        e_dve = ctx.enter_context(nc.semaphore("e_dve"))
        e_h = Signal("e_sum", 1)
        e_var, e_sd = Signal("e_variance"), Signal("e_deviation")
        e_yh = Signal("e_normed")
        e_T = Signal("e_transposed", 2)
        e_yT = Signal("e_yT", 1)
        e_H = Signal("e_hidden")
        e_g = Signal("e_gelu", 2)
        e_y = Signal("e_out", 1)
        e_x = Signal("e_added", 1)
        e_hx = Signal("e_sum_added")
        f_hs = Signal("f_staged")
        f_o = Signal("f_message_rows", 2)
        f_dve = ctx.enter_context(nc.semaphore("f_dve"))
        f_x = Signal("f_stream", 1)
        f_var, f_rstd = Signal("f_variance"), Signal("f_rstd")
        f_xs = Signal("f_normed")
        f_tT = Signal("f_x_transposed")
        f_xT = Signal("f_xT", 1)
        f_L = Signal("f_logits")
        f_lg = Signal("f_logits_out", 1)
        f_sub = Signal("f_shifted")
        f_exp = Signal("f_exp")
        f_sdve = ctx.enter_context(nc.semaphore("f_sdve"))
        f_sw = Signal("f_slices")
        f_S = Signal("f_slices_transposed")
        f_sT = Signal("f_slices_out", 1)
        f_tok = Signal("f_tokens", 2)
        h_ss = Signal("h_staged")
        h_y = Signal("h_out", 2)
        h_ob = Signal("h_rows", 2)
        h_st = [Signal(f"h_stored{u}", 1, 16) for u in range(2)]

        block = ctx.enter_context(nc.Block())

        def cols(t):
            return bass.ds(t * TK, TK)

        def one(t):
            return bass.ds(t, 1)

        def tile(a, t):
            return a[:, one(t), :].rearrange("p a b -> p (a b)")

        def tiles(eng, step):
            with eng.Fori(0, T // 2) as j:
                for u in range(2):
                    step(j, u)
            step(T // 2, 0)

        def skewed(eng, early, late, peel=0):
            early(0, 0)
            for j in range(peel):
                for u in range(2):
                    early(j + (u + 1) // 2, (u + 1) % 2)
                    late(j, u)
            with eng.Fori(peel, T // 2) as j:
                for u in range(2):
                    early(j + (u + 1) // 2, (u + 1) % 2)
                    late(j, u)
            late(T // 2, 0)

        def experts(eng, early, late, tail):
            early(0, 0)
            early(0, 1)
            late(0, 0)
            with eng.Fori(0, T // 2 - 1) as j:
                tail(j, 0)
                early(j + 1, 0)
                late(j, 1)
                tail(j, 1)
                early(j + 1, 1)
                late(j + 1, 0)
            tail(T // 2 - 1, 0)
            early(T // 2, 0)
            late(T // 2 - 1, 1)
            tail(T // 2 - 1, 1)
            late(T // 2, 0)
            tail(T // 2, 0)

        def raw(i):
            return KQ[:, 2, i * 512:(i + 1) * 512].rearrange("p (c n) -> p c n", c=C)

        def row(v):
            return v.rearrange("(a n) -> a n", a=1)

        def every(v, p):
            return row(v).partition_broadcast(p).rearrange("p a n -> p (a n)")

        r_g1, r_g2, r_g3, r_x, r_o, r_g2T = (raw(i) for i in range(6))
        r_q = [KQ[:, 3, i * 128:(i + 1) * 128] for i in range(3)]
        r_qT = [KQ[:, 3, 384 + i * 128:512 + i * 128] for i in range(3)]
        r_b = KQ[:, 3, 768:1024]
        r_jk = KQ[:, 3, 1024:1280]
        r_xb0, r_xb = KQ[:, 3, 1280:1280 + C], KQ[:, 3, 1288:1288 + C]
        r_xbb = KQ[:, 3, 1408:1408 + C * TK].rearrange("p (c n) -> p c n", c=C)
        r_b3b = KQ[:, 3, 1664:1664 + C * TK].rearrange("p (c n) -> p c n", c=C)
        r_rt = KQ[0:NE, 3, 2048:2048 + D]
        r_q32 = [KQ[:, 3, 2304 + 32 * i:2336 + 32 * i] for i in range(3)]
        e_i = KQ[0:NG, 0, 0:2 * GK * TK].bitcast(I32).rearrange("g (a k e) -> g a k e", a=2, k=GK)
        e_f = KQ[0:NG, 1, 0:3 * GK * TK].rearrange("g (a k e) -> g a k e", a=3, k=GK)
        mk, mv = small[:, 0:NM], small[:, NM:2 * NM]
        den, msum, nmax = small[:, 8:8 + C], small[:, 10:11], small[:, 12:12 + C]
        mkT, mvT = stg[0:NM, 2560:2688], stg[0:NM, 2688:2816]
        a_s = [part(stg, 256 * u, [TK, D]) for u in range(2)]
        a_xTb = [part(stg, 512 + 256 * u, [128, C, TK]) for u in range(2)]
        a_prb = [part(stg, 1024 + 256 * u, [TK, D]) for u in range(2)]
        a_sqb = part(stg, 1536, [TK, D])
        k_qb = [part(stg, 1024 + 128 * u, [TK, 128]) for u in range(2)]
        k_kb = [part(stg, 1280 + 128 * u, [TK, 128]) for u in range(2)]
        c_esb, c_erb, c_hhb = part(stg, 0, [128, BT * TK]), part(stg, 640, [TK, BT, 128]), part(big, 6656, [TK, BT, D])
        o_gb, o_gTb = part(stg, 1280, [128, D]), part(stg, 1536, [128, C, 128])
        o_kvb, o_mkb = part(stg, 1792, [128, 128]), part(stg, 1920, [128, NM])
        m_sb = [part(stg, 256 * u, [TK, D]) for u in range(2)]
        m_xTb = [part(stg, 512 + 256 * u, [128, C, TK]) for u in range(2)]
        m_gb = [part(stg, 1024 + 256 * u, [128, C, TK]) for u in range(2)]
        m_qsb = [part(stg, 1536 + 128 * u, [128, TK]) for u in range(2)]
        m_hsb = [part(stg, 1792 + 256 * u, [128, C, TK]) for u in range(2)]
        m_ob, m_gnb = part(stg, 2304, [TK, D]), part(stg, 2560, [TK, D])
        t_prb = [onehot[:, 0, 2 * u:2 * u + 2, :].rearrange("p a b -> p (a b)") for u in range(2)]
        t_qkb = onehot[:, 1, 0:4, :].rearrange("p a b -> p (a b)")
        t_fsb, t_hhb = fsx[0:TK, 0], fsx[0:TK, 1]
        t_fT = fsx[:, 2, 0:C * TK].rearrange("p (c n) -> p c n", c=C)
        t_hT = fsx[:, 3, 0:C * TK].rearrange("p (c n) -> p c n", c=C)
        l_rawb, l_bb, l_jk = part(stg, 0, [128, NHID * D]), part(stg, 2048, [128, D]), part(stg, 2304, [128, D])
        bm = small[:, 16:16 + NHID]
        e_qsb = [part(stg, 256 * u, [128, C, TK]) for u in range(2)]
        e_hb = [part(stg, 512 + 256 * u, [TK, D]) for u in range(2)]
        e_yb = [part(stg, 1024 + 256 * u, [TK, D]) for u in range(2)]
        e_yTb = [part(stg, 1536 + 256 * u, [128, C, TK]) for u in range(2)]
        e_gb = part(big, 6656, [128, NHID, TK])
        f_wx, f_wfx = part(big, 0, [128, C, INNER]), part(big, 1024, [128, C, INNER])
        f_wout, f_raw = part(big, 2048, [128, 4, D]), part(big, 3072, [128, 4, 64])
        f_blkb, f_wxs = part(big, 3328, [128, 4, 128]), part(big, 3840, [128, C, INNER])
        f_wxT, f_bfx = part(big, 4864, [128, 4, D]), part(big, 5888, [1, INNER])
        f_temp, f_bsl = part(big, 6400, [128, HS]), part(big, 6408, [TK, 64])
        f_bxs, f_bxb = part(big, 6472, [TK, INNER]), part(big, 6984, [128, 4, TK])
        f_xsb = [part(stg, 257 * u, [TK, PITCH]) for u in range(2)]
        f_xTb = part(stg, 514, [128, C, TK])
        f_hsb = [part(stg, 770 + 256 * u, [128, C, TK]) for u in range(2)]
        f_lgb = [part(stg, 1538 + 512 * u, [TK, INNER]) for u in range(2)]
        HTf = HT[:, :, :].rearrange("p c n -> p (c n)")
        s_s, s_sT = part(HTf, 0, [128, 4, PITCH]), part(HTf, 1028, [128, 4, C, 128])
        s_tc, s_tb = part(HTf, 2052, [128, 4, 64]), part(HTf, 2308, [128, 4, 128])
        s_q, s_k = part(HTf, 2820, [128, 4, 128]), part(HTf, 3332, [128, 4, 64])
        s_v, s_at = part(HTf, 3588, [128, 4, 128]), part(HTf, 4100, [128, 4, 128])
        s_aT, s_vw = part(HTf, 4612, [128, 4, 128]), part(HTf, 5124, [128, 4, D])
        s_nr, s_ec = part(big, 7484, [1, INNER]), part(big, 6984, [128, 4, 64])
        M2 = fsx
        h_obb = [part(stg, 514 + 256 * u, [TK, D]) for u in range(2)]
        h_ssb = [part(stg, 1026 + 512 * u, [128, 4, TK]) for u in range(2)]

        @block.sync
        def _(sp):
            for s in (*a_st, *t_st, *h_st):
                sp.sem_inc(s.s, s.credit)

            def load(o, i, s):
                sp.dma_start(o, i).then_inc(s.s, 16)

            load(e_i[:, 0], src.rearrange("(g k e) -> g k e", k=GK, e=TK), s_in)
            load(e_i[:, 1], dst.rearrange("(g k e) -> g k e", k=GK, e=TK), s_in)
            load(e_f[:, 2], edge_weight.rearrange("(g k e) -> g k e", k=GK, e=TK), s_in)
            sp.dma_start(base[:, :], dst.rearrange("(a g q) -> a g q", a=1, g=NG)[:, :, 0],
                         allow_slow_non_contiguous=True).then_inc(s_in.s, 16)
            xr = x.rearrange("(b t p) d -> b p t d", b=NB, p=TK)
            for b in range(NB):
                load(X[:, b * BT:(b + 1) * BT, :], xr[b], s_x)
            load(W0, W0g.rearrange("(c p) n -> p c n", p=128), s_in)
            load(Wg, wqkv.rearrange("(c p) n -> p c n", p=128), s_in)
            load(wo0, wout0, s_in)
            load(mk, mem_kv[0].rearrange("h d m -> (h d) m"), s_in)
            load(mv, mem_kv[1].rearrange("h d m -> (h d) m"), s_in)
            for i, v in enumerate((b0g, bout0, gout0)):
                load(rows[:, i, :], every(v, TK), s_in)
            load(b2row[:, :], be2, s_in)
            load(r_rt, router, s_in)
            for v, a in VECS:
                f = v if len(v.shape) == 1 else v.rearrange("a n -> (a n)")
                load(vecs[a:a + f.shape[0] // 128, :], f.rearrange("(k p) -> k p", p=128), s_in)
            for o, i in ((r_g1, g1w1), (r_g2, g1w2), (r_g3, g1w3), (r_x, Wx), (r_o, Wo)):
                load(o, i.rearrange("(c p) n -> p c n", p=128), s_w)
            for o, i in zip(r_q32, (Wq, Wk, Wv)):
                for a in range(4):
                    load(o[32 * a:32 * a + 32, :], i, s_w)
            load(r_b, every(ln1b, 128), s_w)
            load(w1, we1.rearrange("e (c p) n -> p e c n", p=128), s_w12)

            def store_a(j, u):
                sp.wait_ge(*a_pr.done(2 * j + u + 1))
                sp.dma_start(table[0][cols(2 * j + u), :], a_prb[u]).then_inc(a_st[u].s, 16)
            tiles(sp, store_a)

            sp.wait_ge(*ended(4))
            load(w2, we2.rearrange("e (c p) n -> p e c n", p=128), s_w12)

            def store_t(j, u):
                sp.wait_ge(*t_pr.done(2 * j + u + 1))
                sp.dma_start(table[1][cols(2 * j + u), :], t_prb[u]).then_inc(t_st[u].s, 16)
            tiles(sp, store_t)

            sp.wait_ge(*ended(5))
            load(l_rawb.rearrange("p (c n) -> p c n", c=NHID), Wm1.rearrange("(c p) n -> p c n", p=128), l_raw)
            for i, v in enumerate((bo, bm2)):
                load(rows[:, i, :], every(v, TK), l_row)
            load(l_bb, every(ln2b, 128), l_row)
            sp.wait_ge(*l_ev.done(NHID))
            sp.wait_ge(*l_b.done(NHID))
            load(l_rawb.rearrange("p (c n) -> p c n", c=C), Wm2.rearrange("(c p) n -> p c n", p=128), l_raw)

            sp.wait_ge(*ended(9))
            load(f_wx, Wsx.rearrange("(c p) n -> p c n", p=128), f_w)
            load(f_wfx, Wfx.rearrange("(c p) n -> p c n", p=128), f_w)
            load(f_wout, Wout.rearrange("(c p) n -> p c n", p=128), f_w)
            for i, v in enumerate((Wsl, Wsq, Wsk, Wsv)):
                for a in range(2):
                    load(f_raw[64 * a:64 * a + 64, i, :], v, f_w)
            load(f_bfx, row(bfx), f_w)
            load(f_temp, every(temp.rearrange("a h b c -> (a h b c)"), 128), f_w)
            load(rows[:, 0, :], every(bout, TK), f_w)
            load(f_bsl, every(bsl, TK), f_w)

            def store_h(j, u):
                sp.wait_ge(*h_ob.done(2 * j + u + 1))
                sp.dma_start(out[cols(2 * j + u), :], h_obb[u]).then_inc(h_st[u].s, 16)
            tiles(sp, store_h)
            sp.wait_ge(*h_st[0].done(T // 2 + 1))
            sp.wait_ge(*h_st[1].done(T // 2))

        @block.gpsimd
        def _(pool):
            pool.sem_inc(a_kept.s, a_kept.credit)
            pool.sem_inc(t_kept.s, t_kept.credit)
            nc.gpsimd.iota(iota[:, :], [[1, W]], base=0, channel_multiplier=0,
                           allow_small_or_imprecise_dtypes=True).then_inc(s_const.s, 1)
            nc.gpsimd.memset(neghalf[:, :], -0.5)
            nc.gpsimd.memset(ident[:, :], 0.0).then_inc(s_const.s, 1)
            nc.gpsimd.memset(mask32[:, :], 1.0).then_inc(s_const.s, 1)
            pool.wait_ge(*s_const.done(3))
            nc.gpsimd.affine_select(out=ident[:, :], in_=ident[:, :], compare_op=ALU.not_equal, fill=1.0, base=0,
                                    pattern=[[-1, 128]], channel_multiplier=1).then_inc(s_const.s, 1)
            m = mask32[:, :].rearrange("p (b c) -> p b c", c=32)
            nc.gpsimd.affine_select(out=m, in_=m, compare_op=ALU.is_ge, fill=0.0, base=0,
                                    pattern=[[-32, 4], [0, 32]], channel_multiplier=1).then_inc(s_const.s, 1)
            pool.wait_ge(*s_const.done(5))
            nc.gpsimd.affine_select(out=m, in_=m, compare_op=ALU.is_ge, fill=0.0, base=31,
                                    pattern=[[32, 4], [0, 32]], channel_multiplier=-1).then_inc(s_const.s, 1)

            def rstd(st_, var, out, n):
                pool.wait_ge(*var.done(n + 1))
                nc.gpsimd.tensor_tensor(st_[:, 8:9], st_[:, 7:8], neghalf[:, 0:1], ALU.pow).then_inc(out.s, 1)

            def keep_a(j, u):
                t = 2 * j + u
                rstd(st[:, u], a_var, a_rstd, t)
                pool.wait_ge(*s_const.done(6))
                pool.wait_ge(*a_xs.done(t + 1))
                nc.gpsimd.tensor_copy(tile(XN, t), a_s[u])
                nc.gpsimd.tensor_tensor(tile(X, t), tile(X, t), a_s[u], ALU.add).then_inc(a_kept.s, 1)
            tiles(pool, keep_a)
            pool.drain().then_inc(phase, 1)
            pool.wait_ge(*ended(0))
            nc.gpsimd.tensor_scalar(rr[:, :], rr[:, :], 1e-24, None, ALU.max).then_inc(a_rr.s, 1)
            pool.wait_ge(*a_rr.done(1))
            nc.gpsimd.tensor_tensor(rr[:, :], rr[:, :], neghalf[:, :], ALU.pow).then_inc(a_rr.s, 1)

            def gather(layer):
                def fill(h, b):
                    g = 2 * h + b
                    pool.wait_ge(*g_agg[layer].free(g))
                    nc.gpsimd.tensor_copy(idx[:, b, :], src_i[:, bass.ds(g * GK, GK)]).then_inc(g_idx[layer].s, 1)
                    pool.wait_ge(*s_tab.done(3))
                    pool.wait_ge(*g_idx[layer].done(g + 1))
                    for k in range(GK):
                        nc.gpsimd.indirect_dma_start(
                            out=ring[:, b, k, :], out_offset=None, in_=table[layer],
                            in_offset=bass.IndirectOffsetOnAxis(ap=idx[:, b, k:k + 1], axis=0),
                        ).then_inc(g_got[layer][b].s, 16)
                with pool.Fori(0, NG // 2) as h:
                    for b in range(2):
                        fill(h, b)
                fill(NG // 2, 0)

            pool.wait_ge(*s_tab.done(3))
            pool.wait_ge(*a_st[0].done(T // 2 + 1))
            pool.wait_ge(*a_st[1].done(T // 2))
            gather(0)

            pool.wait_ge(*ended(4))

            def stage_m(j, u):
                t = 2 * j + u
                pool.wait_ge(*m_o.free(t))
                nc.gpsimd.tensor_copy(m_qsb[u], KQ[:, 1, cols(t)])
                nc.gpsimd.tensor_copy(m_hsb[u], HT[:, :, cols(t)]).then_inc(m_hs.s, 1)
                pool.wait_ge(*m_sq.done(t + 1))
                nc.gpsimd.tensor_tensor(rt[:, u, 43:44], rt[:, u, 40:41], neghalf[:, 0:1], ALU.pow)\
                    .then_inc(m_rn.s, 1)
                rstd(st[:, u], m_var, m_rstd, t)

            def keep_t(j, u):
                t = 2 * j + u
                rstd(st2[:, 0], t_var, t_rstd, 2 * t)
                pool.wait_ge(*s_const.done(6))
                pool.wait_ge(*t_fs.done(t + 1))
                nc.gpsimd.tensor_copy(tile(XN, t), t_fsb).then_inc(t_kept.s, 1)
                rstd(st2[:, 1], t_var, t_rstd, 2 * t + 1)
            experts(pool, stage_m, lambda j, u: None, keep_t)
            pool.drain().then_inc(phase, 1)
            pool.wait_ge(*ended(5))
            pool.wait_ge(*t_st[0].done(T // 2 + 1))
            pool.wait_ge(*t_st[1].done(T // 2))
            gather(1)

            pool.wait_ge(*ended(9))
            nc.gpsimd.memset(f_xsb[0][:, D:PITCH], 1.0)
            nc.gpsimd.memset(f_xsb[1][:, D:PITCH], 1.0).then_inc(f_one.s, 1)

            def stage_f(j, u):
                t = 2 * j + u
                pool.wait_ge(*f_o.free(t))
                nc.gpsimd.tensor_copy(f_hsb[u], HT[:, :, cols(t)]).then_inc(f_hs.s, 1)
                rstd(st[:, u], f_var, f_rstd, t)
            tiles(pool, stage_f)
            pool.drain().then_inc(phase, 1)
            pool.wait_ge(*ended(10))

            def stage_h(j, u):
                t = 2 * j + u
                pool.wait_ge(*h_y.free(t))
                nc.gpsimd.tensor_copy(h_ssb[u], KQ[:, :, cols(t)])
                nc.gpsimd.tensor_tensor(tile(X, t), tile(X, t), rows[:, 0, :], ALU.add).then_inc(h_ss.s, 1)
            tiles(pool, stage_h)

        @block.tensor
        def _(pe):
            for s in (g_agg[0], c_T[0], c_G[0], m_o, m_y, t_T, t_K, e_o, e_T, e_y, f_o, f_tok, h_y):
                pe.sem_inc(s.s, s.credit)

            def mm(o, l, r, start=True, stop=True):
                return pe.matmul(o, l, r, start=start, stop=stop, skip_group_check=True)

            def tr(o, i):
                k = i.shape[0]
                return pe.transpose(o, i, ident[0:k, 0:k])

            def two(o, l, r):
                for c in range(C):
                    ins = mm(o, l[:, c, :], r[:, c, :], c == 0, c == C - 1)
                return ins

            def by_feature(b, s):
                for c in range(C):
                    ins = tr(bank(b, 128, TK, c * TK), s[:, c * 128:(c + 1) * 128])
                return ins

            def group(layer, h, b):
                g = 2 * h + b
                pe.wait_ge(*g_oh[layer].done(g + 1))
                pe.wait_ge(*g_acc[layer].free(g))
                pe.wait_ge(*g_got[layer][b].done(h + 1))
                for k in range(GK):
                    for c in range(C):
                        ins = mm(bank(6 + b, 128, W, c * W), ring[:, b, k, c * 128:(c + 1) * 128],
                                 onehot[:, b, k, :], k == 0 and c == 0, k == GK - 1)
                ins.then_inc(g_agg[layer].s, 1)

            pe.wait_ge(*s_const.done(6))
            pe.wait_ge(*s_rel.done(2))
            for a in range(3):
                for k in range(GK):
                    ins = tr(bank(a, TK, NG, k * NG), e_f[:, a, k, :])
                ins.then_inc(s_tT.s, 1)
            tr(bank(3, 128, NV), vecs[0:NV, :])
            for c in range(C):
                tr(bank(3, 128, NE, 64 + c * NE), r_rt[:, c * 128:(c + 1) * 128])
            tr(bank(3, NM, 128, 256), mv).then_inc(s_vT.s, 1)
            pe.wait_ge(*s_vTc.done(3))
            pe.wait_ge(*s_tab.done(3))

            def a_early(j, u):
                t = 2 * j + u
                pe.wait_ge(*a_xs.done(t + 1))
                pe.wait_ge(*a_xT.free(t))
                by_feature(u, a_s[u]).then_inc(a_T.s, 1)

            def a_late(j, u):
                t = 2 * j + u
                pe.wait_ge(*a_xT.done(t + 1))
                pe.wait_ge(*a_pr.free(t))
                two(bank(2 + u, TK, D), a_xTb[u], W0).then_inc(a_p.s, 1)
            skewed(pe, a_early, a_late)
            pe.drain().then_inc(phase, 1)
            pe.wait_ge(*ended(0))

            pe.wait_ge(*s_w.done(18))
            pe.wait_ge(*w_blk.done(3))
            k = 0
            for r in (r_g1, r_g2, r_o):
                for c in range(C):
                    for a in range(C):
                        tr(bank(k // 4, 128, 128, (k % 4) * 128), r[:, a, c * 128:(c + 1) * 128])
                        k += 1
            for i in range(3):
                ins = tr(bank(3, 128, 128, i * 128), r_q[i])
            ins.then_inc(w_T.s, 1)
            pe.wait_ge(*w_Tc.done(4))
            pe.wait_ge(*w_b.done(1))
            for c in range(C):
                for m in range(C):
                    mm(bank(0, 128, D, c * D), r_g3[:, m, c * 128:(c + 1) * 128], r_g2T[:, m, :], m == 0, m == C - 1)
            two(bank(1, TK, D), r_b3b, r_g2T)
            for i in range(2):
                for c in range(C):
                    for a in range(C):
                        mm(bank(2 + c, 128, 128, i * D + a * 128), r_x[:, a, c * 128:(c + 1) * 128], r_qT[i])
                for a in range(C):
                    mm(bank(4, TK, 128, i * D + a * 128), r_xbb[:, a, :], r_qT[i])
            for c in range(C):
                for a in range(C):
                    mm(bank(5, 128, 128, c * D + a * 128), r_x[:, a, c * 128:(c + 1) * 128], r_qT[2])
            for a in range(C):
                ins = mm(bank(1, 128, 1, D + a), r_qT[2], r_xb[:, a:a + 1])
            ins.then_inc(w_P.s, 1)
            pe.wait_ge(*w_Pc.done(1))

            def k_early(j, u):
                t = 2 * j + u
                pe.wait_ge(*k_ys.done(t + 1))
                pe.wait_ge(*k_yT.free(t))
                by_feature(u, a_s[u]).then_inc(k_T.s, 1)
                pe.wait_ge(*k_yT.done(t + 1))
                pe.wait_ge(*k_sub.free(t))
                pe.wait_ge(*k_k.free(t))
                two(bank(2 + u, TK, 256), a_xTb[u], Wg[:, :, 0:256]).then_inc(k_L.s, 1)

            def k_late(j, u):
                t = 2 * j + u
                pe.wait_ge(*k_k.done(t + 1))
                pe.wait_ge(*k_KQ.free(t))
                tr(bank(4 + u, 128, TK, 0), k_kb[u])
                pe.wait_ge(*k_q.done(t + 1))
                tr(bank(4 + u, 128, TK, TK), k_qb[u]).then_inc(k_KT.s, 1)
                group(0, j, u)
            skewed(pe, k_early, k_late)
            pe.drain().then_inc(phase, 1)
            pe.wait_ge(*ended(1))

            def context(layer, nk, first):
                def step(g, start, h0):
                    for jj in range(nk):
                        n = g * nk + jj
                        pe.wait_ge(*c_es[layer].done(n + 1))
                        pe.wait_ge(*c_er[layer].free(n))
                        for i in range(BT):
                            ins = tr(bank(i // 4, TK, 128, (i % 4) * 128), c_esb[:, i * TK:(i + 1) * TK])
                        ins.then_inc(c_T[layer].s, 1)
                        if jj == 0:
                            for b in range(2):
                                group(layer, h0 + (first % 2 + b) // 2, (first % 2 + b) % 2)
                        pe.wait_ge(*c_er[layer].done(n + 1))
                        if layer == 1:
                            pe.wait_ge(*c_hh.done(g + 1))
                        for i in range(BT):
                            r = tile(XN, g * BT + i) if layer == 0 else c_hhb[:, i, :]
                            ins = mm(bank(4 + jj, 128, D), c_erb[:, i, :], r, start and i == 0, False)
                        ins.then_inc(c_G[layer].s, 1)
                step(0, True, first // 2)
                with pe.Fori(1, NB) as g:
                    step(g, False, g + first // 2)

            def fold(layer, nk, wv, wo):
                for jj in range(nk):
                    pe.wait_ge(*o_v[layer].done(3 * jj + 1))
                    for c in range(C):
                        ins = tr(bank(0, 128, 128, c * 128), o_gb[:, c * 128:(c + 1) * 128])
                    ins.then_inc(o_pe[layer].s, 1)
                    pe.wait_ge(*o_gTc[layer].done(jj + 1))
                    for c in range(C):
                        ins = mm(bank(1, 128, 128), wv(c, jj), o_gTb[:, c, :], c == 0, c == C - 1 and layer == 1)
                    if layer == 0:
                        pe.wait_ge(*o_mTc.done(1))
                        ins = mm(bank(1, 128, 128), mvT, mkT, False, True)
                    ins.then_inc(o_pe[layer].s, 1)
                    pe.wait_ge(*o_v[layer].done(3 * jj + 2))
                    mm(bank(2, 128, D), o_kvb, wo(jj)).then_inc(o_pe[layer].s, 1)

            context(0, 1, T)
            pe.drain().then_inc(phase, 1)
            pe.wait_ge(*ended(2))
            pe.wait_ge(*o_mem.done(1))
            tr(bank(3, NM, 128), o_mkb).then_inc(o_mT.s, 1)
            fold(0, 1, lambda c, jj: Wg[:, c, 256:384], lambda jj: wo0)
            pe.drain().then_inc(phase, 1)
            pe.wait_ge(*ended(3))

            first = T + 2 * NB
            with pe.Fori(0, (NG - first) // 2) as j:
                for i in range(2):
                    group(0, j + (first + i) // 2, (first + i) % 2)
            pe.drain().then_inc(phase, 1)
            pe.wait_ge(*ended(4))

            def m_early(j, u):
                t = 2 * j + u
                pe.wait_ge(*m_hs.done(t + 1))
                pe.wait_ge(*m_x.free(t))
                mm(bank(5, TK, D), m_qsb[u], M[:, 0, :])
                for c in range(C):
                    ins = tr(bank(5, TK, 128, D + c * 128), m_hsb[u][:, c, :])
                ins.then_inc(m_o.s, 1)
                pe.wait_ge(*m_xs.done(t + 1))
                by_feature(4, m_sb[u]).then_inc(m_T.s, 1)
                pe.wait_ge(*m_xT.done(t + 1))
                two(bank(5, TK, NE), m_xTb[u], rT).then_inc(m_r.s, 1)
                pe.wait_ge(*m_c.done(t + 1))
                tr(bank(4, NE, TK), rt[:, u, 0:NE]).then_inc(m_cT.s, 1)
                pe.wait_ge(*m_cTc.done(t + 1))
                mm(bank(5, TK, D), cT[:, :], b2row[:, :]).then_inc(m_b.s, 1)

            def m_up(t, u, e):
                pe.wait_ge(*m_g.free(NE * t + e))
                for a in range(C):
                    for c in range(C):
                        ins = mm(bank(e % 2, 128, TK, a * TK), w1[:, e, c, a * 128:(a + 1) * 128],
                                 m_xTb[u][:, c, :], c == 0, c == C - 1)
                ins.then_inc(m_h.s, 1)

            def m_late(j, u):
                t = 2 * j + u
                m_up(t, u, 0)
                for e in range(NE):
                    if e + 1 < NE:
                        m_up(t, u, e + 1)
                    pe.wait_ge(*m_g.done(NE * t + e + 1))
                    pe.wait_ge(*m_acc.free(NE * t + e))
                    two(bank(2 + e % 2, TK, D), m_gb[e % 2], w2[:, e]).then_inc(m_y.s, 1)

            def m_tail(j, u):
                t = 2 * j + u
                pe.wait_ge(*t_fs.done(t + 1))
                pe.wait_ge(*t_KQ.free(t))
                by_feature(6, t_fsb).then_inc(t_T.s, 1)
                pe.wait_ge(*t_hh.done(t + 1))
                by_feature(7, t_hhb).then_inc(t_T.s, 1)
                pe.wait_ge(*t_Tc.done(2 * t + 1))
                two(bank(6, TK, 2 * D), t_fT, WA).then_inc(t_A.s, 1)
                pe.wait_ge(*t_Tc.done(2 * t + 2))
                two(bank(7, TK, 2 * D), t_hT, WB).then_inc(t_B.s, 1)
                pe.wait_ge(*t_q.done(t + 1))
                for i in range(4):
                    a = (i + 2) % 4
                    ins = tr(bank(6, 128, TK, i * TK), t_qkb[:, a * 128:(a + 1) * 128])
                ins.then_inc(t_K.s, 1)
            pe.wait_ge(*s_w12.done(2))
            experts(pe, m_early, m_late, m_tail)
            pe.drain().then_inc(phase, 1)
            pe.wait_ge(*ended(5))

            for i in range(2):
                pe.wait_ge(*l_raw.done(i + 1))
                for k in range(NHID):
                    pe.wait_ge(*l_ev.free(i * NHID + k))
                    for c in range(C):
                        a = k * D + c * 128 if i == 0 else c * NHID * 128 + k * 128
                        ins = tr(bank(k % 4, 128, 128, c * 128), l_rawb[:, a:a + 128])
                    ins.then_inc(l_T.s, 1)
            pe.drain().then_inc(phase, 1)
            pe.wait_ge(*ended(6))
            context(1, C, 0)
            pe.drain().then_inc(phase, 1)
            pe.wait_ge(*ended(7))
            fold(1, C, lambda c, jj: WV[:, c, jj * 128:(jj + 1) * 128], lambda jj: WoT[:, jj, :])
            pe.drain().then_inc(phase, 1)
            pe.wait_ge(*ended(8))

            def e_early(j, u):
                t = 2 * j + u
                pe.wait_ge(*e_qs.done(t + 1))
                pe.wait_ge(*e_h.free(t))
                two(bank(0, TK, D), e_qsb[u], M).then_inc(e_o.s, 1)
                pe.wait_ge(*e_yh.done(t + 1))
                pe.wait_ge(*e_yT.free(t))
                by_feature(1, e_yb[u]).then_inc(e_T.s, 1)

            def e_late(j, u):
                t = 2 * j + u
                pe.wait_ge(*e_yT.done(t + 1))
                for a in range(NHID):
                    if a % 2 == 0:
                        pe.wait_ge(*e_g.free(4 * t + a // 2))
                    for c in range(C):
                        ins = mm(bank(2 + (a // 2) % 2, 128, TK, (a % 2) * TK), w1T[:, c, a * 128:(a + 1) * 128],
                                 e_yTb[u][:, c, :], c == 0, c == C - 1)
                    if a % 2:
                        ins.then_inc(e_H.s, 1)
                for i in range(3):
                    group(1, NB + 3 * j + (3 * u + i) // 2, (3 * u + i) % 2)
                pe.wait_ge(*e_g.done(4 * t + 4))
                pe.wait_ge(*e_x.free(t))
                for a in range(NHID):
                    ins = mm(bank(4, TK, D), e_gb[:, a, :], w2T[:, a, :], a == 0, a == NHID - 1)
                ins.then_inc(e_y.s, 1)
            skewed(pe, e_early, e_late)
            pe.drain().then_inc(phase, 1)
            pe.wait_ge(*ended(9))

            pe.wait_ge(*f_w.done(15))
            for a in range(4):
                for c in range(C):
                    ins = tr(bank(a // 2, 128, 128, (a % 2) * 256 + c * 128), f_wx[:, c, a * 128:(a + 1) * 128])
            ins.then_inc(f_T.s, 1)
            pe.wait_ge(*f_blk.done(1))
            pe.wait_ge(*f_Tc.done(2))
            for a in range(4):
                for c in range(C):
                    mm(bank(3 + c, 128, 128, a * 128), f_wxT[:, a, c * 128:(c + 1) * 128], f_blkb[:, 0, :])
                ins = mm(bank(5, TK, 128, a * 128), f_bxb[:, a, :], f_blkb[:, 0, :])
            ins.then_inc(f_P.s, 1)
            pe.wait_ge(*f_ready.done(1))

            def f_early(j, u):
                t = 2 * j + u
                pe.wait_ge(*f_hs.done(t + 1))
                pe.wait_ge(*f_x.free(t))
                for c in range(C):
                    ins = tr(bank(0, TK, 128, c * 128), f_hsb[u][:, c, :])
                ins.then_inc(f_o.s, 1)
                pe.wait_ge(*f_xs.done(t + 1))
                pe.wait_ge(*f_xT.free(t))
                by_feature(1, f_xsb[u]).then_inc(f_tT.s, 1)
                pe.wait_ge(*f_xT.done(t + 1))
                pe.wait_ge(*f_lg.free(t))
                two(bank(2, TK, INNER), f_xTb, f_wxs).then_inc(f_L.s, 1)

            def f_late(j, u):
                t = 2 * j + u
                pe.wait_ge(*f_sw.done(t + 1))
                pe.wait_ge(*f_sT.free(t))
                for a in range(4):
                    ins = tr(bank(3, 128, TK, a * TK), f_lgb[u][:, a * 128:(a + 1) * 128])
                ins.then_inc(f_S.s, 1)
                start = isinstance(j, int) and j == 0 and u == 0
                for a in range(4):
                    ins = mm(bank(4 + a, 128, PITCH), f_lgb[u][:, a * 128:(a + 1) * 128], f_xsb[u], start, False)
                ins.then_inc(f_tok.s, 1)
            skewed(pe, f_early, f_late, peel=1)
            pe.drain().then_inc(phase, 1)
            pe.wait_ge(*ended(10))

            pe.wait_ge(*g_s.done(4))
            for a in range(4):
                for c in range(C):
                    tr(bank(a // 2, 128, 128, (a % 2) * 256 + c * 128), s_s[:, a, c * 128:(c + 1) * 128])
                ins = tr(bank(2, 1, 128, a * 128), s_s[:, a, D:PITCH])
            ins.then_inc(g_T.s, 1)
            pe.wait_ge(*g_Tc.done(3))
            for a in range(4):
                o = bank(3, 128, 128, a * 128)
                for c in range(C):
                    mm(o, f_wfx[:, c, a * 128:(a + 1) * 128], s_sT[:, a, c, :], c == 0, False)
                ins = mm(o, f_bfx[:, a * 128:(a + 1) * 128], s_nr[:, a * 128:(a + 1) * 128], False, True)
            ins.then_inc(g_tok.s, 1)
            pe.wait_ge(*g_tokc.done(4))
            for a in range(4):
                mm(bank(4, 128, 128, a * 128), f_blkb[:, 1, :], s_tb[:, a, :])
                mm(bank(5, 128, 64, a * 64), f_blkb[:, 2, :], s_tc[:, a, :])
                ins = mm(bank(6, 128, 128, a * 128), f_blkb[:, 3, :], s_tb[:, a, :])
            ins.then_inc(g_qkv.s, 1)
            pe.wait_ge(*g_qkvc.done(2))
            pe.wait_ge(*g_kc.done(1))
            for a in range(4):
                mm(bank(7, 128, 64, a * 64), s_q[:, a, :], s_k[:, a, :])
                ins = mm(bank(a // 2, 128, D, (a % 2) * D), s_v[:, a, :], f_wout[:, a, :])
            ins.then_inc(g_sc.s, 1)
            pe.wait_ge(*g_at.done(2))
            for a in range(4):
                ins = tr(bank(2, 128, 128, a * 128), s_at[:, a, :])
            ins.then_inc(g_aT.s, 1)
            pe.wait_ge(*g_aTc.done(1))
            pe.wait_ge(*g_vw.done(2))
            for a in range(4):
                ins = mm(bank(3 + a // 2, 128, D, (a % 2) * D), s_aT[:, a, :], s_vw[:, a, :])
            ins.then_inc(g_M.s, 1)
            pe.wait_ge(*g_Mc.done(2))

            def h_tile(j, u):
                t = 2 * j + u
                pe.wait_ge(*h_ss.done(t + 1))
                pe.wait_ge(*h_ob.free(t))
                for a in range(4):
                    ins = mm(bank(5 + u, TK, D), h_ssb[u][:, a, :], M2[:, a, :], a == 0, a == 3)
                ins.then_inc(h_y.s, 1)
            tiles(pe, h_tile)

        @block.scalar
        def _(act):
            for s in (a_xT, a_sq, a_pr, k_yT, k_k, k_KQ, m_g, t_KQ, l_ev, e_yT, e_g, f_xT, f_sT):
                act.sem_inc(s.s, s.credit)

            def copy(o, i):
                return nc.scalar.activation(o, i, ACT.Copy)

            def blocks(b, p, n):
                return bank(b, p, C * n).rearrange("p (c n) -> p c n", c=C)

            def a_early(j, u):
                t = 2 * j + u
                act.wait_ge(*a_T.done(t + 1))
                copy(a_xTb[u], blocks(u, 128, TK)).then_inc(a_xT.s, 1)
                act.wait_ge(*a_sq.done(t))
                nc.scalar.activation(a_sqb, a_s[u], ACT.Square, accum_out=rr[:, one(t)]).then_inc(a_sq.s, 1)

            def a_late(j, u):
                t = 2 * j + u
                act.wait_ge(*a_p.done(t + 1))
                act.wait_ge(*a_st[u].free(j))
                copy(a_prb[u], bank(2 + u, TK, D)).then_inc(a_pr.s, 1)
            skewed(act, a_early, a_late)
            act.drain().then_inc(phase, 1)
            act.wait_ge(*ended(0))

            act.wait_ge(*w_T.done(1))
            for o, b in ((WA[:, :, 0:D], 0), (r_g2T, 1), (WoT[:, :, :], 2)):
                copy(o, blocks(b, 128, D)).then_inc(w_Tc.s, 1)
            for i in range(3):
                ins = copy(r_qT[i], bank(3, 128, 128, i * 128))
            ins.then_inc(w_Tc.s, 1)
            act.wait_ge(*w_P.done(1))
            copy(WA[:, :, D:2 * D], blocks(0, 128, D))
            copy(rows[:, 3, :], bank(1, TK, D))
            copy(bvc[:, :], bank(1, 128, C, D))
            copy(bqk[:, :], bank(4, TK, 2 * D))
            for c in range(C):
                g = vT[:, V_LN1W + c:V_LN1W + c + 1]
                nc.scalar.activation(WB[:, c, :], bank(2 + c, 128, 2 * D), ACT.Copy, scale=g)
                ins = nc.scalar.activation(WV[:, c, :], bank(5, 128, D, c * D), ACT.Copy, scale=g)
            ins.then_inc(w_Pc.s, 1)

            act.wait_ge(*a_rr.done(2))
            act.wait_ge(*a_st[0].done(T // 2 + 1))
            act.wait_ge(*a_st[1].done(T // 2))

            def k_early(j, u):
                t = 2 * j + u
                act.wait_ge(*k_yT.free(t))
                nc.scalar.activation(a_s[u], tile(XN, t), ACT.Copy, scale=rr[:, one(t)]).then_inc(k_ys.s, 1)
                act.wait_ge(*k_T.done(t + 1))
                copy(a_xTb[u], blocks(u, 128, TK)).then_inc(k_yT.s, 1)

            def k_late(j, u):
                t = 2 * j + u
                act.wait_ge(*k_L.done(t + 1))
                act.wait_ge(*k_sub.done(t + 1))
                copy(k_kb[u], bank(2 + u, TK, 128, 128)).then_inc(k_k.s, 1)
                nc.scalar.activation(k_qb[u], k_qb[u], ACT.Exp).then_inc(k_exp.s, 1)
                act.wait_ge(*k_KT.done(t + 1))
                copy(KQ[:, 0:2, cols(t)], blocks(4 + u, 128, TK)).then_inc(k_KQ.s, 1)
            skewed(act, k_early, k_late)
            act.drain().then_inc(phase, 1)
            act.wait_ge(*ended(1))

            def context(layer, nk):
                act.wait_ge(*c_max[layer].done(1))

                def step(g):
                    for jj in range(nk):
                        act.wait_ge(*c_T[layer].free(g * nk + jj))
                        nc.scalar.activation(c_esb, KQ[:, jj, bass.ds(g * BT * TK, BT * TK)], ACT.Exp,
                                             bias=nmax[:, jj:jj + 1], accum_out=ksum[:, jj, one(g)])\
                            .then_inc(c_es[layer].s, 1)
                with act.Fori(0, NB) as g:
                    step(g)

            context(0, 1)
            nc.scalar.activation(mk, mk, ACT.Exp, bias=nmax[:, 0:1], accum_out=msum)
            act.drain().then_inc(phase, 1)
            act.wait_ge(*ended(2))

            def fold(layer, nk):
                for jj in range(nk):
                    act.wait_ge(*o_pe[layer].done(3 * jj + 1))
                    copy(o_gTb, blocks(0, 128, 128)).then_inc(o_gTc[layer].s, 1)
            act.wait_ge(*o_mT.done(1))
            copy(mkT, bank(3, NM, 128)).then_inc(o_mTc.s, 1)
            fold(0, 1)
            act.drain().then_inc(phase, 1)
            act.wait_ge(*ended(3))
            act.drain().then_inc(phase, 1)
            act.wait_ge(*ended(4))

            def m_early(j, u):
                t = 2 * j + u
                act.wait_ge(*m_bo.done(t + 1))
                nc.scalar.activation(m_sb[u], m_ob, ACT.Square, accum_out=rt[:, u, 40:41]).then_inc(m_ss.s, 1)
                act.wait_ge(*m_T.done(t + 1))
                copy(m_xTb[u], blocks(4, 128, TK)).then_inc(m_xT.s, 1)
                act.wait_ge(*m_mx.done(t + 1))
                nc.scalar.activation(rt[:, u, 8:8 + NE], bank(5, TK, NE), ACT.Exp, bias=rt[:, u, 41:42],
                                     accum_out=rt[:, u, 42:43]).then_inc(m_ex.s, 1)
                act.wait_ge(*m_cT.done(t + 1))
                copy(cT[:, :], bank(4, NE, TK)).then_inc(m_cTc.s, 1)

            def m_late(j, u):
                t = 2 * j + u
                for e in range(NE):
                    act.wait_ge(*m_h.done(NE * t + e + 1))
                    act.wait_ge(*m_y.free(NE * t + e))
                    for a in range(C):
                        b = V_B1 + e * C + a
                        ins = nc.scalar.activation(m_gb[e % 2][:, a, :], bank(e % 2, 128, TK, a * TK), ACT.Gelu,
                                                   bias=vT[:, b:b + 1])
                    ins.then_inc(m_g.s, 1)

            def m_tail(j, u):
                t = 2 * j + u
                act.wait_ge(*t_T.done(2 * t + 1))
                copy(t_fT, blocks(6, 128, TK)).then_inc(t_Tc.s, 1)
                act.wait_ge(*t_T.done(2 * t + 2))
                copy(t_hT, blocks(7, 128, TK)).then_inc(t_Tc.s, 1)
                act.wait_ge(*t_sub.done(t + 1))
                nc.scalar.activation(t_qkb[:, 0:D], t_qkb[:, 0:D], ACT.Exp).then_inc(t_exp.s, 1)
                act.wait_ge(*t_K.done(t + 1))
                copy(KQ[:, :, cols(t)], bank(6, 128, 4 * TK).rearrange("p (c n) -> p c n", c=4))\
                    .then_inc(t_KQ.s, 1)
            experts(act, m_early, m_late, m_tail)
            act.drain().then_inc(phase, 1)
            act.wait_ge(*ended(5))

            for k in range(NHID):
                act.wait_ge(*l_T.done(k + 1))
                for c in range(C):
                    ins = nc.scalar.activation(w1T[:, c, k * 128:(k + 1) * 128], bank(k % 4, 128, 128, c * 128),
                                               ACT.Copy, scale=vT[:, V_LN2W + c:V_LN2W + c + 1])
                ins.then_inc(l_ev.s, 1)
            for k in range(NHID):
                act.wait_ge(*l_T.done(NHID + k + 1))
                copy(w2T[:, k, :], bank(k % 4, 128, D)).then_inc(l_ev.s, 1)
            act.drain().then_inc(phase, 1)
            act.wait_ge(*ended(6))
            context(1, C)
            act.drain().then_inc(phase, 1)
            act.wait_ge(*ended(7))
            fold(1, C)
            act.drain().then_inc(phase, 1)
            act.wait_ge(*ended(8))

            def e_early(j, u):
                t = 2 * j + u
                act.wait_ge(*e_o.free(t))
                copy(e_qsb[u], KQ[:, C:2 * C, cols(t)]).then_inc(e_qs.s, 1)
                act.wait_ge(*e_var.done(t + 1))
                nc.scalar.activation(st[:, u, 9:10], st[:, u, 7:8], ACT.Sqrt, bias=eps[:, 0:1]).then_inc(e_sd.s, 1)
                act.wait_ge(*e_T.done(t + 1))
                copy(e_yTb[u], blocks(1, 128, TK)).then_inc(e_yT.s, 1)

            def e_late(j, u):
                t = 2 * j + u
                act.wait_ge(*e_y.free(t))
                for a in range(NHID):
                    if a % 2 == 0:
                        act.wait_ge(*e_H.done(4 * t + a // 2 + 1))
                    ins = nc.scalar.activation(e_gb[:, a, :], bank(2 + (a // 2) % 2, 128, TK, (a % 2) * TK),
                                               ACT.Gelu, bias=bm[:, a:a + 1])
                    if a % 2:
                        ins.then_inc(e_g.s, 1)
            skewed(act, e_early, e_late)
            act.drain().then_inc(phase, 1)
            act.wait_ge(*ended(9))
            act.wait_ge(*f_T.done(1))
            for i in range(2):
                copy(f_wxT[:, 2 * i:2 * i + 2, :], blocks(i, 128, D)).then_inc(f_Tc.s, 1)

            def f_early(j, u):
                t = 2 * j + u
                act.wait_ge(*f_tT.done(t + 1))
                copy(f_xTb, blocks(1, 128, TK)).then_inc(f_xT.s, 1)

            def f_late(j, u):
                t = 2 * j + u
                act.wait_ge(*f_sub.done(t + 1))
                nc.scalar.activation(f_lgb[u], f_lgb[u], ACT.Exp).then_inc(f_exp.s, 1)
                act.wait_ge(*f_S.done(t + 1))
                copy(KQ[:, :, cols(t)], bank(3, 128, 4 * TK).rearrange("p (c n) -> p c n", c=4))\
                    .then_inc(f_sT.s, 1)
            skewed(act, f_early, f_late)
            act.drain().then_inc(phase, 1)
            act.wait_ge(*ended(10))

            act.wait_ge(*g_T.done(1))
            for i in range(2):
                copy(s_sT[:, 2 * i:2 * i + 2].rearrange("p a c n -> p (a c n)"), bank(i, 128, 512))\
                    .then_inc(g_Tc.s, 1)
            copy(s_nr, bank(2, 1, INNER)).then_inc(g_Tc.s, 1)
            act.wait_ge(*g_qkv.done(1))
            copy(s_q.rearrange("p a n -> p (a n)"), bank(4, 128, 512)).then_inc(g_qkvc.s, 1)
            copy(s_v.rearrange("p a n -> p (a n)"), bank(6, 128, 512)).then_inc(g_qkvc.s, 1)
            act.wait_ge(*g_sc.done(1))
            for i in range(2):
                copy(s_vw[:, 2 * i:2 * i + 2, :], blocks(i, 128, D)).then_inc(g_vw.s, 1)
            act.wait_ge(*g_mx.done(2))
            for a in range(4):
                ins = nc.scalar.activation(s_ec[:, a, :], bank(7, 128, 64, a * 64), ACT.Exp, scale=64 ** -0.5,
                                           bias=small[:, 36 + a:37 + a], accum_out=small[:, 40 + a:41 + a])
            ins.then_inc(g_ex.s, 1)

        @block.vector
        def _(dve):
            v = nc.vector
            for s in (g_acc[0], c_er[0], k_sub, m_x, m_acc, e_h, e_x, f_x, f_lg, h_ob):
                dve.sem_inc(s.s, s.credit)
            v.memset(HT[:, :, :], 0.0)
            v.memset(rt[:, :, :], -1.0)
            v.memset(eps[:, :], EPS)

            once = Steps(dve, dve_steps, 0, passed)
            once.tile(0)

            def plainly(*waits):
                for s, n in waits:
                    dve.wait_ge(s, n)
                dve.sem_inc(passed, 1)

            def norm(st_, o, i, done, var, rstd, n):
                done(v.bn_stats(st_[:, 0:6], i), plain=True)
                done(v.bn_aggr(st_[:, 6:8], st_[:, 0:6]))
                v.tensor_scalar(st_[:, 7:8], st_[:, 7:8], EPS, None, ALU.add).then_inc(var.s, 1)
                dve.wait_ge(*rstd.done(n + 1))
                return v.tensor_scalar(o, i, st_[:, 6:7], st_[:, 8:9], ALU.subtract, ALU.mult)

            def wide(a, n, w):
                return a.rearrange("p (n b) -> p n b", b=1).to_broadcast([a.shape[0], n, w])

            def heads(a, w):
                return a.rearrange("p (h w) -> p h w", w=w)

            def one_hots(layer, h, b):
                g = 2 * h + b
                dve.wait_ge(*g_agg[layer].free(g))
                for k in range(GK):
                    c = g * GK + k
                    if layer == 0:
                        ins = v.tensor_scalar(onehot[:, b, k, :], iota[:, :], dst_r[:, one(c)], w_e[:, one(c)],
                                              ALU.is_equal, ALU.mult)
                    else:
                        ins = v.tensor_scalar(onehot[:, b, k, :], iota[:, :], dst_r[:, one(c)], None, ALU.is_equal)
                ins.then_inc(g_oh[layer].s, 1)

            def add(layer, h, b):
                g = 2 * h + b
                r = dve.value_load(base[0:1, one(g)], min_val=0, max_val=N - 1)
                dve.wait_ge(*g_agg[layer].done(g + 1))
                dve.wait_ge(*g_acc[layer].done(g))
                o = HT[:, :, bass.ds(r, W)]
                v.tensor_tensor(o, o, bank(6 + b, 128, C * W).rearrange("p (c n) -> p c n", c=C), ALU.add)\
                    .then_inc(g_acc[layer].s, 1)

            dve.wait_ge(*s_in.done(22))
            v.tensor_copy(e_f[:, 0:2], e_i).then_inc(s_rel.s, 1)
            dve.wait_ge(*s_rel.done(1))
            v.tensor_scalar(e_f[:, 1], e_f[:, 1], e_f[:, 1, 0, 0:1], None, ALU.subtract).then_inc(s_rel.s, 1)
            for a, o in enumerate((src_i, dst_r, w_e)):
                dve.wait_ge(*s_tT.done(a + 1))
                v.tensor_copy(o[:, :].rearrange("e (g k) -> e g k", k=GK),
                              bank(a, TK, NCH).rearrange("e (k g) -> e g k", k=GK)).then_inc(s_tab.s, 1)
            dve.wait_ge(*s_vT.done(1))
            v.tensor_copy(vT[:, 0:NV], bank(3, 128, NV)).then_inc(s_vTc.s, 1)
            v.tensor_copy(rT[:, :, :], bank(3, 128, C * NE, 64).rearrange("p (c n) -> p c n", c=C))\
                .then_inc(s_vTc.s, 1)
            v.tensor_copy(mvT, bank(3, NM, 128, 256)).then_inc(s_vTc.s, 1)
            dve.wait_ge(*s_vTc.done(1))
            for c in range(C):
                v.tensor_scalar(Wg[:, c, :], Wg[:, c, :], vT[:, V_GPRE + c:V_GPRE + c + 1], float(D) ** 0.5,
                                ALU.mult, ALU.mult)
            v.tensor_scalar(rows[:, 2, :], rows[:, 2, :], float(D) ** 0.5, None, ALU.mult)

            sa = Steps(dve, a_dve, 2, passed)

            def a_tile(j, u):
                t = 2 * j + u
                sa.tile(t)
                plainly(a_xT.free(t), a_sq.free(t), a_kept.free(t))
                norm(st[:, u], a_s[u], tile(X, t), sa.done, a_var, a_rstd, t).then_inc(a_xs.s, 1)
                sa.end()
            dve.wait_ge(*s_x.done(NB))
            tiles(dve, a_tile)
            dve.drain().then_inc(phase, 1)
            dve.wait_ge(*ended(0))
            dve.wait_ge(*a_rr.done(2))

            dve.wait_ge(*s_w.done(18))
            for i in range(3):
                v.tensor_tensor(heads(r_q[i], 32), heads(mask32[:, :], 32),
                                r_q32[i].rearrange("p (a n) -> p a n", a=1).to_broadcast([128, 4, 32]), ALU.mult)\
                    .then_inc(w_blk.s, 1)
            for a in range(C):
                ins = v.tensor_tensor_reduce(r_jk, r_x[:, a, :], r_b, 1.0, 0.0, ALU.mult, ALU.add,
                                             r_xb0[:, a:a + 1])
                once.done(ins)
            once.done(v.tensor_tensor(r_xb, r_xb0, vT[:, V_BX:V_BX + C], ALU.add))
            v.tensor_copy(r_xbb, wide(r_xb, C, TK))
            v.tensor_copy(r_b3b, wide(vT[:, V_B3:V_B3 + C], C, TK)).then_inc(w_b.s, 1)

            sk = Steps(dve, k_dve, 3, passed)
            one_hots(0, 0, 0)
            dve.wait_ge(*a_st[0].done(T // 2 + 1))
            dve.wait_ge(*a_st[1].done(T // 2))

            def k_tile(j, u):
                t = 2 * j + u
                sk.tile(t)
                dve.wait_ge(*k_L.done(t + 1))
                L = heads(bank(2 + u, TK, 128), 32)
                q = heads(k_qb[u], 32)
                sk.done(v.tensor_reduce(qst[:, u, 0:4], L, AX, ALU.max))
                dve.wait_ge(*k_KQ.free(t))
                v.tensor_tensor(q, L, wide(qst[:, u, 0:4], 4, 32), ALU.subtract).then_inc(k_sub.s, 1)
                one_hots(0, j + (u + 1) // 2, (u + 1) % 2)
                dve.wait_ge(*k_exp.done(t + 1))
                sk.done(v.tensor_reduce(qst[:, u, 4:8], q, AX, ALU.add))
                sk.done(v.reciprocal(qst[:, u, 8:12], qst[:, u, 4:8]))
                v.tensor_tensor(q, q, wide(qst[:, u, 8:12], 4, 32), ALU.mult).then_inc(k_q.s, 1)
                add(0, j, u)
                sk.end()
            tiles(dve, k_tile)
            dve.drain().then_inc(phase, 1)
            dve.wait_ge(*ended(1))

            def context(layer, nk, first):
                for jj in range(nk):
                    once.done(v.tensor_reduce(kmax[:, jj:jj + 1], KQ[:, jj, :], AX, ALU.max))
                if layer == 0:
                    once.done(v.tensor_reduce(small[:, 11:12], mk, AX, ALU.max))
                    once.done(v.tensor_tensor(kmax[:, 0:1], kmax[:, 0:1], small[:, 11:12], ALU.max))
                v.tensor_scalar(nmax[:, 0:nk], kmax[:, 0:nk], -1.0, None, ALU.mult).then_inc(c_max[layer].s, 1)

                def step(g, h0, last=False):
                    if layer == 1:
                        dve.wait_ge(*c_G[layer].free(g * nk))
                        for i in range(BT):
                            n = g * BT + i
                            ins = v.tensor_scalar(c_hhb[:, i, :], tile(XN, n), tile(MV, n)[:, 0:1], tile(MV, n)[:, 1:2],
                                                  ALU.subtract, ALU.mult)
                        ins.then_inc(c_hh.s, 1)
                    for jj in range(nk):
                        n = g * nk + jj
                        dve.wait_ge(*c_T[layer].done(n + 1))
                        dve.wait_ge(*c_G[layer].free(n))
                        for b, a, k in ((0, 0, 4), (1, 4, 1)):
                            i = bank(b, TK, k * 128).rearrange("p (a n) -> p a n", n=128)
                            if layer == 0:
                                ins = v.tensor_tensor(c_erb[:, a:a + k, :], i,
                                                      wide(rr[:, bass.ds(g * BT + a, k)], k, 128), ALU.mult)
                            else:
                                ins = v.tensor_copy(c_erb[:, a:a + k, :], i)
                        ins.then_inc(c_er[layer].s, 1)
                        if jj == 0:
                            for b in range(2):
                                q = first % 2 + b
                                one_hots(layer, h0 + (q + 1) // 2, (q + 1) % 2)
                                add(layer, h0 + q // 2, q % 2)
                with dve.Fori(0, NB) as g:
                    step(g, g + first // 2)

            context(0, 1, T)
            dve.drain().then_inc(phase, 1)
            dve.wait_ge(*ended(2))

            def fold(layer, nk, scale):
                for jj in range(nk):
                    once.done(v.tensor_reduce(den[:, jj:jj + 1], ksum[:, jj, :], AX, ALU.add))
                    if layer == 0:
                        once.done(v.tensor_tensor(den[:, 0:1], den[:, 0:1], msum, ALU.add))
                    once.done(v.reciprocal(small[:, 24 + jj:25 + jj], den[:, jj:jj + 1]))
                if layer == 0:
                    v.tensor_scalar(o_mkb, mk, small[:, 24:25], None, ALU.mult).then_inc(o_mem.s, 1)
                for jj in range(nk):
                    v.tensor_scalar(o_gb, bank(4 + jj, 128, D), small[:, 24 + jj:25 + jj], None, ALU.mult)\
                        .then_inc(o_v[layer].s, 1)
                    dve.wait_ge(*o_pe[layer].done(3 * jj + 2))
                    if layer == 0:
                        ins = v.tensor_tensor(o_kvb, bank(1, 128, 128), mask32[:, :], ALU.mult)
                    else:
                        ins = v.scalar_tensor_tensor(out=o_kvb, in0=bank(1, 128, 128), scalar=bvc[:, jj:jj + 1],
                                                     in1=mask32[:, :], op0=ALU.add, op1=ALU.mult)
                    ins.then_inc(o_v[layer].s, 1)
                    dve.wait_ge(*o_pe[layer].done(3 * jj + 3))
                    v.tensor_scalar(M[:, jj, :], bank(2, 128, D), scale, None, ALU.mult).then_inc(o_v[layer].s, 1)
            fold(0, 1, 32 ** -0.5)
            dve.drain().then_inc(phase, 1)
            dve.wait_ge(*ended(3))

            first = T + 2 * NB
            with dve.Fori(0, (NG - first) // 2 - 1) as j:
                for i in range(2):
                    one_hots(0, j + (first + i + 1) // 2, (first + i + 1) % 2)
                    add(0, j + (first + i) // 2, (first + i) % 2)
            one_hots(0, NG // 2, 0)
            add(0, NG // 2 - 1, 1)
            add(0, NG // 2, 0)
            dve.drain().then_inc(phase, 1)
            dve.wait_ge(*ended(4))

            sm, stl = Steps(dve, m_dve, 15, passed), Steps(dve, t_dve, 8, passed)

            def m_early(j, u):
                t = 2 * j + u
                sm.tile(t)
                n, r, Xt = sm.done, rt[:, u], tile(X, t)
                dve.wait_ge(*m_o.done(t + 1))
                v.tensor_tensor(m_ob, bank(5, TK, D), rows[:, 1, :], ALU.add).then_inc(m_bo.s, 1)
                v.tensor_tensor(m_gnb, bank(5, TK, D, D), rows[:, 0, :], ALU.add)
                dve.wait_ge(*m_ss.done(t + 1))
                v.tensor_scalar(r[:, 40:41], r[:, 40:41], 1e-24, None, ALU.max).then_inc(m_sq.s, 1)
                dve.wait_ge(*m_rn.done(t + 1))
                n(v.scalar_tensor_tensor(out=m_ob, in0=m_ob, scalar=r[:, 43:44], in1=rows[:, 2, :],
                                         op0=ALU.mult, op1=ALU.mult))
                n(v.scalar_tensor_tensor(out=m_gnb, in0=m_gnb, scalar=0.0, in1=m_ob, op0=ALU.max, op1=ALU.add))
                n(v.tensor_tensor(Xt, Xt, m_gnb, ALU.add), plain=True)
                norm(st[:, u], m_sb[u], Xt, n, m_var, m_rstd, t).then_inc(m_xs.s, 1)
                dve.wait_ge(*m_r.done(t + 1))
                v.tensor_reduce(r[:, 41:42], bank(5, TK, NE), AX, ALU.max, negate=True).then_inc(m_mx.s, 1)
                n(v.tensor_tensor(Xt, Xt, m_sb[u], ALU.add))
                dve.wait_ge(*m_ex.done(t + 1))
                n(v.reciprocal(r[:, 44:45], r[:, 42:43]))
                n(v.tensor_scalar(r[:, 8:8 + NE], r[:, 8:8 + NE], r[:, 44:45], None, ALU.mult), plain=True)
                n(v.max(r[:, 24:32], r[:, 8:8 + NE]))
                n(v.tensor_copy(r[:, 32:34], r[:, 24:26]))
                n(v.tensor_tensor(r[:, 45:46], r[:, 24:25], r[:, 25:26], ALU.add))
                n(v.tensor_scalar(r[:, 45:46], r[:, 45:46], 1e-12, None, ALU.max), plain=True)
                n(v.match_replace(out=rt2[:, :], in_to_replace=r[:, 32:40], in_values=r[:, 8:22], imm_value=0.0))
                n(v.reciprocal(r[:, 46:47], r[:, 45:46]))
                n(v.tensor_tensor(r[:, 0:NE], r[:, 8:8 + NE], rt2[:, 0:NE], ALU.subtract))
                v.tensor_scalar(r[:, 0:NE], r[:, 0:NE], r[:, 46:47], None, ALU.mult).then_inc(m_c.s, 1)
                dve.wait_ge(*m_b.done(t + 1))
                v.tensor_tensor(Xt, Xt, bank(5, TK, D), ALU.add).then_inc(m_x.s, 1)
                sm.end()

            def m_late(j, u):
                t = 2 * j + u
                Xt = tile(X, t)
                for e in range(NE):
                    dve.wait_ge(*m_y.done(NE * t + e + 1))
                    dve.wait_ge(*m_acc.done(NE * t + e)) if e else dve.wait_ge(*m_x.done(t + 1))
                    v.scalar_tensor_tensor(out=Xt, in0=bank(2 + e % 2, TK, D), scalar=rt[:, u, e:e + 1], in1=Xt,
                                           op0=ALU.mult, op1=ALU.add).then_inc(m_acc.s, 1)

            def m_tail(j, u):
                t = 2 * j + u
                stl.tile(t)
                n, Xt = stl.done, tile(X, t)
                plainly(m_acc.done(NE * t + NE), t_kept.free(t), t_T.free(2 * t))
                norm(st2[:, 0], t_fsb, Xt, n, t_var, t_rstd, 2 * t).then_inc(t_fs.s, 1)
                plainly(t_fs.done(t + 1), t_T.free(2 * t + 1))
                norm(st2[:, 1], t_hhb, t_fsb, n, t_var, t_rstd, 2 * t + 1).then_inc(t_hh.s, 1)
                v.tensor_copy(tile(MV, t), st2[:, 1, 6:9:2])
                dve.wait_ge(*t_A.done(t + 1))
                dve.wait_ge(*t_st[u].free(j))
                v.tensor_tensor(t_prb[u], bank(6, TK, D, D), rows[:, 3, :], ALU.add).then_inc(t_pr.s, 1)
                v.tensor_tensor(Xt, Xt, bank(6, TK, D), ALU.add)
                dve.wait_ge(*t_B.done(t + 1))
                dve.wait_ge(*t_K.free(t))
                n(v.tensor_tensor(t_qkb, bank(7, TK, 2 * D), bqk[:, :], ALU.add))
                q, qs = heads(t_qkb[:, 0:D], 32), qst[:, u]
                n2 = qs[:, 0:H1]
                n(v.tensor_reduce(n2, q, AX, ALU.max))
                v.tensor_tensor(q, q, wide(n2, H1, 32), ALU.subtract).then_inc(t_sub.s, 1)
                dve.wait_ge(*t_exp.done(t + 1))
                n(v.tensor_reduce(qs[:, H1:2 * H1], q, AX, ALU.add))
                n(v.reciprocal(qs[:, 2 * H1:3 * H1], qs[:, H1:2 * H1]))
                v.tensor_tensor(q, q, wide(qs[:, 2 * H1:3 * H1], H1, 32), ALU.mult).then_inc(t_q.s, 1)
                stl.end()
            experts(dve, m_early, m_late, m_tail)
            dve.drain().then_inc(phase, 1)
            dve.wait_ge(*ended(5))

            v.memset(HT[:, :, :], 0.0)
            dve.wait_ge(*l_row.done(3))
            dve.wait_ge(*l_raw.done(1))
            for k in range(NHID):
                if k:
                    dve.wait_ge(*l_b.done(k))
                v.tensor_tensor_reduce(l_jk, l_rawb[:, k * D:(k + 1) * D], l_bb, 1.0, 0.0, ALU.mult, ALU.add,
                                       bm[:, k:k + 1]).then_inc(l_b.s, 1)
            dve.wait_ge(*l_b.done(NHID))
            v.tensor_tensor(bm, bm, vT[:, V_BM1:V_BM1 + NHID], ALU.add)
            dve.wait_ge(*t_st[0].done(T // 2 + 1))
            dve.wait_ge(*t_st[1].done(T // 2))
            one_hots(1, 0, 0)
            dve.drain().then_inc(phase, 1)
            dve.wait_ge(*ended(6))
            context(1, C, 0)
            dve.drain().then_inc(phase, 1)
            dve.wait_ge(*ended(7))
            fold(1, C, 1.0)
            dve.drain().then_inc(phase, 1)
            dve.wait_ge(*ended(8))

            se = Steps(dve, e_dve, 4, passed)

            def e_early(j, u):
                t = 2 * j + u
                se.tile(t)
                dve.wait_ge(*e_o.done(t + 1))
                se.done(v.tensor_tensor(e_hb[u], bank(0, TK, D), rows[:, 0, :], ALU.add))
                v.tensor_tensor(e_hb[u], e_hb[u], tile(XN, t), ALU.add).then_inc(e_h.s, 1)
                plainly(e_h.done(t + 1), e_T.free(t))
                se.done(v.bn_stats(st[:, u, 0:6], e_hb[u]), plain=True)
                v.bn_aggr(st[:, u, 6:8], st[:, u, 0:6]).then_inc(e_var.s, 1)
                dve.wait_ge(*e_sd.done(t + 1))
                se.done(v.reciprocal(st[:, u, 8:9], st[:, u, 9:10]))
                v.tensor_scalar(e_yb[u], e_hb[u], st[:, u, 6:7], st[:, u, 8:9], ALU.subtract, ALU.mult)\
                    .then_inc(e_yh.s, 1)
                se.done(v.tensor_tensor(e_hb[u], e_hb[u], rows[:, 1, :], ALU.add))

            def e_late(j, u, last=False):
                t = 2 * j + u
                for i in range(3):
                    q = 3 * u + i
                    if not (last and i == 2):
                        one_hots(1, NB + 3 * j + (q + 1) // 2, (q + 1) % 2)
                    add(1, NB + 3 * j + q // 2, q % 2)
                Xt = tile(X, t)
                v.tensor_tensor(Xt, Xt, e_hb[u], ALU.add).then_inc(e_hx.s, 1)
                dve.wait_ge(*e_y.done(t + 1))
                dve.wait_ge(*e_hx.done(t + 1))
                v.tensor_tensor(Xt, Xt, bank(4, TK, D), ALU.add).then_inc(e_x.s, 1)
            e_early(0, 0)
            with dve.Fori(0, T // 2) as j:
                for u in range(2):
                    e_early(j + (u + 1) // 2, (u + 1) % 2)
                    e_late(j, u)
            e_late(T // 2, 0, last=True)
            dve.drain().then_inc(phase, 1)
            dve.wait_ge(*ended(9))

            dve.wait_ge(*f_w.done(15))
            once.done(v.memset(f_blkb, 0.0))
            v.tensor_copy(f_blkb[0:64, :, 0:64], f_raw[0:64])
            v.tensor_copy(f_bxb, wide(vT[:, V_BSX:V_BSX + 4], 4, TK))
            v.tensor_copy(f_blkb[64:128, :, 64:128], f_raw[64:128]).then_inc(f_blk.s, 1)
            once.done(v.tensor_scalar(f_temp, f_temp, 0.1, 5.0, ALU.max, ALU.min))
            once.done(v.reciprocal(small[:, 44:52], f_temp))
            dve.wait_ge(*f_P.done(1))
            for c in range(C):
                v.tensor_tensor(heads(f_wxs[:, c, :], 64), heads(bank(3 + c, 128, INNER), 64),
                                wide(small[:, 44:52], HS, 64), ALU.mult)
            once.done(v.tensor_tensor(heads(f_bxs, 64), heads(bank(5, TK, INNER), 64),
                                    f_bsl.rearrange("p (a n) -> p a n", a=1).to_broadcast([TK, HS, 64]), ALU.add))
            once.done(v.tensor_tensor(heads(f_bxs, 64), heads(f_bxs, 64), wide(small[0:TK, 44:52], HS, 64), ALU.mult))
            dve.drain().then_inc(f_ready.s, 1)
            dve.wait_ge(*f_one.done(1))

            sf, sg = Steps(dve, f_dve, 2, passed), Steps(dve, f_sdve, 3, passed)

            def f_early(j, u):
                t = 2 * j + u
                sf.tile(t)
                Xt = tile(X, t)
                dve.wait_ge(*f_o.done(t + 1))
                v.tensor_tensor(Xt, Xt, bank(0, TK, D), ALU.add).then_inc(f_x.s, 1)
                plainly(f_x.done(t + 1), f_tok.free(t))
                norm(st[:, u], f_xsb[u][:, 0:D], Xt, sf.done, f_var, f_rstd, t).then_inc(f_xs.s, 1)
                sf.end()

            def f_late(j, u):
                t = 2 * j + u
                sg.tile(t)
                dve.wait_ge(*f_L.done(t + 1))
                L, s = heads(f_lgb[u], 64), qst[:, u]
                v.tensor_tensor(f_lgb[u], bank(2, TK, INNER), f_bxs, ALU.add).then_inc(f_lg.s, 1)
                dve.wait_ge(*f_lg.done(t + 1))
                sg.done(v.tensor_reduce(s[:, 0:HS], L, AX, ALU.max))
                v.tensor_tensor(L, L, wide(s[:, 0:HS], HS, 64), ALU.subtract).then_inc(f_sub.s, 1)
                dve.wait_ge(*f_exp.done(t + 1))
                sg.done(v.tensor_reduce(s[:, HS:2 * HS], L, AX, ALU.add))
                sg.done(v.reciprocal(s[:, 2 * HS:3 * HS], s[:, HS:2 * HS]))
                v.tensor_tensor(L, L, wide(s[:, 2 * HS:3 * HS], HS, 64), ALU.mult).then_inc(f_sw.s, 1)
                sg.end()
            skewed(dve, f_early, f_late)
            dve.drain().then_inc(phase, 1)
            dve.wait_ge(*ended(10))

            for a in range(4):
                once.done(v.tensor_scalar(small[:, 32 + a:33 + a], bank(4 + a, 128, 1, D), 1e-5, None, ALU.add))
            once.done(v.reciprocal(small[:, 52:56], small[:, 32:36]))
            for a in range(4):
                v.tensor_scalar(s_s[:, a, :], bank(4 + a, 128, PITCH), small[:, 52 + a:53 + a], None, ALU.mult)\
                    .then_inc(g_s.s, 1)
            once.done(v.memset(s_tb, 0.0))
            once.done(v.memset(s_at, 0.0))
            dve.wait_ge(*g_tok.done(1))
            P3 = bank(3, 128, 512).rearrange("p (a n) -> p a n", a=4)
            for lo in (0, 64):
                for o in (s_tc[lo:lo + 64], s_tb[lo:lo + 64, :, lo:lo + 64]):
                    v.tensor_copy(o, P3[lo:lo + 64, :, lo:lo + 64]).then_inc(g_tokc.s, 1)
            dve.wait_ge(*g_qkv.done(1))
            v.tensor_copy(s_k.rearrange("p a n -> p (a n)"), bank(5, 128, 256)).then_inc(g_kc.s, 1)
            dve.wait_ge(*g_sc.done(1))
            v.tensor_reduce(small[:, 32:36], bank(7, 128, 256).rearrange("p (a n) -> p a n", a=4), AX, ALU.max)\
                .then_inc(g_mx.s, 1)
            dve.wait_ge(*g_mx.done(1))
            v.tensor_scalar(small[:, 36:40], small[:, 32:36], -(64 ** -0.5), None, ALU.mult).then_inc(g_mx.s, 1)
            dve.wait_ge(*g_ex.done(1))
            once.done(v.reciprocal(small[:, 52:56], small[:, 40:44]))
            for lo in (0, 64):
                v.tensor_tensor(s_at[lo:lo + 64, :, lo:lo + 64], s_ec[lo:lo + 64],
                                wide(small[lo:lo + 64, 52:56], 4, 64), ALU.mult).then_inc(g_at.s, 1)
            dve.wait_ge(*g_aT.done(1))
            v.tensor_copy(s_aT.rearrange("p a n -> p (a n)"), bank(2, 128, 512)).then_inc(g_aTc.s, 1)
            dve.wait_ge(*g_M.done(1))
            for i in range(2):
                v.tensor_copy(M2[:, 2 * i:2 * i + 2, :], bank(3 + i, 128, 512).rearrange("p (a n) -> p a n", a=2))\
                    .then_inc(g_Mc.s, 1)

            def h_tile(j, u):
                t = 2 * j + u
                dve.wait_ge(*h_ss.done(t + 1))
                dve.wait_ge(*h_y.done(t + 1))
                dve.wait_ge(*h_st[u].free(j))
                v.tensor_tensor(h_obb[u], tile(X, t), bank(5 + u, TK, D), ALU.add).then_inc(h_ob.s, 1)
            tiles(dve, h_tile)


_INS = ['x', 'src', 'dst', 'edge_weight', 'L0_gnn_W', 'L0_gnn_b', 'L0_mix_w_qkv', 'L0_mix_mem_kv',
        'L0_mix_w_out', 'L0_mix_b_out', 'L0_mix_g_out', 'L0_mix_g_pre', 'L0_ffn_router_w', 'L0_ffn_w1',
        'L0_ffn_b1', 'L0_ffn_w2', 'L0_ffn_b2', 'L1_gnn_w1', 'L1_gnn_w2', 'L1_gnn_w3', 'L1_gnn_b3',
        'L1_mix_ln1_w', 'L1_mix_ln1_b', 'L1_mix_Wx', 'L1_mix_bx', 'L1_mix_Wq', 'L1_mix_Wk', 'L1_mix_Wv',
        'L1_mix_Wo', 'L1_mix_bo', 'L1_mix_ln2_w', 'L1_mix_ln2_b', 'L1_mix_W1', 'L1_mix_b1', 'L1_mix_W2',
        'L1_mix_b2', 'L1_ffn_W_fx', 'L1_ffn_b_fx', 'L1_ffn_W_x', 'L1_ffn_b_x', 'L1_ffn_W_slice',
        'L1_ffn_b_slice', 'L1_ffn_W_q', 'L1_ffn_W_k', 'L1_ffn_W_v', 'L1_ffn_W_out', 'L1_ffn_b_out',
        'L1_ffn_temperature']
_OUTS = [((N, D), 'float32')]


def kernel(**inputs):
    import numpy as _np
    import concourse.bacc as _bacc
    from concourse import mybir as _mybir
    from concourse.bass_utils import run_bass_kernel_spmd as _run

    nc = _bacc.Bacc("TRN2", target_bir_lowering=False, num_devices=1)
    arrays, args = {}, []
    for name in _INS:
        a = _np.ascontiguousarray(inputs[name])
        arrays[f"in_{name}_dram"] = a
        args.append(nc.dram_tensor(f"in_{name}_dram", a.shape, _mybir.dt.from_np(a.dtype), kind="ExternalInput").ap())
    for i, (shape, dtype) in enumerate(_OUTS):
        dt = _mybir.dt.from_np(_np.dtype(dtype))
        args.append(nc.dram_tensor(f"out_{i}_dram", shape, dt, kind="ExternalOutput").ap())
    build(nc, *args)
    r = _run(nc, [arrays], core_ids=[0])
    return r.results[0]["out_0_dram"]
```

```python
from contextlib import ExitStack

import concourse.bass as bass
from concourse import mybir

F32 = mybir.dt.float32
I32 = mybir.dt.int32
ALU = mybir.AluOpType
ACT = mybir.ActivationFunctionType
AX = mybir.AxisListType.X

N = 3125
D = 256
TK = 125
T = N // TK
C = D // 128
E = 53125
NCH = E // TK
GK = 5
NG = NCH // GK
W = 96
HTW = N + W
BT = 5
NB = T // BT
NE = 8
NM = 4
NHID = 8
H1 = 8
HS = 8
INNER = 512
G0 = T + 2 * NB
T_G = (NG - G0 + 1) // 3
GSLOTS = (1, 5, 6)
LOOPED = (T_G - 3) // 2
PITCH = D + 1
EPS = 1e-5


class Steps:

    def __init__(self, eng, sem, per, passed):
        self.eng, self.sem, self.per, self.passed, self.k = eng, sem, per, passed, 0

    def tile(self, t):
        self.base, self.k = t * self.per, 0

    def done(self, ins, plain=False):
        self.k += 1
        ins.then_inc(self.sem, 1)
        self.eng.wait_ge(self.sem, self.base + self.k)
        if plain:
            self.eng.sem_inc(self.passed, 1)

    def end(self):
        assert self.k == self.per, (self.k, self.per)


def build(nc, x, src, dst, edge_weight, W0g, b0g, wqkv, mem_kv, wout0, bout0, gout0, gpre, router, we1, be1,
          we2, be2, g1w1, g1w2, g1w3, g1b3, ln1w, ln1b, Wx, bx, Wq, Wk, Wv, Wo, bo, ln2w, ln2b, Wm1, bm1, Wm2, bm2,
          Wfx, bfx, Wsx, bsx, Wsl, bsl, Wsq, Wsk, Wsv, Wout, bout, temp, out):
    table = [nc.dram_tensor(f"table{i}", (N, D), F32, kind="Internal").ap() for i in range(2)]
    with ExitStack() as ctx:
        def sb(name, shape, dt=F32):
            return ctx.enter_context(nc.sbuf_tensor(name, shape, dt))

        def sem(name):
            return ctx.enter_context(nc.semaphore(name))

        X = sb("X", [TK, T, D])
        XN = sb("XN", [TK, T, D])
        KQ = sb("KQ", [128, 4, N])
        HT = sb("HT", [128, C, HTW])
        big = sb("big", [128, 8192])
        stg = sb("stg", [128, 2562])
        onehot = sb("onehot", [TK, 2, GK, W])
        src_i = sb("src_i", [TK, NCH], I32)
        dst_r = sb("dst_r", [TK, NCH])
        w_e = sb("w_e", [TK, NCH])
        tq = sb("tq", [TK, 3 * D])
        idx = sb("idx", [TK, 2, GK], I32)
        base = sb("base", [1, NG], I32)
        iota = sb("iota", [TK, W])
        ident = sb("ident", [128, 128])
        mask32 = sb("mask32", [128, 128])
        WA = sb("WA", [128, C, 2 * D])
        WB = sb("WB", [128, C, 2 * D])
        WV = sb("WV", [128, C, D])
        WoT = sb("WoT", [128, C, D])
        M = sb("M", [128, C, D])
        rT = sb("rT", [128, C, NE])
        vecs = sb("vecs", [48, 128])
        vT = sb("vT", [128, 48])
        b2row = sb("b2row", [NE, D])
        rows = sb("rows", [TK, 4, D])
        bqk = sb("bqk", [TK, 2 * D])
        bvc = sb("bvc", [128, C])
        rr = sb("rr", [TK, T])
        kmax = sb("kmax", [128, C])
        ksum = sb("ksum", [128, C, NB])
        small = sb("small", [128, 64])
        MV = sb("MV", [TK, T, 2])
        st = sb("st", [TK, 2, 10])
        st2 = sb("st2", [TK, 2, 10])
        qst = sb("qst", [TK, 2, 3 * H1])
        fsx = sb("fsx", [128, 4, D])
        rt = sb("rt", [TK, 2, 48])
        rt2 = sb("rt2", [TK, 14])
        cT = sb("cT", [NE, TK])
        eps = sb("eps", [TK, 1])
        neghalf = sb("neghalf", [TK, T])
        pb = ctx.enter_context(nc.psum_tensor("pb", [128, 8, 512], F32))

        V_GPRE, V_B1, V_LN1W, V_BX, V_LN2W, V_BM1, V_B3, V_BSX = 0, 2, 18, 20, 22, 24, 32, 34
        NV = 38
        VECS = ((gpre, V_GPRE), (be1, V_B1), (ln1w, V_LN1W), (bx, V_BX), (ln2w, V_LN2W), (bm1, V_BM1),
                (g1b3, V_B3), (bsx, V_BSX))

        def part(buf, at, shape):
            n = 1
            for s in shape[1:]:
                n *= s
            v = buf[0:shape[0], at:at + n]
            if len(shape) == 3:
                v = v.rearrange("p (a b) -> p a b", b=shape[2])
            if len(shape) == 4:
                v = v.rearrange("p (a b c) -> p a b c", b=shape[2], c=shape[3])
            return v

        rows_ = part(big, 4096, [TK, 2, GK, D])
        ring = [[rows_[:, b, k, :] for k in range(GK)] for b in range(2)]
        ring2 = [[XN[:, T - 1 - k, :] for k in range(GK)],
                 [KQ[0:TK, (0, 2, 3)[k // 2], N - (1 + k % 2) * D:N - (k % 2) * D] for k in range(GK)]]
        w1 = part(big, 0, [128, NE, C, D])
        w2 = part(big, 4096, [128, NE, C, D])
        w1T = part(big, 0, [128, C, NHID * 128])
        w2T = part(big, 2048, [128, NHID, D])
        W0, Wg, wo0 = part(big, 6656, [128, C, D]), part(big, 7168, [128, C, 384]), part(big, 7936, [128, D])

        def bank(i, p, n, at=0):
            return pb[0:p, i, at:at + n]

        class Signal:

            def __init__(self, name, free=0, unit=1, sem=None, after=0):
                self.s = ctx.enter_context(nc.semaphore(name)) if sem is None else sem
                self.credit, self.unit, self.after = free * unit, unit, after

            def done(self, k):
                return self.s, (k + self.after) * self.unit + self.credit

            def free(self, k):
                return self.s, (k + self.after + 1) * self.unit

            def next(self, n):
                return Signal(None, self.credit // self.unit, self.unit, self.s, self.after + n)

        def in_turn(name, *counts):
            s, after, made = ctx.enter_context(nc.semaphore(name)), 0, []
            for n in counts:
                made.append(Signal(None, sem=s, after=after))
                after += n
            return made

        s_in = Signal("s_in", unit=16)
        s_x = Signal("s_x", unit=16)
        s_w = Signal("s_w", unit=16)
        s_w12 = Signal("s_w12", unit=16)
        l_raw = Signal("l_loaded", unit=16)
        l_row = Signal("l_rows_loaded", unit=16)
        f_w = Signal("f_loaded", unit=16)
        phase = ctx.enter_context(nc.semaphore("phase_ended"))
        ENDS = (4, 3, 3, 3, 4, 3, 3, 3, 3, 4)

        def ended(i):
            return phase, sum(ENDS[:i + 1])

        s_const, a_rr, f_one = in_turn("pool_once", 6, 2, 1)
        (s_tT, s_vT, w_T, w_P, o_mT, o_pe0, l_T, o_pe1, f_T, f_P, g_T, g_tok, g_qkv, g_sc, g_aT, g_M) = in_turn(
            "pe_once", 3, 1, 1, 1, 1, 3, 2 * NHID, 3 * C, 1, 1, 1, 1, 1, 1, 1, 1)
        o_pe = (o_pe0, o_pe1)
        w_Tc, w_Pc, o_mTc, o_gTc0, o_gTc1, f_Tc, g_Tc, g_qkvc, g_vw, g_ex = in_turn(
            "act_once", 4, 1, 1, 1, C, 2, 3, 2, 2, 1)
        o_gTc = (o_gTc0, o_gTc1)
        (s_rel, s_tab, s_vTc, w_blk, w_b, c_max0, o_mem, o_v0, l_b, c_max1, o_v1, f_blk, f_ready, g_s, g_tokc,
         g_kc, g_mx, g_at, g_aTc, g_Mc) = in_turn(
            "dve_once", 2, 3, 3, 3, 1, 1, 1, 3, NHID, 1, 3 * C, 1, 1, 4, 4, 1, 2, 2, 1, 2)
        c_max, o_v = (c_max0, c_max1), (o_v0, o_v1)
        passed = ctx.enter_context(nc.semaphore("dve_passed"))
        dve_steps = ctx.enter_context(nc.semaphore("dve_steps"))
        g_idx, g_oh = Signal("g_staged"), Signal("g_onehot")
        g_agg, g_acc = Signal("g_summed", 2), Signal("g_added", 2)
        g_got = [Signal(f"g_got{b}", unit=16 * GK) for b in range(2)]
        g_idx, g_oh, g_agg, g_acc = ((s, s.next(NG)) for s in (g_idx, g_oh, g_agg, g_acc))
        g_got = (g_got, [g_got[0].next(NG // 2 + 1), g_got[1].next(NG // 2)])
        a_dve = ctx.enter_context(nc.semaphore("a_dve"))
        a_var, a_rstd = Signal("a_variance"), Signal("a_rstd")
        a_xs = Signal("a_normed")
        a_T = Signal("a_transposed")
        a_xT = Signal("a_xT", 2)
        a_sq = Signal("a_squared", 2)
        a_kept = Signal("a_kept", 2)
        a_p = Signal("a_projected")
        a_pr = Signal("a_rows", 2)
        a_st = [Signal(f"a_stored{u}", 1, 16) for u in range(2)]
        k_ys = Signal("k_scaled")
        k_T = Signal("k_transposed")
        k_yT = Signal("k_yT", 2)
        k_L = Signal("k_logits")
        k_k = Signal("k_keys", 2)
        k_sub = Signal("k_shifted", 2)
        k_exp = Signal("k_exp")
        k_dve = ctx.enter_context(nc.semaphore("k_dve"))
        k_q = Signal("k_queries")
        k_KT = Signal("k_kq_transposed")
        k_KQ = Signal("k_kq_out", 2)
        c_es, c_T, c_er, c_G = (Signal("c_exp"), Signal("c_transposed", 1), Signal("c_rows", 1),
                                Signal("c_summed", 1))
        c_es, c_T, c_er, c_G = ((s, s.next(NB)) for s in (c_es, c_T, c_er, c_G))
        c_hh = Signal("c_normed")
        m_hs = Signal("m_staged")
        m_o = Signal("m_out_rows", 1)
        m_bo = Signal("m_biased")
        m_ss = Signal("m_norm")
        m_dve = ctx.enter_context(nc.semaphore("m_dve"))
        m_sq, m_rn = Signal("m_norm_bounded"), Signal("m_norm_inverse")
        m_var, m_rstd = Signal("m_variance"), Signal("m_rstd")
        m_xs = Signal("m_normed")
        m_T = Signal("m_transposed")
        m_xT = Signal("m_xT")
        m_r = Signal("m_router")
        m_mx = Signal("m_router_max")
        m_ex = Signal("m_router_exp")
        m_c = Signal("m_weights")
        m_cT = Signal("m_weights_transposed")
        m_cTc = Signal("m_weights_out")
        m_b = Signal("m_bias")
        m_x = Signal("m_started", 1)
        m_h = Signal("m_hidden")
        m_g = Signal("m_gelu", 2)
        m_y = Signal("m_out", 2)
        m_acc = Signal("m_added", 2)
        t_dve = ctx.enter_context(nc.semaphore("t_dve"))
        t_var, t_rstd = Signal("t_variance"), Signal("t_rstd")
        t_fs = Signal("t_normed")
        t_kept = Signal("t_kept", 1)
        t_hh = Signal("t_normed_twice")
        t_T = Signal("t_transposed", 2)
        t_Tc = Signal("t_transposed_out")
        t_A = Signal("t_messages")
        t_B = Signal("t_logits")
        t_pr = Signal("t_rows")
        t_st = Signal("t_stored", 1, 16)
        t_sub = Signal("t_shifted")
        t_exp = Signal("t_exp")
        t_q = Signal("t_queries")
        t_K = Signal("t_kq_transposed", 1)
        t_KQ = Signal("t_kq_out", 1)
        l_ev = Signal("l_transposed_out", 4)
        e_qs = Signal("e_staged")
        e_o = Signal("e_mixed", 2)
        e_dve = ctx.enter_context(nc.semaphore("e_dve"))
        e_h = Signal("e_sum", 1)
        e_var, e_sd = Signal("e_variance"), Signal("e_deviation")
        e_yh = Signal("e_normed")
        e_T = Signal("e_transposed", 2)
        e_yT = Signal("e_yT", 1)
        e_H = Signal("e_hidden")
        e_g = Signal("e_gelu", 2)
        e_y = Signal("e_out", 1)
        e_x = Signal("e_added", 1)
        e_hx = Signal("e_sum_added")
        f_hs = Signal("f_staged")
        f_o = Signal("f_message_rows", 2)
        f_dve = ctx.enter_context(nc.semaphore("f_dve"))
        f_x = Signal("f_stream", 1)
        f_var, f_rstd = Signal("f_variance"), Signal("f_rstd")
        f_xs = Signal("f_normed")
        f_tT = Signal("f_x_transposed")
        f_xT = Signal("f_xT", 1)
        f_L = Signal("f_logits")
        f_lg = Signal("f_logits_out", 1)
        f_sub = Signal("f_shifted")
        f_exp = Signal("f_exp")
        f_sdve = ctx.enter_context(nc.semaphore("f_sdve"))
        f_sw = Signal("f_slices")
        f_S = Signal("f_slices_transposed")
        f_sT = Signal("f_slices_out", 1)
        f_tok = Signal("f_tokens", 2)
        h_ss = Signal("h_staged")
        h_y = Signal("h_out", 2)
        h_ob = Signal("h_rows", 2)
        h_st = [Signal(f"h_stored{u}", 1, 16) for u in range(2)]

        block = ctx.enter_context(nc.Block())

        def cols(t):
            return bass.ds(t * TK, TK)

        def one(t):
            return bass.ds(t, 1)

        def tile(a, t):
            return a[:, one(t), :].rearrange("p a b -> p (a b)")

        def tiles(eng, step):
            with eng.Fori(0, T // 2) as j:
                for u in range(2):
                    step(j, u)
            step(T // 2, 0)

        def skewed(eng, early, late, peel=0):
            early(0, 0)
            for j in range(peel):
                for u in range(2):
                    early(j + (u + 1) // 2, (u + 1) % 2)
                    late(j, u)
            with eng.Fori(peel, T // 2) as j:
                for u in range(2):
                    early(j + (u + 1) // 2, (u + 1) % 2)
                    late(j, u)
            late(T // 2, 0)

        def woven(eng, step, peel=0):
            step(None, (0, 0))
            for j in range(peel):
                step((j, 0), (j, 1))
                step((j, 1), (j + 1, 0))
            with eng.Fori(peel, T // 2) as j:
                step((j, 0), (j, 1))
                step((j, 1), (j + 1, 0))
            step((T // 2, 0), None)

        def experts(eng, slot):
            def one_tile(now, nxt, prv, adds, first=None, at=()):
                for e in range(NE):
                    slot(e, now, nxt, prv, later(first, at.index(e)) if e in at else None, adds)
            one_tile(None, (0, 0), None, G0)
            g0 = (G0 // 2, G0 % 2)
            one_tile((0, 0), (0, 1), None, G0, g0, GSLOTS[1:])
            with eng.Fori(0, LOOPED) as j:
                g = later((j * 3 + g0[0], g0[1]), 2)
                one_tile((j, 1), (j + 1, 0), (j, 0), j * 6 + (G0 + 2), g, GSLOTS)
                one_tile((j + 1, 0), (j + 1, 1), (j, 1), j * 6 + (G0 + 5), later(g, 3), GSLOTS)
            for t in range(2 * LOOPED + 1, T_G):
                one_tile(*((i // 2, i % 2) for i in (t, t + 1, t - 1)), G0 + 3 * t - 1, later(g0, 3 * t - 1), GSLOTS)
            with eng.Fori(T_G // 2, T // 2 - 1) as j:
                one_tile((j, 1), (j + 1, 0), (j, 0), NG)
                one_tile((j + 1, 0), (j + 1, 1), (j, 1), NG)
            one_tile((T // 2 - 1, 1), (T // 2, 0), (T // 2 - 1, 0), NG)
            one_tile((T // 2, 0), None, (T // 2 - 1, 1), NG)
            one_tile(None, None, (T // 2, 0), NG)

        def raw(i):
            return KQ[:, 2, i * 512:(i + 1) * 512].rearrange("p (c n) -> p c n", c=C)

        def row(v):
            return v.rearrange("(a n) -> a n", a=1)

        def later(g, k):
            return g[0] + (g[1] + k) // 2, (g[1] + k) % 2

        def there(g):
            return not isinstance(g[0], int) or 2 * g[0] + g[1] < NG

        def every(v, p):
            return row(v).partition_broadcast(p).rearrange("p a n -> p (a n)")

        r_g1, r_g2, r_g3, r_x, r_o, r_g2T = (raw(i) for i in range(6))
        r_q = [KQ[:, 3, i * 128:(i + 1) * 128] for i in range(3)]
        r_qT = [KQ[:, 3, 384 + i * 128:512 + i * 128] for i in range(3)]
        r_b = KQ[:, 3, 768:1024]
        r_jk = KQ[:, 3, 1024:1280]
        r_xb0, r_xb = KQ[:, 3, 1280:1280 + C], KQ[:, 3, 1288:1288 + C]
        r_xbb = KQ[:, 3, 1408:1408 + C * TK].rearrange("p (c n) -> p c n", c=C)
        r_b3b = KQ[:, 3, 1664:1664 + C * TK].rearrange("p (c n) -> p c n", c=C)
        r_rt = KQ[0:NE, 3, 2048:2048 + D]
        r_q32 = [KQ[:, 3, 2304 + 32 * i:2336 + 32 * i] for i in range(3)]
        e_i = KQ[0:NG, 0, 0:2 * GK * TK].bitcast(I32).rearrange("g (a k e) -> g a k e", a=2, k=GK)
        e_f = KQ[0:NG, 1, 0:3 * GK * TK].rearrange("g (a k e) -> g a k e", a=3, k=GK)
        mk, mv = small[:, 0:NM], small[:, NM:2 * NM]
        den, msum, nmax = small[:, 8:8 + C], small[:, 10:11], small[:, 12:12 + C]
        mkT, mvT = stg[0:NM, 2304:2432], stg[0:NM, 2432:2560]
        a_s = [part(stg, 256 * u, [TK, D]) for u in range(2)]
        a_xTb = [part(stg, 512 + 256 * u, [128, C, TK]) for u in range(2)]
        a_prb = [part(stg, 1024 + 256 * u, [TK, D]) for u in range(2)]
        a_sqb = part(stg, 1536, [TK, D])
        k_qb = [part(stg, 1024 + 128 * u, [TK, 128]) for u in range(2)]
        k_kb = [part(stg, 1280 + 128 * u, [TK, 128]) for u in range(2)]
        c_esb, c_erb, c_hhb = part(stg, 0, [128, BT * TK]), part(stg, 640, [TK, BT, 128]), part(big, 6656, [TK, BT, D])
        o_gb, o_gTb = part(stg, 1280, [128, D]), part(stg, 1536, [128, C, 128])
        o_kvb, o_mkb = part(stg, 1792, [128, 128]), part(stg, 1920, [128, NM])
        m_sb = [part(stg, 256 * u, [TK, D]) for u in range(2)]
        m_xTb = [part(stg, 512 + 256 * u, [128, C, TK]) for u in range(2)]
        m_gb = [part(stg, 1024 + 256 * u, [128, C, TK]) for u in range(2)]
        m_qsb, m_hsb = part(stg, 1536, [128, TK]), part(stg, 1664, [128, C, TK])
        m_ob, m_gnb = part(stg, 1920, [TK, D]), part(stg, 2176, [TK, D])
        t_prb, t_qkb = tq[:, 0:D], tq[:, D:3 * D]
        t_fsb, t_hhb = fsx[0:TK, 0], fsx[0:TK, 1]
        t_fT = fsx[:, 2, 0:C * TK].rearrange("p (c n) -> p c n", c=C)
        t_hT = fsx[:, 3, 0:C * TK].rearrange("p (c n) -> p c n", c=C)
        l_rawb, l_bb, l_jk = part(stg, 0, [128, NHID * D]), part(stg, 2048, [128, D]), part(stg, 2304, [128, D])
        bm = small[:, 16:16 + NHID]
        e_qsb = [part(stg, 256 * u, [128, C, TK]) for u in range(2)]
        e_hb = [part(stg, 512 + 256 * u, [TK, D]) for u in range(2)]
        e_yb = [part(stg, 1024 + 256 * u, [TK, D]) for u in range(2)]
        e_yTb = [part(stg, 1536 + 256 * u, [128, C, TK]) for u in range(2)]
        e_gb = part(big, 6656, [128, NHID, TK])
        f_wx, f_wfx = part(big, 0, [128, C, INNER]), part(big, 1024, [128, C, INNER])
        f_wout, f_raw = part(big, 2048, [128, 4, D]), part(big, 3072, [128, 4, 64])
        f_blkb, f_wxs = part(big, 3328, [128, 4, 128]), part(big, 3840, [128, C, INNER])
        f_wxT, f_bfx = part(big, 4864, [128, 4, D]), part(big, 5888, [1, INNER])
        f_temp, f_bsl = part(big, 6400, [128, HS]), part(big, 6408, [TK, 64])
        f_bxs, f_bxb = part(big, 6472, [TK, INNER]), part(big, 6984, [128, 4, TK])
        f_xsb = [part(stg, 257 * u, [TK, PITCH]) for u in range(2)]
        f_xTb = part(stg, 514, [128, C, TK])
        f_hsb = [part(stg, 770 + 256 * u, [128, C, TK]) for u in range(2)]
        f_lgb = [part(stg, 1538 + 512 * u, [TK, INNER]) for u in range(2)]
        HTf = HT[:, :, :].rearrange("p c n -> p (c n)")
        s_s, s_sT = part(HTf, 0, [128, 4, PITCH]), part(HTf, 1028, [128, 4, C, 128])
        s_tc, s_tb = part(HTf, 2052, [128, 4, 64]), part(HTf, 2308, [128, 4, 128])
        s_q, s_k = part(HTf, 2820, [128, 4, 128]), part(HTf, 3332, [128, 4, 64])
        s_v, s_at = part(HTf, 3588, [128, 4, 128]), part(HTf, 4100, [128, 4, 128])
        s_aT, s_vw = part(HTf, 4612, [128, 4, 128]), part(HTf, 5124, [128, 4, D])
        s_nr, s_ec = part(big, 7484, [1, INNER]), part(big, 6984, [128, 4, 64])
        M2 = fsx
        h_obb = [part(stg, 514 + 256 * u, [TK, D]) for u in range(2)]
        h_ssb = [part(stg, 1026 + 512 * u, [128, 4, TK]) for u in range(2)]

        @block.sync
        def _(sp):
            for s in (*a_st, t_st, *h_st):
                sp.sem_inc(s.s, s.credit)

            def load(o, i, s):
                sp.dma_start(o, i).then_inc(s.s, 16)

            load(e_i[:, 0], src.rearrange("(g k e) -> g k e", k=GK, e=TK), s_in)
            load(e_i[:, 1], dst.rearrange("(g k e) -> g k e", k=GK, e=TK), s_in)
            load(e_f[:, 2], edge_weight.rearrange("(g k e) -> g k e", k=GK, e=TK), s_in)
            sp.dma_start(base[:, :], dst.rearrange("(a g q) -> a g q", a=1, g=NG)[:, :, 0],
                         allow_slow_non_contiguous=True).then_inc(s_in.s, 16)
            xr = x.rearrange("(b t p) d -> b p t d", b=NB, p=TK)
            for b in range(NB):
                load(X[:, b * BT:(b + 1) * BT, :], xr[b], s_x)
            load(W0, W0g.rearrange("(c p) n -> p c n", p=128), s_in)
            load(Wg, wqkv.rearrange("(c p) n -> p c n", p=128), s_in)
            load(wo0, wout0, s_in)
            load(mk, mem_kv[0].rearrange("h d m -> (h d) m"), s_in)
            load(mv, mem_kv[1].rearrange("h d m -> (h d) m"), s_in)
            for i, v in enumerate((b0g, bout0, gout0)):
                load(rows[:, i, :], every(v, TK), s_in)
            load(b2row[:, :], be2, s_in)
            load(r_rt, router, s_in)
            for v, a in VECS:
                f = v if len(v.shape) == 1 else v.rearrange("a n -> (a n)")
                load(vecs[a:a + f.shape[0] // 128, :], f.rearrange("(k p) -> k p", p=128), s_in)
            for o, i in ((r_g1, g1w1), (r_g2, g1w2), (r_g3, g1w3), (r_x, Wx), (r_o, Wo)):
                load(o, i.rearrange("(c p) n -> p c n", p=128), s_w)
            for o, i in zip(r_q32, (Wq, Wk, Wv)):
                for a in range(4):
                    load(o[32 * a:32 * a + 32, :], i, s_w)
            load(r_b, every(ln1b, 128), s_w)
            load(w1, we1.rearrange("e (c p) n -> p e c n", p=128), s_w12)

            def store_a(j, u):
                sp.wait_ge(*a_pr.done(2 * j + u + 1))
                sp.dma_start(table[0][cols(2 * j + u), :], a_prb[u]).then_inc(a_st[u].s, 16)
            tiles(sp, store_a)

            sp.wait_ge(*ended(3))
            load(w2, we2.rearrange("e (c p) n -> p e c n", p=128), s_w12)

            def store_t(j, u):
                sp.wait_ge(*t_pr.done(2 * j + u + 1))
                sp.dma_start(table[1][cols(2 * j + u), :], t_prb).then_inc(t_st.s, 16)
            tiles(sp, store_t)

            sp.wait_ge(*ended(4))
            load(l_rawb.rearrange("p (c n) -> p c n", c=NHID), Wm1.rearrange("(c p) n -> p c n", p=128), l_raw)
            for i, v in enumerate((bo, bm2)):
                load(rows[:, i, :], every(v, TK), l_row)
            load(l_bb, every(ln2b, 128), l_row)
            sp.wait_ge(*l_ev.done(NHID))
            sp.wait_ge(*l_b.done(NHID))
            load(l_rawb.rearrange("p (c n) -> p c n", c=C), Wm2.rearrange("(c p) n -> p c n", p=128), l_raw)

            sp.wait_ge(*ended(8))
            load(f_wx, Wsx.rearrange("(c p) n -> p c n", p=128), f_w)
            load(f_wfx, Wfx.rearrange("(c p) n -> p c n", p=128), f_w)
            load(f_wout, Wout.rearrange("(c p) n -> p c n", p=128), f_w)
            for i, v in enumerate((Wsl, Wsq, Wsk, Wsv)):
                for a in range(2):
                    load(f_raw[64 * a:64 * a + 64, i, :], v, f_w)
            load(f_bfx, row(bfx), f_w)
            load(f_temp, every(temp.rearrange("a h b c -> (a h b c)"), 128), f_w)
            load(rows[:, 0, :], every(bout, TK), f_w)
            load(f_bsl, every(bsl, TK), f_w)

            def store_h(j, u):
                sp.wait_ge(*h_ob.done(2 * j + u + 1))
                sp.dma_start(out[cols(2 * j + u), :], h_obb[u]).then_inc(h_st[u].s, 16)
            tiles(sp, store_h)
            sp.wait_ge(*h_st[0].done(T // 2 + 1))
            sp.wait_ge(*h_st[1].done(T // 2))

        @block.gpsimd
        def _(pool):
            pool.sem_inc(a_kept.s, a_kept.credit)
            pool.sem_inc(t_kept.s, t_kept.credit)
            nc.gpsimd.iota(iota[:, :], [[1, W]], base=0, channel_multiplier=0,
                           allow_small_or_imprecise_dtypes=True).then_inc(s_const.s, 1)
            nc.gpsimd.memset(neghalf[:, :], -0.5)
            nc.gpsimd.memset(ident[:, :], 0.0).then_inc(s_const.s, 1)
            nc.gpsimd.memset(mask32[:, :], 1.0).then_inc(s_const.s, 1)
            pool.wait_ge(*s_const.done(3))
            nc.gpsimd.affine_select(out=ident[:, :], in_=ident[:, :], compare_op=ALU.not_equal, fill=1.0, base=0,
                                    pattern=[[-1, 128]], channel_multiplier=1).then_inc(s_const.s, 1)
            m = mask32[:, :].rearrange("p (b c) -> p b c", c=32)
            nc.gpsimd.affine_select(out=m, in_=m, compare_op=ALU.is_ge, fill=0.0, base=0,
                                    pattern=[[-32, 4], [0, 32]], channel_multiplier=1).then_inc(s_const.s, 1)
            pool.wait_ge(*s_const.done(5))
            nc.gpsimd.affine_select(out=m, in_=m, compare_op=ALU.is_ge, fill=0.0, base=31,
                                    pattern=[[32, 4], [0, 32]], channel_multiplier=-1).then_inc(s_const.s, 1)

            def rstd(st_, var, out, n):
                pool.wait_ge(*var.done(n + 1))
                nc.gpsimd.tensor_tensor(st_[:, 8:9], st_[:, 7:8], neghalf[:, 0:1], ALU.pow).then_inc(out.s, 1)

            def keep_a(j, u):
                t = 2 * j + u
                rstd(st[:, u], a_var, a_rstd, t)
                pool.wait_ge(*s_const.done(6))
                pool.wait_ge(*a_xs.done(t + 1))
                nc.gpsimd.tensor_copy(tile(XN, t), a_s[u])
                nc.gpsimd.tensor_tensor(tile(X, t), tile(X, t), a_s[u], ALU.add).then_inc(a_kept.s, 1)
            tiles(pool, keep_a)
            pool.drain().then_inc(phase, 1)
            pool.wait_ge(*ended(0))
            nc.gpsimd.tensor_scalar(rr[:, :], rr[:, :], 1e-24, None, ALU.max).then_inc(a_rr.s, 1)
            pool.wait_ge(*a_rr.done(1))
            nc.gpsimd.tensor_tensor(rr[:, :], rr[:, :], neghalf[:, :], ALU.pow).then_inc(a_rr.s, 1)

            def fill(layer, g, ring):
                h, b = g
                g = 2 * h + b
                pool.wait_ge(*g_agg[layer].free(g))
                nc.gpsimd.tensor_copy(idx[:, b, :], src_i[:, bass.ds(g * GK, GK)]).then_inc(g_idx[layer].s, 1)
                pool.wait_ge(*s_tab.done(3))
                pool.wait_ge(*g_idx[layer].done(g + 1))
                for k in range(GK):
                    nc.gpsimd.indirect_dma_start(
                        out=ring[b][k], out_offset=None, in_=table[layer],
                        in_offset=bass.IndirectOffsetOnAxis(ap=idx[:, b, k:k + 1], axis=0),
                    ).then_inc(g_got[layer][b].s, 16)

            pool.wait_ge(*s_tab.done(3))
            pool.wait_ge(*a_st[0].done(T // 2 + 1))
            pool.wait_ge(*a_st[1].done(T // 2))
            with pool.Fori(0, G0 // 2) as h:
                for b in range(2):
                    fill(0, (h, b), ring)
            fill(0, (G0 // 2, 0), ring)

            pool.wait_ge(*ended(2))
            fill(0, (G0 // 2, 1), ring2)
            fill(0, (G0 // 2 + 1, 0), ring2)
            pool.wait_ge(*ended(3))

            def stage_m(nxt, adds):
                t = 2 * nxt[0] + nxt[1]
                pool.wait_ge(*m_o.free(t))
                pool.wait_ge(*g_acc[0].done(adds))
                nc.gpsimd.tensor_copy(m_qsb, KQ[:, 1, cols(t)])
                nc.gpsimd.tensor_copy(m_hsb, HT[:, :, cols(t)]).then_inc(m_hs.s, 1)

            def m_slot(e, now, nxt, prv, g, adds):
                if nxt:
                    t, u = 2 * nxt[0] + nxt[1], nxt[1]
                    if e == 0 and now is None:
                        stage_m(nxt, adds)
                    if e == 1:
                        pool.wait_ge(*m_sq.done(t + 1))
                        nc.gpsimd.tensor_tensor(rt[:, u, 43:44], rt[:, u, 40:41], neghalf[:, 0:1], ALU.pow)\
                            .then_inc(m_rn.s, 1)
                    if e == 2:
                        rstd(st[:, u], m_var, m_rstd, t)
                if prv:
                    t = 2 * prv[0] + prv[1]
                    if e == 0:
                        rstd(st2[:, 0], t_var, t_rstd, 2 * t)
                    if e == 1:
                        rstd(st2[:, 1], t_var, t_rstd, 2 * t + 1)
                    if e == 2:
                        pool.wait_ge(*t_fs.done(t + 1))
                        nc.gpsimd.tensor_copy(tile(XN, t), t_fsb).then_inc(t_kept.s, 1)
                if e == 3 and nxt and not (isinstance(nxt[0], int) and 2 * nxt[0] + nxt[1] == T - 1):
                    stage_m(later(nxt, 1), adds)
                if g and there(later(g, 2)):
                    fill(0, later(g, 2), ring2)
            experts(pool, m_slot)
            pool.drain().then_inc(phase, 1)
            pool.wait_ge(*ended(4))
            pool.wait_ge(*t_st.done(T))
            with pool.Fori(0, NG // 2) as h:
                for b in range(2):
                    fill(1, (h, b), ring)
            fill(1, (NG // 2, 0), ring)

            pool.wait_ge(*ended(8))
            nc.gpsimd.memset(f_xsb[0][:, D:PITCH], 1.0)
            nc.gpsimd.memset(f_xsb[1][:, D:PITCH], 1.0).then_inc(f_one.s, 1)

            def stage_f(j, u):
                t = 2 * j + u
                pool.wait_ge(*f_o.free(t))
                nc.gpsimd.tensor_copy(f_hsb[u], HT[:, :, cols(t)]).then_inc(f_hs.s, 1)
                rstd(st[:, u], f_var, f_rstd, t)
            tiles(pool, stage_f)
            pool.drain().then_inc(phase, 1)
            pool.wait_ge(*ended(9))

            def stage_h(j, u):
                t = 2 * j + u
                pool.wait_ge(*h_y.free(t))
                nc.gpsimd.tensor_copy(h_ssb[u], KQ[:, :, cols(t)])
                nc.gpsimd.tensor_tensor(tile(X, t), tile(X, t), rows[:, 0, :], ALU.add).then_inc(h_ss.s, 1)
            tiles(pool, stage_h)

        @block.tensor
        def _(pe):
            for s in (g_agg[0], c_T[0], c_G[0], m_o, m_y, t_T, t_K, e_o, e_T, e_y, f_o, f_tok, h_y):
                pe.sem_inc(s.s, s.credit)

            def mm(o, l, r, start=True, stop=True):
                return pe.matmul(o, l, r, start=start, stop=stop, skip_group_check=True)

            def tr(o, i):
                k = i.shape[0]
                return pe.transpose(o, i, ident[0:k, 0:k])

            def two(o, l, r):
                for c in range(C):
                    ins = mm(o, l[:, c, :], r[:, c, :], c == 0, c == C - 1)
                return ins

            def by_feature(b, s):
                for c in range(C):
                    ins = tr(bank(b, 128, TK, c * TK), s[:, c * 128:(c + 1) * 128])
                return ins

            def group(layer, h, b, ring=ring, at=None):
                g = 2 * h + b
                pe.wait_ge(*g_oh[layer].done(g + 1))
                pe.wait_ge(*(g_acc[layer].free(g) if at is None else g_acc[layer].done(g)))
                pe.wait_ge(*g_got[layer][b].done(h + 1))
                at = 6 + b if at is None else at
                for k in range(GK):
                    for c in range(C):
                        ins = mm(bank(at, 128, W, c * W), ring[b][k][:, c * 128:(c + 1) * 128],
                                 onehot[:, b, k, :], k == 0 and c == 0, k == GK - 1)
                ins.then_inc(g_agg[layer].s, 1)

            pe.wait_ge(*s_const.done(6))
            pe.wait_ge(*s_rel.done(2))
            for a in range(3):
                for k in range(GK):
                    ins = tr(bank(a, TK, NG, k * NG), e_f[:, a, k, :])
                ins.then_inc(s_tT.s, 1)
            tr(bank(3, 128, NV), vecs[0:NV, :])
            for c in range(C):
                tr(bank(3, 128, NE, 64 + c * NE), r_rt[:, c * 128:(c + 1) * 128])
            tr(bank(3, NM, 128, 256), mv).then_inc(s_vT.s, 1)
            pe.wait_ge(*s_vTc.done(3))
            pe.wait_ge(*s_tab.done(3))

            def a_early(j, u):
                t = 2 * j + u
                pe.wait_ge(*a_xs.done(t + 1))
                pe.wait_ge(*a_xT.free(t))
                by_feature(u, a_s[u]).then_inc(a_T.s, 1)

            def a_late(j, u):
                t = 2 * j + u
                pe.wait_ge(*a_xT.done(t + 1))
                pe.wait_ge(*a_pr.free(t))
                two(bank(2 + u, TK, D), a_xTb[u], W0).then_inc(a_p.s, 1)
            skewed(pe, a_early, a_late)
            pe.drain().then_inc(phase, 1)
            pe.wait_ge(*ended(0))

            pe.wait_ge(*s_w.done(18))
            pe.wait_ge(*w_blk.done(3))
            k = 0
            for r in (r_g1, r_g2, r_o):
                for c in range(C):
                    for a in range(C):
                        tr(bank(k // 4, 128, 128, (k % 4) * 128), r[:, a, c * 128:(c + 1) * 128])
                        k += 1
            for i in range(3):
                ins = tr(bank(3, 128, 128, i * 128), r_q[i])
            ins.then_inc(w_T.s, 1)
            pe.wait_ge(*w_Tc.done(4))
            pe.wait_ge(*w_b.done(1))
            for c in range(C):
                for m in range(C):
                    mm(bank(0, 128, D, c * D), r_g3[:, m, c * 128:(c + 1) * 128], r_g2T[:, m, :], m == 0, m == C - 1)
            two(bank(1, TK, D), r_b3b, r_g2T)
            for i in range(2):
                for c in range(C):
                    for a in range(C):
                        mm(bank(2 + c, 128, 128, i * D + a * 128), r_x[:, a, c * 128:(c + 1) * 128], r_qT[i])
                for a in range(C):
                    mm(bank(4, TK, 128, i * D + a * 128), r_xbb[:, a, :], r_qT[i])
            for c in range(C):
                for a in range(C):
                    mm(bank(5, 128, 128, c * D + a * 128), r_x[:, a, c * 128:(c + 1) * 128], r_qT[2])
            for a in range(C):
                ins = mm(bank(1, 128, 1, D + a), r_qT[2], r_xb[:, a:a + 1])
            ins.then_inc(w_P.s, 1)
            pe.wait_ge(*w_Pc.done(1))

            def k_early(j, u):
                t = 2 * j + u
                pe.wait_ge(*k_ys.done(t + 1))
                pe.wait_ge(*k_yT.free(t))
                by_feature(u, a_s[u]).then_inc(k_T.s, 1)
                pe.wait_ge(*k_yT.done(t + 1))
                pe.wait_ge(*k_sub.free(t))
                pe.wait_ge(*k_k.free(t))
                two(bank(2 + u, TK, 256), a_xTb[u], Wg[:, :, 0:256]).then_inc(k_L.s, 1)

            def k_late(j, u):
                t = 2 * j + u
                pe.wait_ge(*k_k.done(t + 1))
                pe.wait_ge(*k_KQ.free(t))
                tr(bank(4 + u, 128, TK, 0), k_kb[u])
                pe.wait_ge(*k_q.done(t + 1))
                tr(bank(4 + u, 128, TK, TK), k_qb[u]).then_inc(k_KT.s, 1)
                group(0, j, u)
            skewed(pe, k_early, k_late)
            pe.drain().then_inc(phase, 1)
            pe.wait_ge(*ended(1))

            def context(layer, nk, first):
                def step(g, start, h0):
                    for jj in range(nk):
                        n = g * nk + jj
                        pe.wait_ge(*c_es[layer].done(n + 1))
                        pe.wait_ge(*c_er[layer].free(n))
                        for i in range(BT):
                            ins = tr(bank(i // 4, TK, 128, (i % 4) * 128), c_esb[:, i * TK:(i + 1) * TK])
                        ins.then_inc(c_T[layer].s, 1)
                        if jj == 0:
                            for b in range(2):
                                group(layer, h0 + (first % 2 + b) // 2, (first % 2 + b) % 2)
                        pe.wait_ge(*c_er[layer].done(n + 1))
                        if layer == 1:
                            pe.wait_ge(*c_hh.done(g + 1))
                        for i in range(BT):
                            r = tile(XN, g * BT + i) if layer == 0 else c_hhb[:, i, :]
                            ins = mm(bank(4 + jj, 128, D), c_erb[:, i, :], r, start and i == 0, False)
                        ins.then_inc(c_G[layer].s, 1)
                step(0, True, first // 2)
                with pe.Fori(1, NB) as g:
                    step(g, False, g + first // 2)

            def fold(layer, nk, wv, wo):
                for jj in range(nk):
                    pe.wait_ge(*o_v[layer].done(3 * jj + 1))
                    for c in range(C):
                        ins = tr(bank(0, 128, 128, c * 128), o_gb[:, c * 128:(c + 1) * 128])
                    ins.then_inc(o_pe[layer].s, 1)
                    pe.wait_ge(*o_gTc[layer].done(jj + 1))
                    for c in range(C):
                        ins = mm(bank(1, 128, 128), wv(c, jj), o_gTb[:, c, :], c == 0, c == C - 1 and layer == 1)
                    if layer == 0:
                        pe.wait_ge(*o_mTc.done(1))
                        ins = mm(bank(1, 128, 128), mvT, mkT, False, True)
                    ins.then_inc(o_pe[layer].s, 1)
                    pe.wait_ge(*o_v[layer].done(3 * jj + 2))
                    mm(bank(2, 128, D), o_kvb, wo(jj)).then_inc(o_pe[layer].s, 1)

            context(0, 1, T)
            pe.drain().then_inc(phase, 1)
            pe.wait_ge(*ended(2))
            pe.wait_ge(*o_mem.done(1))
            tr(bank(3, NM, 128), o_mkb).then_inc(o_mT.s, 1)
            fold(0, 1, lambda c, jj: Wg[:, c, 256:384], lambda jj: wo0)
            pe.drain().then_inc(phase, 1)
            pe.wait_ge(*ended(3))

            def m_up(t, u, e):
                pe.wait_ge(*m_g.free(NE * t + e))
                for a in range(C):
                    for c in range(C):
                        ins = mm(bank(e % 2, 128, TK, a * TK), w1[:, e, c, a * 128:(a + 1) * 128],
                                 m_xTb[u][:, c, :], c == 0, c == C - 1)
                ins.then_inc(m_h.s, 1)

            def m_slot(e, now, nxt, prv, g, adds):
                if nxt:
                    t, u = 2 * nxt[0] + nxt[1], nxt[1]
                    if e == 0:
                        pe.wait_ge(*m_hs.done(t + 1))
                        pe.wait_ge(*m_x.free(t))
                        mm(bank(4, TK, D), m_qsb, M[:, 0, :])
                        for c in range(C):
                            ins = tr(bank(4, TK, 128, D + c * 128), m_hsb[:, c, :])
                        ins.then_inc(m_o.s, 1)
                    if e == 4:
                        pe.wait_ge(*m_xs.done(t + 1))
                        by_feature(4, m_sb[u]).then_inc(m_T.s, 1)
                    if e == 5:
                        pe.wait_ge(*m_xT.done(t + 1))
                        two(bank(4, TK, NE), m_xTb[u], rT).then_inc(m_r.s, 1)
                    if e == 7:
                        pe.wait_ge(*m_c.done(t + 1))
                        tr(bank(4, NE, TK), rt[:, u, 0:NE]).then_inc(m_cT.s, 1)
                if prv:
                    t = 2 * prv[0] + prv[1]
                    if e == 2:
                        pe.wait_ge(*t_fs.done(t + 1))
                        pe.wait_ge(*t_KQ.free(t))
                        by_feature(6, t_fsb).then_inc(t_T.s, 1)
                    if e == 3:
                        pe.wait_ge(*t_hh.done(t + 1))
                        by_feature(7, t_hhb).then_inc(t_T.s, 1)
                        pe.wait_ge(*t_Tc.done(2 * t + 1))
                        two(bank(6, TK, 2 * D), t_fT, WA).then_inc(t_A.s, 1)
                    if e == 4:
                        pe.wait_ge(*t_Tc.done(2 * t + 2))
                        two(bank(7, TK, 2 * D), t_hT, WB).then_inc(t_B.s, 1)
                    if e == 7:
                        pe.wait_ge(*t_q.done(t + 1))
                        for i in range(4):
                            a = (i + 2) % 4
                            ins = tr(bank(6, 128, TK, i * TK), t_qkb[:, a * 128:(a + 1) * 128])
                        ins.then_inc(t_K.s, 1)
                if g:
                    group(0, *g, ring2, at=5)
                if now and e + 1 < NE:
                    m_up(2 * now[0] + now[1], now[1], e + 1)
                if nxt and e + 1 == NE:
                    m_up(2 * nxt[0] + nxt[1], nxt[1], 0)
                if now:
                    n = NE * (2 * now[0] + now[1]) + e
                    pe.wait_ge(*m_g.done(n + 1))
                    pe.wait_ge(*m_acc.free(n))
                    two(bank(2 + e % 2, TK, D), m_gb[e % 2], w2[:, e]).then_inc(m_y.s, 1)
                if nxt and e == 7:
                    pe.wait_ge(*m_cTc.done(2 * nxt[0] + nxt[1] + 1))
                    mm(bank(4, TK, D), cT[:, :], b2row[:, :]).then_inc(m_b.s, 1)
            pe.wait_ge(*s_w12.done(2))
            experts(pe, m_slot)
            pe.drain().then_inc(phase, 1)
            pe.wait_ge(*ended(4))

            for i in range(2):
                pe.wait_ge(*l_raw.done(i + 1))
                for k in range(NHID):
                    pe.wait_ge(*l_ev.free(i * NHID + k))
                    for c in range(C):
                        a = k * D + c * 128 if i == 0 else c * NHID * 128 + k * 128
                        ins = tr(bank(k % 4, 128, 128, c * 128), l_rawb[:, a:a + 128])
                    ins.then_inc(l_T.s, 1)
            pe.drain().then_inc(phase, 1)
            pe.wait_ge(*ended(5))
            context(1, C, 0)
            pe.drain().then_inc(phase, 1)
            pe.wait_ge(*ended(6))
            fold(1, C, lambda c, jj: WV[:, c, jj * 128:(jj + 1) * 128], lambda jj: WoT[:, jj, :])
            pe.drain().then_inc(phase, 1)
            pe.wait_ge(*ended(7))

            def e_up(t, u, pairs):
                for a in range(2 * pairs[0], 2 * pairs[-1] + 2):
                    if a % 2 == 0:
                        pe.wait_ge(*e_g.free(4 * t + a // 2))
                    for c in range(C):
                        ins = mm(bank(2 + (a // 2) % 2, 128, TK, (a % 2) * TK), w1T[:, c, a * 128:(a + 1) * 128],
                                 e_yTb[u][:, c, :], c == 0, c == C - 1)
                    if a % 2:
                        ins.then_inc(e_H.s, 1)

            def e_step(now, nxt):
                if now:
                    j, u = now
                    t = 2 * j + u
                    gs = [later((NB + 3 * j, 0), 3 * u + i) for i in range(3)]
                    pe.wait_ge(*e_yT.done(t + 1))
                    e_up(t, u, (0, 1))
                if nxt:
                    n, w = 2 * nxt[0] + nxt[1], nxt[1]
                    pe.wait_ge(*e_qs.done(n + 1))
                    pe.wait_ge(*e_h.free(n))
                    two(bank(0, TK, D), e_qsb[w], M).then_inc(e_o.s, 1)
                if now:
                    group(1, *gs[0])
                    e_up(t, u, (2, 3))
                    group(1, *gs[1])
                if nxt:
                    pe.wait_ge(*e_yh.done(n + 1))
                    pe.wait_ge(*e_yT.free(n))
                    by_feature(1, e_yb[w]).then_inc(e_T.s, 1)
                if now:
                    pe.wait_ge(*e_g.done(4 * t + 4))
                    pe.wait_ge(*e_x.free(t))
                    for a in range(NHID):
                        ins = mm(bank(4, TK, D), e_gb[:, a, :], w2T[:, a, :], a == 0, a == NHID - 1)
                    ins.then_inc(e_y.s, 1)
                    group(1, *gs[2])
            woven(pe, e_step)
            pe.drain().then_inc(phase, 1)
            pe.wait_ge(*ended(8))

            pe.wait_ge(*f_w.done(15))
            for a in range(4):
                for c in range(C):
                    ins = tr(bank(a // 2, 128, 128, (a % 2) * 256 + c * 128), f_wx[:, c, a * 128:(a + 1) * 128])
            ins.then_inc(f_T.s, 1)
            pe.wait_ge(*f_blk.done(1))
            pe.wait_ge(*f_Tc.done(2))
            for a in range(4):
                for c in range(C):
                    mm(bank(3 + c, 128, 128, a * 128), f_wxT[:, a, c * 128:(c + 1) * 128], f_blkb[:, 0, :])
                ins = mm(bank(5, TK, 128, a * 128), f_bxb[:, a, :], f_blkb[:, 0, :])
            ins.then_inc(f_P.s, 1)
            pe.wait_ge(*f_ready.done(1))

            def f_early(j, u):
                t = 2 * j + u
                pe.wait_ge(*f_hs.done(t + 1))
                pe.wait_ge(*f_x.free(t))
                for c in range(C):
                    ins = tr(bank(0, TK, 128, c * 128), f_hsb[u][:, c, :])
                ins.then_inc(f_o.s, 1)
                pe.wait_ge(*f_xs.done(t + 1))
                pe.wait_ge(*f_xT.free(t))
                by_feature(1, f_xsb[u]).then_inc(f_tT.s, 1)
                pe.wait_ge(*f_xT.done(t + 1))
                pe.wait_ge(*f_lg.free(t))
                two(bank(2, TK, INNER), f_xTb, f_wxs).then_inc(f_L.s, 1)

            def f_late(j, u):
                t = 2 * j + u
                pe.wait_ge(*f_sw.done(t + 1))
                pe.wait_ge(*f_sT.free(t))
                for a in range(4):
                    ins = tr(bank(3, 128, TK, a * TK), f_lgb[u][:, a * 128:(a + 1) * 128])
                ins.then_inc(f_S.s, 1)
                start = isinstance(j, int) and j == 0 and u == 0
                for a in range(4):
                    ins = mm(bank(4 + a, 128, PITCH), f_lgb[u][:, a * 128:(a + 1) * 128], f_xsb[u], start, False)
                ins.then_inc(f_tok.s, 1)
            skewed(pe, f_early, f_late, peel=1)
            pe.drain().then_inc(phase, 1)
            pe.wait_ge(*ended(9))

            pe.wait_ge(*g_s.done(4))
            for a in range(4):
                for c in range(C):
                    tr(bank(a // 2, 128, 128, (a % 2) * 256 + c * 128), s_s[:, a, c * 128:(c + 1) * 128])
                ins = tr(bank(2, 1, 128, a * 128), s_s[:, a, D:PITCH])
            ins.then_inc(g_T.s, 1)
            pe.wait_ge(*g_Tc.done(3))
            for a in range(4):
                o = bank(3, 128, 128, a * 128)
                for c in range(C):
                    mm(o, f_wfx[:, c, a * 128:(a + 1) * 128], s_sT[:, a, c, :], c == 0, False)
                ins = mm(o, f_bfx[:, a * 128:(a + 1) * 128], s_nr[:, a * 128:(a + 1) * 128], False, True)
            ins.then_inc(g_tok.s, 1)
            pe.wait_ge(*g_tokc.done(4))
            for a in range(4):
                mm(bank(4, 128, 128, a * 128), f_blkb[:, 1, :], s_tb[:, a, :])
                mm(bank(5, 128, 64, a * 64), f_blkb[:, 2, :], s_tc[:, a, :])
                ins = mm(bank(6, 128, 128, a * 128), f_blkb[:, 3, :], s_tb[:, a, :])
            ins.then_inc(g_qkv.s, 1)
            pe.wait_ge(*g_qkvc.done(2))
            pe.wait_ge(*g_kc.done(1))
            for a in range(4):
                mm(bank(7, 128, 64, a * 64), s_q[:, a, :], s_k[:, a, :])
                ins = mm(bank(a // 2, 128, D, (a % 2) * D), s_v[:, a, :], f_wout[:, a, :])
            ins.then_inc(g_sc.s, 1)
            pe.wait_ge(*g_at.done(2))
            for a in range(4):
                ins = tr(bank(2, 128, 128, a * 128), s_at[:, a, :])
            ins.then_inc(g_aT.s, 1)
            pe.wait_ge(*g_aTc.done(1))
            pe.wait_ge(*g_vw.done(2))
            for a in range(4):
                ins = mm(bank(3 + a // 2, 128, D, (a % 2) * D), s_aT[:, a, :], s_vw[:, a, :])
            ins.then_inc(g_M.s, 1)
            pe.wait_ge(*g_Mc.done(2))

            def h_tile(j, u):
                t = 2 * j + u
                pe.wait_ge(*h_ss.done(t + 1))
                pe.wait_ge(*h_ob.free(t))
                for a in range(4):
                    ins = mm(bank(5 + u, TK, D), h_ssb[u][:, a, :], M2[:, a, :], a == 0, a == 3)
                ins.then_inc(h_y.s, 1)
            tiles(pe, h_tile)

        @block.scalar
        def _(act):
            for s in (a_xT, a_sq, a_pr, k_yT, k_k, k_KQ, m_g, t_KQ, l_ev, e_yT, e_g, f_xT, f_sT):
                act.sem_inc(s.s, s.credit)

            def copy(o, i):
                return nc.scalar.activation(o, i, ACT.Copy)

            def blocks(b, p, n):
                return bank(b, p, C * n).rearrange("p (c n) -> p c n", c=C)

            def a_early(j, u):
                t = 2 * j + u
                act.wait_ge(*a_T.done(t + 1))
                copy(a_xTb[u], blocks(u, 128, TK)).then_inc(a_xT.s, 1)
                act.wait_ge(*a_sq.done(t))
                nc.scalar.activation(a_sqb, a_s[u], ACT.Square, accum_out=rr[:, one(t)]).then_inc(a_sq.s, 1)

            def a_late(j, u):
                t = 2 * j + u
                act.wait_ge(*a_p.done(t + 1))
                act.wait_ge(*a_st[u].free(j))
                copy(a_prb[u], bank(2 + u, TK, D)).then_inc(a_pr.s, 1)
            skewed(act, a_early, a_late)
            act.drain().then_inc(phase, 1)
            act.wait_ge(*ended(0))

            act.wait_ge(*w_T.done(1))
            for o, b in ((WA[:, :, 0:D], 0), (r_g2T, 1), (WoT[:, :, :], 2)):
                copy(o, blocks(b, 128, D)).then_inc(w_Tc.s, 1)
            for i in range(3):
                ins = copy(r_qT[i], bank(3, 128, 128, i * 128))
            ins.then_inc(w_Tc.s, 1)
            act.wait_ge(*w_P.done(1))
            copy(WA[:, :, D:2 * D], blocks(0, 128, D))
            copy(rows[:, 3, :], bank(1, TK, D))
            copy(bvc[:, :], bank(1, 128, C, D))
            copy(bqk[:, :], bank(4, TK, 2 * D))
            for c in range(C):
                g = vT[:, V_LN1W + c:V_LN1W + c + 1]
                nc.scalar.activation(WB[:, c, :], bank(2 + c, 128, 2 * D), ACT.Copy, scale=g)
                ins = nc.scalar.activation(WV[:, c, :], bank(5, 128, D, c * D), ACT.Copy, scale=g)
            ins.then_inc(w_Pc.s, 1)

            act.wait_ge(*a_rr.done(2))
            act.wait_ge(*a_st[0].done(T // 2 + 1))
            act.wait_ge(*a_st[1].done(T // 2))

            def k_early(j, u):
                t = 2 * j + u
                act.wait_ge(*k_yT.free(t))
                nc.scalar.activation(a_s[u], tile(XN, t), ACT.Copy, scale=rr[:, one(t)]).then_inc(k_ys.s, 1)
                act.wait_ge(*k_T.done(t + 1))
                copy(a_xTb[u], blocks(u, 128, TK)).then_inc(k_yT.s, 1)

            def k_late(j, u):
                t = 2 * j + u
                act.wait_ge(*k_L.done(t + 1))
                act.wait_ge(*k_sub.done(t + 1))
                copy(k_kb[u], bank(2 + u, TK, 128, 128)).then_inc(k_k.s, 1)
                nc.scalar.activation(k_qb[u], k_qb[u], ACT.Exp).then_inc(k_exp.s, 1)
                act.wait_ge(*k_KT.done(t + 1))
                copy(KQ[:, 0:2, cols(t)], blocks(4 + u, 128, TK)).then_inc(k_KQ.s, 1)
            skewed(act, k_early, k_late)
            act.drain().then_inc(phase, 1)
            act.wait_ge(*ended(1))

            def context(layer, nk):
                act.wait_ge(*c_max[layer].done(1))

                def step(g):
                    for jj in range(nk):
                        act.wait_ge(*c_T[layer].free(g * nk + jj))
                        nc.scalar.activation(c_esb, KQ[:, jj, bass.ds(g * BT * TK, BT * TK)], ACT.Exp,
                                             bias=nmax[:, jj:jj + 1], accum_out=ksum[:, jj, one(g)])\
                            .then_inc(c_es[layer].s, 1)
                with act.Fori(0, NB) as g:
                    step(g)

            context(0, 1)
            nc.scalar.activation(mk, mk, ACT.Exp, bias=nmax[:, 0:1], accum_out=msum)
            act.drain().then_inc(phase, 1)
            act.wait_ge(*ended(2))

            def fold(layer, nk):
                for jj in range(nk):
                    act.wait_ge(*o_pe[layer].done(3 * jj + 1))
                    copy(o_gTb, blocks(0, 128, 128)).then_inc(o_gTc[layer].s, 1)
            act.wait_ge(*o_mT.done(1))
            copy(mkT, bank(3, NM, 128)).then_inc(o_mTc.s, 1)
            fold(0, 1)
            act.drain().then_inc(phase, 1)
            act.wait_ge(*ended(3))

            def m_slot(e, now, nxt, prv, g, adds):
                if nxt and e == 1:
                    t, u = 2 * nxt[0] + nxt[1], nxt[1]
                    act.wait_ge(*m_bo.done(t + 1))
                    nc.scalar.activation(m_sb[u], m_ob, ACT.Square, accum_out=rt[:, u, 40:41]).then_inc(m_ss.s, 1)
                if now:
                    n = NE * (2 * now[0] + now[1]) + e
                    act.wait_ge(*m_h.done(n + 1))
                    act.wait_ge(*m_y.free(n))
                    for a in range(C):
                        b = V_B1 + e * C + a
                        ins = nc.scalar.activation(m_gb[e % 2][:, a, :], bank(e % 2, 128, TK, a * TK), ACT.Gelu,
                                                   bias=vT[:, b:b + 1])
                    ins.then_inc(m_g.s, 1)
                if prv:
                    t = 2 * prv[0] + prv[1]
                    if e == 2:
                        act.wait_ge(*t_T.done(2 * t + 1))
                        copy(t_fT, blocks(6, 128, TK)).then_inc(t_Tc.s, 1)
                    if e == 3:
                        act.wait_ge(*t_T.done(2 * t + 2))
                        copy(t_hT, blocks(7, 128, TK)).then_inc(t_Tc.s, 1)
                    if e == 5:
                        act.wait_ge(*t_sub.done(t + 1))
                        nc.scalar.activation(t_qkb[:, 0:D], t_qkb[:, 0:D], ACT.Exp).then_inc(t_exp.s, 1)
                if nxt:
                    t, u = 2 * nxt[0] + nxt[1], nxt[1]
                    if e == 4:
                        act.wait_ge(*m_T.done(t + 1))
                        copy(m_xTb[u], blocks(4, 128, TK)).then_inc(m_xT.s, 1)
                    if e == 5:
                        act.wait_ge(*m_mx.done(t + 1))
                        nc.scalar.activation(rt[:, u, 8:8 + NE], bank(4, TK, NE), ACT.Exp, bias=rt[:, u, 41:42],
                                             accum_out=rt[:, u, 42:43]).then_inc(m_ex.s, 1)
                    if e == 7:
                        act.wait_ge(*m_cT.done(t + 1))
                        copy(cT[:, :], bank(4, NE, TK)).then_inc(m_cTc.s, 1)
                if prv and e == 7:
                    t = 2 * prv[0] + prv[1]
                    act.wait_ge(*t_K.done(t + 1))
                    copy(KQ[:, :, cols(t)], bank(6, 128, 4 * TK).rearrange("p (c n) -> p c n", c=4))\
                        .then_inc(t_KQ.s, 1)
            experts(act, m_slot)
            act.drain().then_inc(phase, 1)
            act.wait_ge(*ended(4))

            for k in range(NHID):
                act.wait_ge(*l_T.done(k + 1))
                for c in range(C):
                    ins = nc.scalar.activation(w1T[:, c, k * 128:(k + 1) * 128], bank(k % 4, 128, 128, c * 128),
                                               ACT.Copy, scale=vT[:, V_LN2W + c:V_LN2W + c + 1])
                ins.then_inc(l_ev.s, 1)
            for k in range(NHID):
                act.wait_ge(*l_T.done(NHID + k + 1))
                copy(w2T[:, k, :], bank(k % 4, 128, D)).then_inc(l_ev.s, 1)
            act.drain().then_inc(phase, 1)
            act.wait_ge(*ended(5))
            context(1, C)
            act.drain().then_inc(phase, 1)
            act.wait_ge(*ended(6))
            fold(1, C)
            act.drain().then_inc(phase, 1)
            act.wait_ge(*ended(7))

            def stage_e(j, u):
                t = 2 * j + u
                act.wait_ge(*e_o.free(t))
                copy(e_qsb[u], KQ[:, C:2 * C, cols(t)]).then_inc(e_qs.s, 1)

            def e_gelu(t, pairs):
                for a in range(2 * pairs[0], 2 * pairs[-1] + 2):
                    if a % 2 == 0:
                        act.wait_ge(*e_H.done(4 * t + a // 2 + 1))
                    ins = nc.scalar.activation(e_gb[:, a, :], bank(2 + (a // 2) % 2, 128, TK, (a % 2) * TK),
                                               ACT.Gelu, bias=bm[:, a:a + 1])
                    if a % 2:
                        ins.then_inc(e_g.s, 1)

            def e_step(now, nxt):
                if nxt:
                    stage_e(*nxt)
                if now:
                    t = 2 * now[0] + now[1]
                    act.wait_ge(*e_y.free(t))
                    e_gelu(t, (0, 1))
                if nxt:
                    n, w = 2 * nxt[0] + nxt[1], nxt[1]
                    act.wait_ge(*e_var.done(n + 1))
                    nc.scalar.activation(st[:, w, 9:10], st[:, w, 7:8], ACT.Sqrt, bias=eps[:, 0:1]).then_inc(e_sd.s, 1)
                if now:
                    e_gelu(t, (2, 3))
                if nxt:
                    act.wait_ge(*e_T.done(n + 1))
                    copy(e_yTb[w], blocks(1, 128, TK)).then_inc(e_yT.s, 1)
            woven(act, e_step)
            act.drain().then_inc(phase, 1)
            act.wait_ge(*ended(8))
            act.wait_ge(*f_T.done(1))
            for i in range(2):
                copy(f_wxT[:, 2 * i:2 * i + 2, :], blocks(i, 128, D)).then_inc(f_Tc.s, 1)

            def f_early(j, u):
                t = 2 * j + u
                act.wait_ge(*f_tT.done(t + 1))
                copy(f_xTb, blocks(1, 128, TK)).then_inc(f_xT.s, 1)

            def f_late(j, u):
                t = 2 * j + u
                act.wait_ge(*f_sub.done(t + 1))
                nc.scalar.activation(f_lgb[u], f_lgb[u], ACT.Exp).then_inc(f_exp.s, 1)
                act.wait_ge(*f_S.done(t + 1))
                copy(KQ[:, :, cols(t)], bank(3, 128, 4 * TK).rearrange("p (c n) -> p c n", c=4))\
                    .then_inc(f_sT.s, 1)
            skewed(act, f_early, f_late)
            act.drain().then_inc(phase, 1)
            act.wait_ge(*ended(9))

            act.wait_ge(*g_T.done(1))
            for i in range(2):
                copy(s_sT[:, 2 * i:2 * i + 2].rearrange("p a c n -> p (a c n)"), bank(i, 128, 512))\
                    .then_inc(g_Tc.s, 1)
            copy(s_nr, bank(2, 1, INNER)).then_inc(g_Tc.s, 1)
            act.wait_ge(*g_qkv.done(1))
            copy(s_q.rearrange("p a n -> p (a n)"), bank(4, 128, 512)).then_inc(g_qkvc.s, 1)
            copy(s_v.rearrange("p a n -> p (a n)"), bank(6, 128, 512)).then_inc(g_qkvc.s, 1)
            act.wait_ge(*g_sc.done(1))
            for i in range(2):
                copy(s_vw[:, 2 * i:2 * i + 2, :], blocks(i, 128, D)).then_inc(g_vw.s, 1)
            act.wait_ge(*g_mx.done(2))
            for a in range(4):
                ins = nc.scalar.activation(s_ec[:, a, :], bank(7, 128, 64, a * 64), ACT.Exp, scale=64 ** -0.5,
                                           bias=small[:, 36 + a:37 + a], accum_out=small[:, 40 + a:41 + a])
            ins.then_inc(g_ex.s, 1)

        @block.vector
        def _(dve):
            v = nc.vector
            for s in (g_acc[0], c_er[0], k_sub, m_x, m_acc, e_h, e_x, f_x, f_lg, h_ob):
                dve.sem_inc(s.s, s.credit)
            v.memset(HT[:, :, :], 0.0)
            v.memset(rt[:, :, :], -1.0)
            v.memset(eps[:, :], EPS)

            once = Steps(dve, dve_steps, 0, passed)
            once.tile(0)

            def plainly(*waits):
                for s, n in waits:
                    dve.wait_ge(s, n)
                dve.sem_inc(passed, 1)

            def moments(st_, i, done, var):
                done(v.bn_stats(st_[:, 0:6], i), plain=True)
                done(v.bn_aggr(st_[:, 6:8], st_[:, 0:6]))
                v.tensor_scalar(st_[:, 7:8], st_[:, 7:8], EPS, None, ALU.add).then_inc(var.s, 1)

            def scaled(st_, o, i, rstd, n):
                dve.wait_ge(*rstd.done(n + 1))
                return v.tensor_scalar(o, i, st_[:, 6:7], st_[:, 8:9], ALU.subtract, ALU.mult)

            def norm(st_, o, i, done, var, rstd, n):
                moments(st_, i, done, var)
                return scaled(st_, o, i, rstd, n)

            def wide(a, n, w):
                return a.rearrange("p (n b) -> p n b", b=1).to_broadcast([a.shape[0], n, w])

            def heads(a, w):
                return a.rearrange("p (h w) -> p h w", w=w)

            def one_hots(layer, h, b):
                g = 2 * h + b
                dve.wait_ge(*g_agg[layer].free(g))
                for k in range(GK):
                    c = g * GK + k
                    if layer == 0:
                        ins = v.tensor_scalar(onehot[:, b, k, :], iota[:, :], dst_r[:, one(c)], w_e[:, one(c)],
                                              ALU.is_equal, ALU.mult)
                    else:
                        ins = v.tensor_scalar(onehot[:, b, k, :], iota[:, :], dst_r[:, one(c)], None, ALU.is_equal)
                ins.then_inc(g_oh[layer].s, 1)

            def add(layer, h, b, at=None):
                g = 2 * h + b
                r = dve.value_load(base[0:1, one(g)], min_val=0, max_val=N - 1)
                dve.wait_ge(*g_agg[layer].done(g + 1))
                dve.wait_ge(*g_acc[layer].done(g))
                o = HT[:, :, bass.ds(r, W)]
                v.tensor_tensor(o, o, bank(6 + b if at is None else at, 128, C * W).rearrange("p (c n) -> p c n", c=C), ALU.add)\
                    .then_inc(g_acc[layer].s, 1)

            dve.wait_ge(*s_in.done(22))
            v.tensor_copy(e_f[:, 0:2], e_i).then_inc(s_rel.s, 1)
            dve.wait_ge(*s_rel.done(1))
            v.tensor_scalar(e_f[:, 1], e_f[:, 1], e_f[:, 1, 0, 0:1], None, ALU.subtract).then_inc(s_rel.s, 1)
            for a, o in enumerate((src_i, dst_r, w_e)):
                dve.wait_ge(*s_tT.done(a + 1))
                v.tensor_copy(o[:, :].rearrange("e (g k) -> e g k", k=GK),
                              bank(a, TK, NCH).rearrange("e (k g) -> e g k", k=GK)).then_inc(s_tab.s, 1)
            dve.wait_ge(*s_vT.done(1))
            v.tensor_copy(vT[:, 0:NV], bank(3, 128, NV)).then_inc(s_vTc.s, 1)
            v.tensor_copy(rT[:, :, :], bank(3, 128, C * NE, 64).rearrange("p (c n) -> p c n", c=C))\
                .then_inc(s_vTc.s, 1)
            v.tensor_copy(mvT, bank(3, NM, 128, 256)).then_inc(s_vTc.s, 1)
            dve.wait_ge(*s_vTc.done(1))
            for c in range(C):
                v.tensor_scalar(Wg[:, c, :], Wg[:, c, :], vT[:, V_GPRE + c:V_GPRE + c + 1], float(D) ** 0.5,
                                ALU.mult, ALU.mult)
            v.tensor_scalar(rows[:, 2, :], rows[:, 2, :], float(D) ** 0.5, None, ALU.mult)

            sa = Steps(dve, a_dve, 2, passed)

            def a_tile(j, u):
                t = 2 * j + u
                sa.tile(t)
                plainly(a_xT.free(t), a_sq.free(t), a_kept.free(t))
                norm(st[:, u], a_s[u], tile(X, t), sa.done, a_var, a_rstd, t).then_inc(a_xs.s, 1)
                sa.end()
            dve.wait_ge(*s_x.done(NB))
            tiles(dve, a_tile)
            dve.drain().then_inc(phase, 1)
            dve.wait_ge(*ended(0))
            dve.wait_ge(*a_rr.done(2))

            dve.wait_ge(*s_w.done(18))
            for i in range(3):
                v.tensor_tensor(heads(r_q[i], 32), heads(mask32[:, :], 32),
                                r_q32[i].rearrange("p (a n) -> p a n", a=1).to_broadcast([128, 4, 32]), ALU.mult)\
                    .then_inc(w_blk.s, 1)
            for a in range(C):
                ins = v.tensor_tensor_reduce(r_jk, r_x[:, a, :], r_b, 1.0, 0.0, ALU.mult, ALU.add,
                                             r_xb0[:, a:a + 1])
                once.done(ins)
            once.done(v.tensor_tensor(r_xb, r_xb0, vT[:, V_BX:V_BX + C], ALU.add))
            v.tensor_copy(r_xbb, wide(r_xb, C, TK))
            v.tensor_copy(r_b3b, wide(vT[:, V_B3:V_B3 + C], C, TK)).then_inc(w_b.s, 1)

            sk = Steps(dve, k_dve, 3, passed)
            one_hots(0, 0, 0)
            dve.wait_ge(*a_st[0].done(T // 2 + 1))
            dve.wait_ge(*a_st[1].done(T // 2))

            def k_tile(j, u):
                t = 2 * j + u
                sk.tile(t)
                dve.wait_ge(*k_L.done(t + 1))
                L = heads(bank(2 + u, TK, 128), 32)
                q = heads(k_qb[u], 32)
                sk.done(v.tensor_reduce(qst[:, u, 0:4], L, AX, ALU.max))
                dve.wait_ge(*k_KQ.free(t))
                v.tensor_tensor(q, L, wide(qst[:, u, 0:4], 4, 32), ALU.subtract).then_inc(k_sub.s, 1)
                one_hots(0, j + (u + 1) // 2, (u + 1) % 2)
                dve.wait_ge(*k_exp.done(t + 1))
                sk.done(v.tensor_reduce(qst[:, u, 4:8], q, AX, ALU.add))
                sk.done(v.reciprocal(qst[:, u, 8:12], qst[:, u, 4:8]))
                v.tensor_tensor(q, q, wide(qst[:, u, 8:12], 4, 32), ALU.mult).then_inc(k_q.s, 1)
                add(0, j, u)
                sk.end()
            tiles(dve, k_tile)
            dve.drain().then_inc(phase, 1)
            dve.wait_ge(*ended(1))

            def context(layer, nk, first):
                for jj in range(nk):
                    once.done(v.tensor_reduce(kmax[:, jj:jj + 1], KQ[:, jj, :], AX, ALU.max))
                if layer == 0:
                    once.done(v.tensor_reduce(small[:, 11:12], mk, AX, ALU.max))
                    once.done(v.tensor_tensor(kmax[:, 0:1], kmax[:, 0:1], small[:, 11:12], ALU.max))
                v.tensor_scalar(nmax[:, 0:nk], kmax[:, 0:nk], -1.0, None, ALU.mult).then_inc(c_max[layer].s, 1)

                def step(g, h0, last=False):
                    if layer == 1:
                        dve.wait_ge(*c_G[layer].free(g * nk))
                        for i in range(BT):
                            n = g * BT + i
                            ins = v.tensor_scalar(c_hhb[:, i, :], tile(XN, n), tile(MV, n)[:, 0:1], tile(MV, n)[:, 1:2],
                                                  ALU.subtract, ALU.mult)
                        ins.then_inc(c_hh.s, 1)
                    for jj in range(nk):
                        n = g * nk + jj
                        dve.wait_ge(*c_T[layer].done(n + 1))
                        dve.wait_ge(*c_G[layer].free(n))
                        for b, a, k in ((0, 0, 4), (1, 4, 1)):
                            i = bank(b, TK, k * 128).rearrange("p (a n) -> p a n", n=128)
                            if layer == 0:
                                ins = v.tensor_tensor(c_erb[:, a:a + k, :], i,
                                                      wide(rr[:, bass.ds(g * BT + a, k)], k, 128), ALU.mult)
                            else:
                                ins = v.tensor_copy(c_erb[:, a:a + k, :], i)
                        ins.then_inc(c_er[layer].s, 1)
                        if jj == 0:
                            for b in range(2):
                                q = first % 2 + b
                                one_hots(layer, h0 + (q + 1) // 2, (q + 1) % 2)
                                add(layer, h0 + q // 2, q % 2)
                with dve.Fori(0, NB) as g:
                    step(g, g + first // 2)

            context(0, 1, T)
            dve.drain().then_inc(phase, 1)
            dve.wait_ge(*ended(2))

            def fold(layer, nk, scale):
                for jj in range(nk):
                    once.done(v.tensor_reduce(den[:, jj:jj + 1], ksum[:, jj, :], AX, ALU.add))
                    if layer == 0:
                        once.done(v.tensor_tensor(den[:, 0:1], den[:, 0:1], msum, ALU.add))
                    once.done(v.reciprocal(small[:, 24 + jj:25 + jj], den[:, jj:jj + 1]))
                if layer == 0:
                    v.tensor_scalar(o_mkb, mk, small[:, 24:25], None, ALU.mult).then_inc(o_mem.s, 1)
                for jj in range(nk):
                    v.tensor_scalar(o_gb, bank(4 + jj, 128, D), small[:, 24 + jj:25 + jj], None, ALU.mult)\
                        .then_inc(o_v[layer].s, 1)
                    dve.wait_ge(*o_pe[layer].done(3 * jj + 2))
                    if layer == 0:
                        ins = v.tensor_tensor(o_kvb, bank(1, 128, 128), mask32[:, :], ALU.mult)
                    else:
                        ins = v.scalar_tensor_tensor(out=o_kvb, in0=bank(1, 128, 128), scalar=bvc[:, jj:jj + 1],
                                                     in1=mask32[:, :], op0=ALU.add, op1=ALU.mult)
                    ins.then_inc(o_v[layer].s, 1)
                    dve.wait_ge(*o_pe[layer].done(3 * jj + 3))
                    v.tensor_scalar(M[:, jj, :], bank(2, 128, D), scale, None, ALU.mult).then_inc(o_v[layer].s, 1)
            fold(0, 1, 32 ** -0.5)
            dve.drain().then_inc(phase, 1)
            dve.wait_ge(*ended(3))

            sm, stl = Steps(dve, m_dve, 15, passed), Steps(dve, t_dve, 8, passed)

            def m_early(e, j, u):
                t = 2 * j + u
                n, r, Xt = sm.done, rt[:, u], tile(X, t)
                if e == 1:
                    dve.wait_ge(*m_ss.done(t + 1))
                    v.tensor_scalar(r[:, 40:41], r[:, 40:41], 1e-24, None, ALU.max).then_inc(m_sq.s, 1)
                if e == 0:
                    sm.tile(t)
                    dve.wait_ge(*m_o.done(t + 1))
                    v.tensor_tensor(m_ob, bank(4, TK, D), rows[:, 1, :], ALU.add).then_inc(m_bo.s, 1)
                    v.tensor_tensor(m_gnb, bank(4, TK, D, D), rows[:, 0, :], ALU.add)
                if e == 2:
                    dve.wait_ge(*m_rn.done(t + 1))
                    n(v.scalar_tensor_tensor(out=m_ob, in0=m_ob, scalar=r[:, 43:44], in1=rows[:, 2, :],
                                             op0=ALU.mult, op1=ALU.mult))
                    n(v.scalar_tensor_tensor(out=m_gnb, in0=m_gnb, scalar=0.0, in1=m_ob, op0=ALU.max, op1=ALU.add))
                    n(v.tensor_tensor(Xt, Xt, m_gnb, ALU.add), plain=True)
                    moments(st[:, u], Xt, n, m_var)
                if e == 3:
                    scaled(st[:, u], m_sb[u], Xt, m_rstd, t).then_inc(m_xs.s, 1)
                    dve.wait_ge(*m_xs.done(t + 1))
                    n(v.tensor_tensor(Xt, Xt, m_sb[u], ALU.add))
                if e == 5:
                    dve.wait_ge(*m_r.done(t + 1))
                    v.tensor_reduce(r[:, 41:42], bank(4, TK, NE), AX, ALU.max, negate=True).then_inc(m_mx.s, 1)
                if e == 6:
                    dve.wait_ge(*m_ex.done(t + 1))
                    n(v.reciprocal(r[:, 44:45], r[:, 42:43]))
                    n(v.tensor_scalar(r[:, 8:8 + NE], r[:, 8:8 + NE], r[:, 44:45], None, ALU.mult), plain=True)
                    n(v.max(r[:, 24:32], r[:, 8:8 + NE]))
                    n(v.tensor_copy(r[:, 32:34], r[:, 24:26]))
                    n(v.tensor_tensor(r[:, 45:46], r[:, 24:25], r[:, 25:26], ALU.add))
                    n(v.tensor_scalar(r[:, 45:46], r[:, 45:46], 1e-12, None, ALU.max), plain=True)
                    n(v.match_replace(out=rt2[:, :], in_to_replace=r[:, 32:40], in_values=r[:, 8:22], imm_value=0.0))
                    n(v.reciprocal(r[:, 46:47], r[:, 45:46]))
                    n(v.tensor_tensor(r[:, 0:NE], r[:, 8:8 + NE], rt2[:, 0:NE], ALU.subtract))
                    v.tensor_scalar(r[:, 0:NE], r[:, 0:NE], r[:, 46:47], None, ALU.mult).then_inc(m_c.s, 1)
                    sm.end()

            def m_tail(e, j, u):
                t = 2 * j + u
                n, Xt = stl.done, tile(X, t)
                if e == 0:
                    stl.tile(t)
                    plainly(m_acc.done(NE * t + NE))
                    moments(st2[:, 0], Xt, n, t_var)
                if e == 1:
                    dve.wait_ge(*t_kept.free(t))
                    dve.wait_ge(*t_T.free(2 * t))
                    scaled(st2[:, 0], t_fsb, Xt, t_rstd, 2 * t).then_inc(t_fs.s, 1)
                    plainly(t_fs.done(t + 1))
                    moments(st2[:, 1], t_fsb, n, t_var)
                if e == 2:
                    dve.wait_ge(*t_T.free(2 * t + 1))
                    scaled(st2[:, 1], t_hhb, t_fsb, t_rstd, 2 * t + 1).then_inc(t_hh.s, 1)
                    v.tensor_copy(tile(MV, t), st2[:, 1, 6:9:2])
                if e == 4:
                    dve.wait_ge(*t_A.done(t + 1))
                    dve.wait_ge(*t_st.free(t))
                    v.tensor_tensor(t_prb, bank(6, TK, D, D), rows[:, 3, :], ALU.add).then_inc(t_pr.s, 1)
                    v.tensor_tensor(Xt, Xt, bank(6, TK, D), ALU.add)
                q, qs = heads(t_qkb[:, 0:D], 32), qst[:, u]
                if e == 5:
                    dve.wait_ge(*t_B.done(t + 1))
                    dve.wait_ge(*t_K.free(t))
                    n(v.tensor_tensor(t_qkb, bank(7, TK, 2 * D), bqk[:, :], ALU.add))
                    n(v.tensor_reduce(qs[:, 0:H1], q, AX, ALU.max))
                    v.tensor_tensor(q, q, wide(qs[:, 0:H1], H1, 32), ALU.subtract).then_inc(t_sub.s, 1)
                if e == 6:
                    dve.wait_ge(*t_exp.done(t + 1))
                    n(v.tensor_reduce(qs[:, H1:2 * H1], q, AX, ALU.add))
                    n(v.reciprocal(qs[:, 2 * H1:3 * H1], qs[:, H1:2 * H1]))
                    v.tensor_tensor(q, q, wide(qs[:, 2 * H1:3 * H1], H1, 32), ALU.mult).then_inc(t_q.s, 1)
                    stl.end()

            def m_slot(e, now, nxt, prv, g, adds):
                if prv:
                    m_tail(e, *prv)
                if nxt and e:
                    m_early(e, *nxt)
                if g:
                    if there(later(g, 1)):
                        one_hots(0, *later(g, 1))
                    add(0, *g, at=5)
                if now:
                    t, u = 2 * now[0] + now[1], now[1]
                    Xt = tile(X, t)
                    dve.wait_ge(*m_y.done(NE * t + e + 1))
                    dve.wait_ge(*(m_acc.done(NE * t + e) if e else m_x.done(t + 1)))
                    v.scalar_tensor_tensor(out=Xt, in0=bank(2 + e % 2, TK, D), scalar=rt[:, u, e:e + 1], in1=Xt,
                                           op0=ALU.mult, op1=ALU.add).then_inc(m_acc.s, 1)
                if nxt and e == 0:
                    m_early(e, *nxt)
                if nxt and e == 7:
                    Xt = tile(X, 2 * nxt[0] + nxt[1])
                    dve.wait_ge(*m_b.done(2 * nxt[0] + nxt[1] + 1))
                    v.tensor_tensor(Xt, Xt, bank(4, TK, D), ALU.add).then_inc(m_x.s, 1)
            experts(dve, m_slot)
            dve.drain().then_inc(phase, 1)
            dve.wait_ge(*ended(4))

            v.memset(HT[:, :, :], 0.0)
            dve.wait_ge(*l_row.done(3))
            dve.wait_ge(*l_raw.done(1))
            for k in range(NHID):
                if k:
                    dve.wait_ge(*l_b.done(k))
                v.tensor_tensor_reduce(l_jk, l_rawb[:, k * D:(k + 1) * D], l_bb, 1.0, 0.0, ALU.mult, ALU.add,
                                       bm[:, k:k + 1]).then_inc(l_b.s, 1)
            dve.wait_ge(*l_b.done(NHID))
            v.tensor_tensor(bm, bm, vT[:, V_BM1:V_BM1 + NHID], ALU.add)
            one_hots(1, 0, 0)
            dve.drain().then_inc(phase, 1)
            dve.wait_ge(*ended(5))
            context(1, C, 0)
            dve.drain().then_inc(phase, 1)
            dve.wait_ge(*ended(6))
            fold(1, C, 1.0)
            dve.drain().then_inc(phase, 1)
            dve.wait_ge(*ended(7))

            se = Steps(dve, e_dve, 4, passed)

            def e_step(now, nxt):
                if now:
                    j, u = now
                    gs = [later((NB + 3 * j, 0), 3 * u + i) for i in range(4)]
                if nxt:
                    n, w = 2 * nxt[0] + nxt[1], nxt[1]
                    se.tile(n)
                    dve.wait_ge(*e_o.done(n + 1))
                    se.done(v.tensor_tensor(e_hb[w], bank(0, TK, D), rows[:, 0, :], ALU.add))
                    v.tensor_tensor(e_hb[w], e_hb[w], tile(XN, n), ALU.add).then_inc(e_h.s, 1)
                    plainly(e_h.done(n + 1))
                    se.done(v.bn_stats(st[:, w, 0:6], e_hb[w]), plain=True)
                    v.bn_aggr(st[:, w, 6:8], st[:, w, 0:6]).then_inc(e_var.s, 1)
                if now:
                    one_hots(1, *gs[1])
                    add(1, *gs[0])
                if nxt:
                    dve.wait_ge(*e_T.free(n))
                    dve.wait_ge(*e_sd.done(n + 1))
                    se.done(v.reciprocal(st[:, w, 8:9], st[:, w, 9:10]))
                    v.tensor_scalar(e_yb[w], e_hb[w], st[:, w, 6:7], st[:, w, 8:9], ALU.subtract, ALU.mult)\
                        .then_inc(e_yh.s, 1)
                    se.done(v.tensor_tensor(e_hb[w], e_hb[w], rows[:, 1, :], ALU.add))
                    se.end()
                if now:
                    t = 2 * j + u
                    one_hots(1, *gs[2])
                    add(1, *gs[1])
                    Xt = tile(X, t)
                    v.tensor_tensor(Xt, Xt, e_hb[u], ALU.add).then_inc(e_hx.s, 1)
                    dve.wait_ge(*e_y.done(t + 1))
                    dve.wait_ge(*e_hx.done(t + 1))
                    v.tensor_tensor(Xt, Xt, bank(4, TK, D), ALU.add).then_inc(e_x.s, 1)
                    if nxt:
                        one_hots(1, *gs[3])
                    add(1, *gs[2])
            woven(dve, e_step)
            dve.drain().then_inc(phase, 1)
            dve.wait_ge(*ended(8))

            dve.wait_ge(*f_w.done(15))
            once.done(v.memset(f_blkb, 0.0))
            v.tensor_copy(f_blkb[0:64, :, 0:64], f_raw[0:64])
            v.tensor_copy(f_bxb, wide(vT[:, V_BSX:V_BSX + 4], 4, TK))
            v.tensor_copy(f_blkb[64:128, :, 64:128], f_raw[64:128]).then_inc(f_blk.s, 1)
            once.done(v.tensor_scalar(f_temp, f_temp, 0.1, 5.0, ALU.max, ALU.min))
            once.done(v.reciprocal(small[:, 44:52], f_temp))
            dve.wait_ge(*f_P.done(1))
            for c in range(C):
                v.tensor_tensor(heads(f_wxs[:, c, :], 64), heads(bank(3 + c, 128, INNER), 64),
                                wide(small[:, 44:52], HS, 64), ALU.mult)
            once.done(v.tensor_tensor(heads(f_bxs, 64), heads(bank(5, TK, INNER), 64),
                                    f_bsl.rearrange("p (a n) -> p a n", a=1).to_broadcast([TK, HS, 64]), ALU.add))
            once.done(v.tensor_tensor(heads(f_bxs, 64), heads(f_bxs, 64), wide(small[0:TK, 44:52], HS, 64), ALU.mult))
            dve.drain().then_inc(f_ready.s, 1)
            dve.wait_ge(*f_one.done(1))

            sf, sg = Steps(dve, f_dve, 2, passed), Steps(dve, f_sdve, 3, passed)

            def f_early(j, u):
                t = 2 * j + u
                sf.tile(t)
                Xt = tile(X, t)
                dve.wait_ge(*f_o.done(t + 1))
                v.tensor_tensor(Xt, Xt, bank(0, TK, D), ALU.add).then_inc(f_x.s, 1)
                plainly(f_x.done(t + 1), f_tok.free(t))
                norm(st[:, u], f_xsb[u][:, 0:D], Xt, sf.done, f_var, f_rstd, t).then_inc(f_xs.s, 1)
                sf.end()

            def f_late(j, u):
                t = 2 * j + u
                sg.tile(t)
                dve.wait_ge(*f_L.done(t + 1))
                L, s = heads(f_lgb[u], 64), qst[:, u]
                v.tensor_tensor(f_lgb[u], bank(2, TK, INNER), f_bxs, ALU.add).then_inc(f_lg.s, 1)
                dve.wait_ge(*f_lg.done(t + 1))
                sg.done(v.tensor_reduce(s[:, 0:HS], L, AX, ALU.max))
                v.tensor_tensor(L, L, wide(s[:, 0:HS], HS, 64), ALU.subtract).then_inc(f_sub.s, 1)
                dve.wait_ge(*f_exp.done(t + 1))
                sg.done(v.tensor_reduce(s[:, HS:2 * HS], L, AX, ALU.add))
                sg.done(v.reciprocal(s[:, 2 * HS:3 * HS], s[:, HS:2 * HS]))
                v.tensor_tensor(L, L, wide(s[:, 2 * HS:3 * HS], HS, 64), ALU.mult).then_inc(f_sw.s, 1)
                sg.end()
            skewed(dve, f_early, f_late)
            dve.drain().then_inc(phase, 1)
            dve.wait_ge(*ended(9))

            for a in range(4):
                once.done(v.tensor_scalar(small[:, 32 + a:33 + a], bank(4 + a, 128, 1, D), 1e-5, None, ALU.add))
            once.done(v.reciprocal(small[:, 52:56], small[:, 32:36]))
            for a in range(4):
                v.tensor_scalar(s_s[:, a, :], bank(4 + a, 128, PITCH), small[:, 52 + a:53 + a], None, ALU.mult)\
                    .then_inc(g_s.s, 1)
            once.done(v.memset(s_tb, 0.0))
            once.done(v.memset(s_at, 0.0))
            dve.wait_ge(*g_tok.done(1))
            P3 = bank(3, 128, 512).rearrange("p (a n) -> p a n", a=4)
            for lo in (0, 64):
                for o in (s_tc[lo:lo + 64], s_tb[lo:lo + 64, :, lo:lo + 64]):
                    v.tensor_copy(o, P3[lo:lo + 64, :, lo:lo + 64]).then_inc(g_tokc.s, 1)
            dve.wait_ge(*g_qkv.done(1))
            v.tensor_copy(s_k.rearrange("p a n -> p (a n)"), bank(5, 128, 256)).then_inc(g_kc.s, 1)
            dve.wait_ge(*g_sc.done(1))
            v.tensor_reduce(small[:, 32:36], bank(7, 128, 256).rearrange("p (a n) -> p a n", a=4), AX, ALU.max)\
                .then_inc(g_mx.s, 1)
            dve.wait_ge(*g_mx.done(1))
            v.tensor_scalar(small[:, 36:40], small[:, 32:36], -(64 ** -0.5), None, ALU.mult).then_inc(g_mx.s, 1)
            dve.wait_ge(*g_ex.done(1))
            once.done(v.reciprocal(small[:, 52:56], small[:, 40:44]))
            for lo in (0, 64):
                v.tensor_tensor(s_at[lo:lo + 64, :, lo:lo + 64], s_ec[lo:lo + 64],
                                wide(small[lo:lo + 64, 52:56], 4, 64), ALU.mult).then_inc(g_at.s, 1)
            dve.wait_ge(*g_aT.done(1))
            v.tensor_copy(s_aT.rearrange("p a n -> p (a n)"), bank(2, 128, 512)).then_inc(g_aTc.s, 1)
            dve.wait_ge(*g_M.done(1))
            for i in range(2):
                v.tensor_copy(M2[:, 2 * i:2 * i + 2, :], bank(3 + i, 128, 512).rearrange("p (a n) -> p a n", a=2))\
                    .then_inc(g_Mc.s, 1)

            def h_tile(j, u):
                t = 2 * j + u
                dve.wait_ge(*h_ss.done(t + 1))
                dve.wait_ge(*h_y.done(t + 1))
                dve.wait_ge(*h_st[u].free(j))
                v.tensor_tensor(h_obb[u], tile(X, t), bank(5 + u, TK, D), ALU.add).then_inc(h_ob.s, 1)
            tiles(dve, h_tile)


_INS = ['x', 'src', 'dst', 'edge_weight', 'L0_gnn_W', 'L0_gnn_b', 'L0_mix_w_qkv', 'L0_mix_mem_kv',
        'L0_mix_w_out', 'L0_mix_b_out', 'L0_mix_g_out', 'L0_mix_g_pre', 'L0_ffn_router_w', 'L0_ffn_w1',
        'L0_ffn_b1', 'L0_ffn_w2', 'L0_ffn_b2', 'L1_gnn_w1', 'L1_gnn_w2', 'L1_gnn_w3', 'L1_gnn_b3',
        'L1_mix_ln1_w', 'L1_mix_ln1_b', 'L1_mix_Wx', 'L1_mix_bx', 'L1_mix_Wq', 'L1_mix_Wk', 'L1_mix_Wv',
        'L1_mix_Wo', 'L1_mix_bo', 'L1_mix_ln2_w', 'L1_mix_ln2_b', 'L1_mix_W1', 'L1_mix_b1', 'L1_mix_W2',
        'L1_mix_b2', 'L1_ffn_W_fx', 'L1_ffn_b_fx', 'L1_ffn_W_x', 'L1_ffn_b_x', 'L1_ffn_W_slice',
        'L1_ffn_b_slice', 'L1_ffn_W_q', 'L1_ffn_W_k', 'L1_ffn_W_v', 'L1_ffn_W_out', 'L1_ffn_b_out',
        'L1_ffn_temperature']
_OUTS = [((N, D), 'float32')]


def kernel(**inputs):
    import numpy as _np
    import concourse.bacc as _bacc
    from concourse import mybir as _mybir
    from concourse.bass_utils import run_bass_kernel_spmd as _run

    nc = _bacc.Bacc("TRN2", target_bir_lowering=False, num_devices=1)
    arrays, args = {}, []
    for name in _INS:
        a = _np.ascontiguousarray(inputs[name])
        arrays[f"in_{name}_dram"] = a
        args.append(nc.dram_tensor(f"in_{name}_dram", a.shape, _mybir.dt.from_np(a.dtype), kind="ExternalInput").ap())
    for i, (shape, dtype) in enumerate(_OUTS):
        dt = _mybir.dt.from_np(_np.dtype(dtype))
        args.append(nc.dram_tensor(f"out_{i}_dram", shape, dt, kind="ExternalOutput").ap())
    build(nc, *args)
    r = _run(nc, [arrays], core_ids=[0])
    return r.results[0]["out_0_dram"]
```

```python
from contextlib import ExitStack

import concourse.bass as bass
from concourse import mybir

F32 = mybir.dt.float32
I32 = mybir.dt.int32
ALU = mybir.AluOpType
ACT = mybir.ActivationFunctionType
AX = mybir.AxisListType.X

N = 3125
D = 256
TK = 125
T = N // TK
C = D // 128
E = 53125
NCH = E // TK
GK = 5
NG = NCH // GK
W = 96
NW = (N + W - 1) // W
FAR = 4096.0
HTW = N + W
BT = 5
NB = T // BT
NE = 8
NM = 4
NHID = 8
H1 = 8
HS = 8
INNER = 512
G0 = T + 2 * NB
T_G = (NG - G0 + 1) // 3
GSLOTS = (1, 3, 6)
LOOPED = (T_G - 3) // 2
LOW = -(-TK // 3)
G1 = 2 * NB
LAG = 3
PEELED = 6
LOW0 = max([TK * ((g - G0 + 1) // 3 + 3) - LOW * g for g in range(G0, NG)] +
           [TK * ((g - G1) // 3 - LAG + 1) - LOW * g for g in range(G1, NG)])
PITCH = D + 1
EPS = 1e-5


class Steps:

    def __init__(self, eng, sem, per, passed):
        self.eng, self.sem, self.per, self.passed, self.k = eng, sem, per, passed, 0

    def tile(self, t):
        self.base, self.k = t * self.per, 0

    def done(self, ins, plain=False):
        self.k += 1
        ins.then_inc(self.sem, 1)
        self.eng.wait_ge(self.sem, self.base + self.k)
        if plain:
            self.eng.sem_inc(self.passed, 1)

    def end(self):
        assert self.k == self.per, (self.k, self.per)


def build(nc, x, src, dst, edge_weight, W0g, b0g, wqkv, mem_kv, wout0, bout0, gout0, gpre, router, we1, be1,
          we2, be2, g1w1, g1w2, g1w3, g1b3, ln1w, ln1b, Wx, bx, Wq, Wk, Wv, Wo, bo, ln2w, ln2b, Wm1, bm1, Wm2, bm2,
          Wfx, bfx, Wsx, bsx, Wsl, bsl, Wsq, Wsk, Wsv, Wout, bout, temp, out):
    table = [nc.dram_tensor(f"table{i}", (N, D), F32, kind="Internal").ap() for i in range(2)]
    with ExitStack() as ctx:
        def sb(name, shape, dt=F32):
            return ctx.enter_context(nc.sbuf_tensor(name, shape, dt))

        def sem(name):
            return ctx.enter_context(nc.semaphore(name))

        X = sb("X", [TK, T, D])
        XN = sb("XN", [TK, T, D])
        KQ = sb("KQ", [128, 4, N])
        HT = sb("HT", [128, C, HTW])
        big = sb("big", [128, 8192])
        stg = sb("stg", [128, 2562])
        onehot = sb("onehot", [TK, 2, GK, W])
        src_i = sb("src_i", [TK, NCH], I32)
        dst_r = sb("dst_r", [TK, NCH])
        w_e = sb("w_e", [TK, NCH])
        tq = sb("tq", [TK, 3 * D])
        idx = sb("idx", [TK, 2, GK], I32)
        base = sb("base", [1, NG], I32)
        x_low, x_left, x_one = sb("x_low", [NG, 1]), sb("x_left", [NG, 1]), sb("x_one", [NG, 1])
        x_cnt = sb("x_cnt", [1, 1], I32)
        x_d = sb("x_d", [TK, GK])
        iota = sb("iota", [TK, W])
        ident = sb("ident", [128, 128])
        mask32 = sb("mask32", [128, 128])
        WA = sb("WA", [128, C, 2 * D])
        WB = sb("WB", [128, C, 2 * D])
        WV = sb("WV", [128, C, D])
        WoT = sb("WoT", [128, C, D])
        M = sb("M", [128, C, D])
        rT = sb("rT", [128, C, NE])
        vecs = sb("vecs", [48, 128])
        vT = sb("vT", [128, 48])
        b2row = sb("b2row", [NE, D])
        rows = sb("rows", [TK, 4, D])
        bqk = sb("bqk", [TK, 2 * D])
        bvc = sb("bvc", [128, C])
        rr = sb("rr", [TK, T])
        kmax = sb("kmax", [128, C])
        ksum = sb("ksum", [128, C, NB])
        small = sb("small", [128, 64])
        MV = sb("MV", [TK, T, 2])
        st = sb("st", [TK, 2, 9])
        st2 = sb("st2", [TK, 2, 9])
        qst = sb("qst", [TK, 2, 3 * H1])
        fsx = sb("fsx", [128, 4, D])
        rt = sb("rt", [TK, 2, 48])
        rt2 = sb("rt2", [TK, 14])
        cT = sb("cT", [NE, TK])
        neghalf = sb("neghalf", [TK, T])
        pb = ctx.enter_context(nc.psum_tensor("pb", [128, 8, 512], F32))

        V_GPRE, V_B1, V_LN1W, V_BX, V_LN2W, V_BM1, V_B3, V_BSX = 0, 2, 18, 20, 22, 24, 32, 34
        NV = 38
        VECS = ((gpre, V_GPRE), (be1, V_B1), (ln1w, V_LN1W), (bx, V_BX), (ln2w, V_LN2W), (bm1, V_BM1),
                (g1b3, V_B3), (bsx, V_BSX))

        def part(buf, at, shape):
            n = 1
            for s in shape[1:]:
                n *= s
            v = buf[0:shape[0], at:at + n]
            if len(shape) == 3:
                v = v.rearrange("p (a b) -> p a b", b=shape[2])
            if len(shape) == 4:
                v = v.rearrange("p (a b c) -> p a b c", b=shape[2], c=shape[3])
            return v

        rows_ = part(big, 4096, [TK, 2, GK, D])
        ring = [[rows_[:, b, k, :] for k in range(GK)] for b in range(2)]
        ring2 = [[XN[:, T - 1 - k, :] for k in range(GK)],
                 [KQ[0:TK, (0, 2, 3)[k // 2], N - (1 + k % 2) * D:N - (k % 2) * D] for k in range(GK)]]
        w1 = part(big, 0, [128, NE, C, D])
        w2 = part(big, 4096, [128, NE, C, D])
        w1T = part(big, 0, [128, C, NHID * 128])
        w2T = part(big, 2048, [128, NHID, D])
        W0, Wg, wo0 = part(big, 6656, [128, C, D]), part(big, 7168, [128, C, 384]), part(big, 7936, [128, D])

        def bank(i, p, n, at=0):
            return pb[0:p, i, at:at + n]

        class Signal:

            def __init__(self, name, free=0, unit=1, sem=None, after=0):
                self.s = ctx.enter_context(nc.semaphore(name)) if sem is None else sem
                self.credit, self.unit, self.after = free * unit, unit, after

            def done(self, k):
                return self.s, (k + self.after) * self.unit + self.credit

            def free(self, k):
                return self.s, (k + self.after + 1) * self.unit

            def next(self, n):
                return Signal(None, self.credit // self.unit, self.unit, self.s, self.after + n)

        def in_turn(name, *counts):
            s, after, made = ctx.enter_context(nc.semaphore(name)), 0, []
            for n in counts:
                made.append(Signal(None, sem=s, after=after))
                after += n
            return made

        s_in = Signal("s_in", unit=16)
        s_x = Signal("s_x", unit=16)
        s_w = Signal("s_w", unit=16)
        s_w12 = Signal("s_w12", unit=16)
        l_raw = Signal("l_loaded", unit=16)
        l_row = Signal("l_rows_loaded", unit=16)
        f_w = Signal("f_loaded", unit=16)
        g_w = Signal("g_loaded", unit=16)
        phase = ctx.enter_context(nc.semaphore("phase_ended"))
        ENDS = (4, 3, 3, 3, 4, 3, 3, 3, 4)

        def ended(i):
            return phase, sum(ENDS[:i + 1])

        s_const, a_rr = in_turn("pool_once", 6, 2)
        (s_tT, s_cnt, s_vT, o_mT, o_pe0, w_T, w_P, l_T, f_T, f_P, o_pe1, g_T, g_tok, g_qkv, g_sc, g_aT,
         g_M) = in_turn("pe_once", 3, 1, 1, 1, 3, 1, 1, 2 * NHID, 1, 1, 3 * C, 1, 1, 1, 1, 1, 1)
        o_pe = (o_pe0, o_pe1)
        o_mTc, o_gTc0, w_Tc, w_Pc, f_Tc, o_gTc1, g_Tc, g_qkvc, g_vw, g_ex = in_turn(
            "act_once", 1, 1, 4, 1, 2, C, 3, 2, 2, 1)
        o_gTc = (o_gTc0, o_gTc1)
        (s_rel, s_tab, s_left, s_vTc, c_max0, o_mem, o_v0, w_blk, w_b, l_b, f_blk, f_ready, c_max1, o_v1, g_blk,
         g_s, g_tokc, g_kc, g_mx, g_at, g_aTc, g_Mc) = in_turn(
            "dve_once", 2, 3, 1, 3, 1, 1, 3, 3, 1, NHID, 1, 1, 1, 3 * C, 1, 4, 4, 1, 2, 2, 1, 2)
        c_max, o_v = (c_max0, c_max1), (o_v0, o_v1)
        passed, pe_passed, pool_passed = (ctx.enter_context(nc.semaphore(f"{e}_passed")) for e in ("dve", "pe", "pool"))
        dve_steps = ctx.enter_context(nc.semaphore("dve_steps"))
        x_n, x_idx, x_got = Signal("x_counted"), Signal("x_staged"), Signal("x_got", unit=16 * GK)
        x_off, x_oh = Signal("x_shifted", 1), Signal("x_onehot")
        x_sum, x_acc = Signal("x_summed", 1), Signal("x_added", 1)
        g_idx, g_oh = Signal("g_staged"), Signal("g_onehot")
        g_agg, g_acc = Signal("g_summed", 2), Signal("g_added", 2)
        g_got = [Signal(f"g_got{b}", unit=16 * GK) for b in range(2)]
        g_idx, g_oh, g_agg, g_acc = ((s, s.next(NG)) for s in (g_idx, g_oh, g_agg, g_acc))
        g_got = (g_got, [g_got[0].next(NG // 2 + 1), g_got[1].next(NG // 2)])
        a_dve = ctx.enter_context(nc.semaphore("a_dve"))
        a_var, a_rstd = Signal("a_variance"), Signal("a_rstd")
        a_xs = Signal("a_normed")
        a_T = Signal("a_transposed")
        a_xT = Signal("a_xT", 2)
        a_sq = Signal("a_squared", 2)
        a_kept = Signal("a_kept", 2)
        a_p = Signal("a_projected", 2)
        a_pr = Signal("a_rows", 2)
        a_st = [Signal(f"a_stored{u}", 1, 16) for u in range(2)]
        k_ys = Signal("k_scaled")
        k_T = Signal("k_transposed", 2)
        k_yT = Signal("k_yT", 2)
        k_L = Signal("k_logits", 2)
        k_k = Signal("k_keys", 2)
        k_sub = Signal("k_shifted", 2)
        k_exp = Signal("k_exp")
        k_mdve = ctx.enter_context(nc.semaphore("k_mdve"))
        k_dve = ctx.enter_context(nc.semaphore("k_dve"))
        k_q = Signal("k_queries")
        k_KT = Signal("k_kq_transposed")
        k_KQ = Signal("k_kq_out", 2)
        c_es, c_T, c_er, c_G = (Signal("c_exp"), Signal("c_transposed", 1), Signal("c_rows", 1),
                                Signal("c_summed", 1))
        c_es, c_T, c_er, c_G = ((s, s.next(NB)) for s in (c_es, c_T, c_er, c_G))
        c_hh = Signal("c_normed")
        m_hs = Signal("m_staged")
        m_o = Signal("m_out_rows", 1)
        m_bo = Signal("m_biased")
        m_ss = Signal("m_norm")
        m_dve = ctx.enter_context(nc.semaphore("m_dve"))
        m_sq, m_rn = Signal("m_norm_bounded"), Signal("m_norm_inverse")
        m_var, m_rstd = Signal("m_variance"), Signal("m_rstd")
        m_xs = Signal("m_normed")
        m_T = Signal("m_transposed")
        m_xT = Signal("m_xT")
        m_r = Signal("m_router")
        m_mx = Signal("m_router_max")
        m_ex = Signal("m_router_exp")
        m_c = Signal("m_weights")
        m_cT = Signal("m_weights_transposed")
        m_cTc = Signal("m_weights_out")
        m_b = Signal("m_bias")
        m_x = Signal("m_started", 1)
        m_h = Signal("m_hidden")
        m_g = Signal("m_gelu", 2)
        m_y = Signal("m_out", 2)
        m_acc = Signal("m_added", 2)
        t_dve = ctx.enter_context(nc.semaphore("t_dve"))
        t_var, t_rstd = Signal("t_variance"), Signal("t_rstd")
        t_fs = Signal("t_normed")
        t_kept = Signal("t_kept", 1)
        t_hh = Signal("t_normed_twice")
        t_T = Signal("t_transposed", 2)
        t_Tc = Signal("t_transposed_out")
        t_A = Signal("t_messages")
        t_B = Signal("t_logits")
        t_pr = Signal("t_rows")
        t_st = Signal("t_stored", 1, 16)
        t_sub = Signal("t_shifted")
        t_exp = Signal("t_exp")
        t_q = Signal("t_queries")
        t_K = Signal("t_kq_transposed", 1)
        t_KQ = Signal("t_kq_out", 1)
        l_ev = Signal("l_transposed_out", 4)
        e_qs = Signal("e_staged")
        e_o = Signal("e_mixed", 2)
        e_dve = ctx.enter_context(nc.semaphore("e_dve"))
        e_h = Signal("e_sum", 1)
        e_var, e_rstd = Signal("e_variance"), Signal("e_rstd")
        e_yh = Signal("e_normed")
        e_T = Signal("e_transposed", 2)
        e_yT = Signal("e_yT", 1)
        e_H = Signal("e_hidden")
        e_g = Signal("e_gelu", 2)
        e_y = Signal("e_out", 1)
        e_x = Signal("e_added", 1)
        e_hx = Signal("e_sum_added")
        f_hs = Signal("f_staged")
        f_o = Signal("f_message_rows", 2)
        f_dve = ctx.enter_context(nc.semaphore("f_dve"))
        f_x = Signal("f_stream", 1)
        f_var, f_rstd = Signal("f_variance"), Signal("f_rstd")
        f_xs = Signal("f_normed")
        f_tT = Signal("f_x_transposed")
        f_xT = Signal("f_xT", 1)
        f_L = Signal("f_logits")
        f_lg = Signal("f_logits_out", 2)
        f_sub = Signal("f_shifted")
        f_exp = Signal("f_exp")
        f_mdve = ctx.enter_context(nc.semaphore("f_mdve"))
        f_sdve = ctx.enter_context(nc.semaphore("f_sdve"))
        f_sw = Signal("f_slices")
        f_S = Signal("f_slices_transposed")
        f_sT = Signal("f_slices_out", 3)
        f_tok = Signal("f_tokens", 2)
        h_bx = Signal("h_biased")
        h_ss = Signal("h_staged")
        h_y = Signal("h_out", 2)
        h_ob = Signal("h_rows", 2)
        h_st = [Signal(f"h_stored{u}", 1, 16) for u in range(2)]

        block = ctx.enter_context(nc.Block())

        def cols(t):
            return bass.ds(t * TK, TK)

        def one(t):
            return bass.ds(t, 1)

        def tile(a, t):
            return a[:, one(t), :].rearrange("p a b -> p (a b)")

        def tiles(eng, step):
            with eng.Fori(0, T // 2) as j:
                for u in range(2):
                    step(j, u)
            step(T // 2, 0)

        def staged(eng, step, peel=0):
            step((0, 0), None, None)
            step((0, 1), (0, 0), None)

            def both(j):
                step((j + 1, 0), (j, 1), (j, 0))
                step((j + 1, 1), (j + 1, 0), (j, 1))
            for j in range(peel):
                both(j)
            with eng.Fori(peel, T // 2 - 1) as j:
                both(j)
            step((T // 2, 0), (T // 2 - 1, 1), (T // 2 - 1, 0))
            step(None, (T // 2, 0), (T // 2 - 1, 1))
            step(None, None, (T // 2, 0))

        def mixed(eng, step):
            def one_tile(t, j=None):
                def at(k, per):
                    if j is None:
                        return (k // 2, k % 2) if k >= 0 else None
                    return j * per + k // 2, k % 2
                now, nxt = t < T, t + 1 < T or j is not None
                a, b, c = (at(t - LAG - i, 1) if t - LAG - i < T else None for i in range(3))
                g = G1 + 3 * t
                gs = [at(g + i, 3) for i in range(3)] if now else []
                step(at(t, 1) if now else None, at(t + 1, 1) if nxt else None, gs, a, b, c,
                     min(g, NG) if j is None else j * 6 + g)
            step(None, (0, 0), [], None, None, None, 0)
            for t in range(PEELED):
                one_tile(t)
            with eng.Fori(0, (T - 1 - PEELED) // 2) as j:
                one_tile(PEELED, j)
                one_tile(PEELED + 1, j)
            for t in range(T - 1, T + LAG + 2):
                one_tile(t)

        def experts(eng, slot):
            def one_tile(now, nxt, prv, adds, first=None, at=()):
                for e in range(NE):
                    slot(e, now, nxt, prv, later(first, at.index(e)) if e in at else None, adds)
            one_tile(None, (0, 0), None, G0)
            g0 = (G0 // 2, G0 % 2)
            one_tile((0, 0), (0, 1), None, G0, g0, GSLOTS[1:])
            with eng.Fori(0, LOOPED) as j:
                g = later((j * 3 + g0[0], g0[1]), 2)
                one_tile((j, 1), (j + 1, 0), (j, 0), j * 6 + (G0 + 2), g, GSLOTS)
                one_tile((j + 1, 0), (j + 1, 1), (j, 1), j * 6 + (G0 + 5), later(g, 3), GSLOTS)
            for t in range(2 * LOOPED + 1, T_G):
                one_tile(*((i // 2, i % 2) for i in (t, t + 1, t - 1)), G0 + 3 * t - 1, later(g0, 3 * t - 1), GSLOTS)
            with eng.Fori(T_G // 2, T // 2 - 1) as j:
                one_tile((j, 1), (j + 1, 0), (j, 0), NG)
                one_tile((j + 1, 0), (j + 1, 1), (j, 1), NG)
            one_tile((T // 2 - 1, 1), (T // 2, 0), (T // 2 - 1, 0), NG)
            one_tile((T // 2, 0), None, (T // 2 - 1, 1), NG)
            one_tile(None, None, (T // 2, 0), NG)

        def raw(i):
            return KQ[:, 2, i * 512:(i + 1) * 512].rearrange("p (c n) -> p c n", c=C)

        def row(v):
            return v.rearrange("(a n) -> a n", a=1)

        def leftover(eng):
            eng.wait_ge(*s_left.done(1))
            return eng.value_load(x_cnt[0:1, 0:1], min_val=0, max_val=E)

        def later(g, k):
            return g[0] + (g[1] + k) // 2, (g[1] + k) % 2

        def there(g):
            return not isinstance(g[0], int) or 2 * g[0] + g[1] < NG

        def every(v, p):
            return row(v).partition_broadcast(p).rearrange("p a n -> p (a n)")

        r_g1, r_g2, r_g3, r_x, r_o = (raw(i) for i in range(5))
        r_g2T = KQ[:, 0, 0:C * D].rearrange("p (c n) -> p c n", c=C)
        r_q = [KQ[:, 3, i * 128:(i + 1) * 128] for i in range(3)]
        r_qT = [KQ[:, 3, 384 + i * 128:512 + i * 128] for i in range(3)]
        r_b = KQ[:, 3, 768:1024]
        r_jk = KQ[:, 3, 1024:1280]
        r_xb0, r_xb = KQ[:, 3, 1280:1280 + C], KQ[:, 3, 1288:1288 + C]
        r_xbb = KQ[:, 3, 1408:1408 + C * TK].rearrange("p (c n) -> p c n", c=C)
        r_b3b = KQ[:, 3, 1664:1664 + C * TK].rearrange("p (c n) -> p c n", c=C)
        r_rt = KQ[0:NE, 3, 2048:2048 + D]
        r_q32 = [KQ[:, 3, 2304 + 32 * i:2336 + 32 * i] for i in range(3)]
        e_i = KQ[0:NG, 0, 0:2 * GK * TK].bitcast(I32).rearrange("g (a k e) -> g a k e", a=2, k=GK)
        e_f = KQ[0:NG, 1, 0:3 * GK * TK].rearrange("g (a k e) -> g a k e", a=3, k=GK)
        e_rel, e_bad = (KQ[0:NG, 1, i * GK * TK:(i + 1) * GK * TK].rearrange("g (k e) -> g k e", k=GK) for i in (3, 4))
        x_lowr = KQ[0:1, 3, 2560:2560 + NG].bitcast(I32)
        mk, mv = small[:, 0:NM], small[:, NM:2 * NM]
        den, msum, nmax = small[:, 8:8 + C], small[:, 10:11], small[:, 12:12 + C]
        mkT, mvT = stg[0:NM, 2304:2432], stg[0:NM, 2432:2560]
        a_s = [part(stg, 256 * u, [TK, D]) for u in range(2)]
        a_xTb = [part(stg, 512 + 256 * u, [128, C, TK]) for u in range(2)]
        a_prb = [part(stg, 1024 + 256 * u, [TK, D]) for u in range(2)]
        a_sqb = part(stg, 1536, [TK, D])
        k_qb = [part(stg, 1024 + 128 * u, [TK, 128]) for u in range(2)]
        k_kb = [part(stg, 1280 + 128 * u, [TK, 128]) for u in range(2)]
        c_esb, c_erb, c_hhb = part(stg, 0, [128, BT * TK]), part(stg, 640, [TK, BT, 128]), part(big, 6656, [TK, BT, D])
        o_gb, o_gTb = part(stg, 1280, [128, D]), part(stg, 1536, [128, C, 128])
        o_kvb, o_mkb = part(stg, 1792, [128, 128]), part(stg, 1920, [128, NM])
        m_sb = [part(stg, 256 * u, [TK, D]) for u in range(2)]
        m_xTb = [part(stg, 512 + 256 * u, [128, C, TK]) for u in range(2)]
        m_gb = [part(stg, 1024 + 256 * u, [128, C, TK]) for u in range(2)]
        m_qsb, m_hsb = part(stg, 1536, [128, TK]), part(stg, 1664, [128, C, TK])
        m_ob, m_gnb = part(stg, 1920, [TK, D]), part(stg, 2176, [TK, D])
        t_prb, t_qkb = tq[:, 0:D], tq[:, D:3 * D]
        t_fsb, t_hhb = fsx[0:TK, 0], fsx[0:TK, 1]
        t_fT = fsx[:, 2, 0:C * TK].rearrange("p (c n) -> p c n", c=C)
        t_hT = fsx[:, 3, 0:C * TK].rearrange("p (c n) -> p c n", c=C)
        l_rawb, l_bb, l_jk = part(stg, 0, [128, NHID * D]), part(stg, 2048, [128, D]), part(stg, 2304, [128, D])
        bm = small[:, 16:16 + NHID]
        e_qsb = [part(stg, 256 * u, [128, C, TK]) for u in range(2)]
        e_hb = [part(stg, 512 + 256 * u, [TK, D]) for u in range(2)]
        e_yb = [part(stg, 1024 + 256 * u, [TK, D]) for u in range(2)]
        e_yTb = [part(stg, 1536 + 256 * u, [128, C, TK]) for u in range(2)]
        e_gb = part(big, 6656, [128, NHID, TK])
        f_wx, f_wxs, f_bxs = WA, WA, bqk
        f_wxT = WB[:, :, :].rearrange("p c (a n) -> p (c a) n", n=D)
        fs = fsx[:, :, :].rearrange("p a n -> p (a n)")
        f_raw, f_blkb, f_bxb = part(fs, 0, [128, 64]), part(fs, 64, [128, 128]), part(fs, 192, [128, 4, TK])
        f_temp, f_bsl = part(fs, 700, [128, HS]), part(fs, 708, [TK, 64])
        f_xTb = part(fs, 0, [128, C, TK])
        f_hsb = [part(fs, 256 * (u + 1), [128, C, TK]) for u in range(2)]
        f_xsb = [tq[:, D * u:D * (u + 1)] for u in range(2)]
        f_lgb = [w[0:TK, :, :].rearrange("p c n -> p (c n)") for w in (WV, WoT)]
        f_nrm = part(stg, 2048, [128, 4, T])
        g_wfx, g_wout = part(big, 0, [128, C, INNER]), part(big, 1024, [128, 4, D])
        g_raw = part(big, 2048, [128, 3, 64])
        g_blkb, g_bfx = part(big, 2304, [128, 3, 128]), part(big, 2688, [1, INNER])
        HTf = HT[:, :, :].rearrange("p c n -> p (c n)")
        s_s, s_sT = part(HTf, 0, [128, 4, PITCH]), part(HTf, 1028, [128, 4, C, 128])
        s_tc, s_tb = part(HTf, 2052, [128, 4, 64]), part(HTf, 2308, [128, 4, 128])
        s_q, s_k = part(HTf, 2820, [128, 4, 128]), part(HTf, 3332, [128, 4, 64])
        s_v, s_at = part(HTf, 3588, [128, 4, 128]), part(HTf, 4100, [128, 4, 128])
        s_aT, s_vw = part(HTf, 4612, [128, 4, 128]), part(HTf, 5124, [128, 4, D])
        s_nr, s_ec = part(big, 7484, [1, INNER]), part(big, 6984, [128, 4, 64])
        M2 = fsx
        h_obb = [part(stg, 514 + 256 * u, [TK, D]) for u in range(2)]
        h_ssb = [part(stg, 1026 + 512 * u, [128, 4, TK]) for u in range(2)]

        @block.sync
        def _(sp):
            for s in (*a_st, t_st, *h_st):
                sp.sem_inc(s.s, s.credit)

            def load(o, i, s):
                sp.dma_start(o, i).then_inc(s.s, 16)

            load(e_i[:, 0], src.rearrange("(g k e) -> g k e", k=GK, e=TK), s_in)
            load(e_i[:, 1], dst.rearrange("(g k e) -> g k e", k=GK, e=TK), s_in)
            load(e_f[:, 2], edge_weight.rearrange("(g k e) -> g k e", k=GK, e=TK), s_in)
            sp.dma_start(base[:, :], dst.rearrange("(a g q) -> a g q", a=1, g=NG)[:, :, 0],
                         allow_slow_non_contiguous=True).then_inc(s_in.s, 16)
            xr = x.rearrange("(b t p) d -> b p t d", b=NB, p=TK)
            for b in range(NB):
                load(X[:, b * BT:(b + 1) * BT, :], xr[b], s_x)
            load(W0, W0g.rearrange("(c p) n -> p c n", p=128), s_in)
            load(Wg, wqkv.rearrange("(c p) n -> p c n", p=128), s_in)
            load(wo0, wout0, s_in)
            load(mk, mem_kv[0].rearrange("h d m -> (h d) m"), s_in)
            load(mv, mem_kv[1].rearrange("h d m -> (h d) m"), s_in)
            for i, v in enumerate((b0g, bout0, gout0)):
                load(rows[:, i, :], every(v, TK), s_in)
            load(b2row[:, :], be2, s_in)
            load(r_rt, router, s_in)
            for v, a in VECS:
                f = v if len(v.shape) == 1 else v.rearrange("a n -> (a n)")
                load(vecs[a:a + f.shape[0] // 128, :], f.rearrange("(k p) -> k p", p=128), s_in)
            for o, i in ((r_g1, g1w1), (r_g2, g1w2), (r_g3, g1w3), (r_x, Wx), (r_o, Wo)):
                load(o, i.rearrange("(c p) n -> p c n", p=128), s_w)
            for o, i in zip(r_q32, (Wq, Wk, Wv)):
                for a in range(4):
                    load(o[32 * a:32 * a + 32, :], i, s_w)
            load(r_b, every(ln1b, 128), s_w)
            load(w1, we1.rearrange("e (c p) n -> p e c n", p=128), s_w12)

            def store_a(j, u):
                sp.wait_ge(*a_pr.done(2 * j + u + 1))
                sp.dma_start(table[0][cols(2 * j + u), :], a_prb[u]).then_inc(a_st[u].s, 16)
            tiles(sp, store_a)

            sp.wait_ge(*ended(3))
            load(w2, we2.rearrange("e (c p) n -> p e c n", p=128), s_w12)

            def store_t(j, u):
                sp.wait_ge(*t_pr.done(2 * j + u + 1))
                sp.dma_start(table[1][cols(2 * j + u), :], t_prb).then_inc(t_st.s, 16)
            tiles(sp, store_t)

            sp.wait_ge(*ended(4))
            load(l_rawb.rearrange("p (c n) -> p c n", c=NHID), Wm1.rearrange("(c p) n -> p c n", p=128), l_raw)
            for i, v in enumerate((bo, bm2)):
                load(rows[:, i, :], every(v, TK), l_row)
            load(l_bb, every(ln2b, 128), l_row)
            load(f_wx[:, :, :], Wsx.rearrange("(c p) n -> p c n", p=128), f_w)
            for a in range(2):
                load(f_raw[64 * a:64 * a + 64, :], Wsl, f_w)
            load(f_temp, every(temp.rearrange("a h b c -> (a h b c)"), 128), f_w)
            load(f_bsl, every(bsl, TK), f_w)
            sp.wait_ge(*l_ev.done(NHID))
            sp.wait_ge(*l_b.done(NHID))
            load(l_rawb.rearrange("p (c n) -> p c n", c=C), Wm2.rearrange("(c p) n -> p c n", p=128), l_raw)

            sp.wait_ge(*ended(8))
            load(g_wfx, Wfx.rearrange("(c p) n -> p c n", p=128), g_w)
            load(g_wout, Wout.rearrange("(c p) n -> p c n", p=128), g_w)
            for i, v in enumerate((Wsq, Wsk, Wsv)):
                for a in range(2):
                    load(g_raw[64 * a:64 * a + 64, i, :], v, g_w)
            load(g_bfx, row(bfx), g_w)
            load(rows[:, 0, :], every(bout, TK), g_w)

            def store_h(j, u):
                sp.wait_ge(*h_ob.done(2 * j + u + 1))
                sp.dma_start(out[cols(2 * j + u), :], h_obb[u]).then_inc(h_st[u].s, 16)
            tiles(sp, store_h)
            sp.wait_ge(*h_st[0].done(T // 2 + 1))
            sp.wait_ge(*h_st[1].done(T // 2))

        @block.gpsimd
        def _(pool):
            pool.sem_inc(a_kept.s, a_kept.credit)
            pool.sem_inc(t_kept.s, t_kept.credit)
            nc.gpsimd.iota(iota[:, :], [[1, W]], base=0, channel_multiplier=0,
                           allow_small_or_imprecise_dtypes=True).then_inc(s_const.s, 1)
            nc.gpsimd.memset(neghalf[:, :], -0.5)
            nc.gpsimd.memset(x_one[:, :], 1.0)
            nc.gpsimd.iota(x_low[:, :], [[0, 1]], base=LOW0, channel_multiplier=LOW,
                           allow_small_or_imprecise_dtypes=True)
            nc.gpsimd.iota(x_lowr, [[LOW, NG]], base=LOW0, channel_multiplier=0)
            nc.gpsimd.memset(ident[:, :], 0.0).then_inc(s_const.s, 1)
            nc.gpsimd.memset(mask32[:, :], 1.0).then_inc(s_const.s, 1)
            pool.wait_ge(*s_const.done(3))
            nc.gpsimd.affine_select(out=ident[:, :], in_=ident[:, :], compare_op=ALU.not_equal, fill=1.0, base=0,
                                    pattern=[[-1, 128]], channel_multiplier=1).then_inc(s_const.s, 1)
            m = mask32[:, :].rearrange("p (b c) -> p b c", c=32)
            nc.gpsimd.affine_select(out=m, in_=m, compare_op=ALU.is_ge, fill=0.0, base=0,
                                    pattern=[[-32, 4], [0, 32]], channel_multiplier=1).then_inc(s_const.s, 1)
            pool.wait_ge(*s_const.done(5))
            nc.gpsimd.affine_select(out=m, in_=m, compare_op=ALU.is_ge, fill=0.0, base=31,
                                    pattern=[[32, 4], [0, 32]], channel_multiplier=-1).then_inc(s_const.s, 1)

            def rstd(st_, var, out, n):
                pool.wait_ge(*var.done(n + 1))
                nc.gpsimd.tensor_tensor(st_[:, 8:9], st_[:, 7:8], neghalf[:, 0:1], ALU.pow).then_inc(out.s, 1)

            def a_step(a, b, c):
                if a:
                    rstd(st[:, a[1]], a_var, a_rstd, 2 * a[0] + a[1])
                if b:
                    t, u = 2 * b[0] + b[1], b[1]
                    pool.wait_ge(*a_xs.done(t + 1))
                    nc.gpsimd.tensor_tensor(tile(X, t), tile(X, t), a_s[u], ALU.add).then_inc(a_kept.s, 1)
            staged(pool, a_step)
            pool.drain().then_inc(phase, 1)
            pool.wait_ge(*ended(0))
            nc.gpsimd.tensor_scalar(rr[:, :], rr[:, :], 1e-24, None, ALU.max).then_inc(a_rr.s, 1)
            pool.wait_ge(*a_rr.done(1))
            nc.gpsimd.tensor_tensor(rr[:, :], rr[:, :], neghalf[:, :], ALU.pow).then_inc(a_rr.s, 1)

            def fill(layer, g, ring):
                h, b = g
                g = 2 * h + b
                pool.wait_ge(*g_agg[layer].free(g))
                nc.gpsimd.tensor_copy(idx[:, b, :], src_i[:, bass.ds(g * GK, GK)]).then_inc(g_idx[layer].s, 1)
                pool.wait_ge(*s_tab.done(3))
                pool.wait_ge(*g_idx[layer].done(g + 1))
                for k in range(GK):
                    nc.gpsimd.indirect_dma_start(
                        out=ring[b][k], out_offset=None, in_=table[layer],
                        in_offset=bass.IndirectOffsetOnAxis(ap=idx[:, b, k:k + 1], axis=0),
                    ).then_inc(g_got[layer][b].s, 16)

            def left_out(layer):
                with pool.If(leftover(pool) > 0):
                    with pool.Fori(0, NG) as g:
                        pool.wait_ge(*x_sum.done(g * NW + layer * NG * NW))
                        nc.gpsimd.tensor_copy(idx[:, 0, :], src_i[:, bass.ds(g * GK, GK)]).then_inc(x_idx.s, 1)
                        pool.wait_ge(*x_idx.done(g + (layer * NG + 1)))
                        pool.sem_inc(pool_passed, 1)
                        for k in range(GK):
                            nc.gpsimd.indirect_dma_start(
                                out=ring[0][k], out_offset=None, in_=table[layer],
                                in_offset=bass.IndirectOffsetOnAxis(ap=idx[:, 0, k:k + 1], axis=0),
                            ).then_inc(x_got.s, 16)
                    pool.wait_ge(*x_sum.done((layer + 1) * NG * NW))

            pool.wait_ge(*s_tab.done(3))
            pool.wait_ge(*a_st[0].done(T // 2 + 1))
            pool.wait_ge(*a_st[1].done(T // 2))
            left_out(0)
            with pool.Fori(0, G0 // 2) as h:
                for b in range(2):
                    fill(0, (h, b), ring)
            fill(0, (G0 // 2, 0), ring)

            pool.wait_ge(*ended(2))
            fill(0, (G0 // 2, 1), ring2)
            fill(0, (G0 // 2 + 1, 0), ring2)
            pool.wait_ge(*ended(3))

            def stage_m(nxt, adds):
                t = 2 * nxt[0] + nxt[1]
                pool.wait_ge(*m_o.free(t))
                pool.wait_ge(*g_acc[0].done(adds))
                nc.gpsimd.tensor_copy(m_qsb, KQ[:, 1, cols(t)])
                nc.gpsimd.tensor_copy(m_hsb, HT[:, :, cols(t)]).then_inc(m_hs.s, 1)

            def m_slot(e, now, nxt, prv, g, adds):
                if nxt:
                    t, u = 2 * nxt[0] + nxt[1], nxt[1]
                    if e == 0 and now is None:
                        stage_m(nxt, adds)
                    if e == 1:
                        pool.wait_ge(*m_sq.done(t + 1))
                        nc.gpsimd.tensor_tensor(rt[:, u, 43:44], rt[:, u, 40:41], neghalf[:, 0:1], ALU.pow)\
                            .then_inc(m_rn.s, 1)
                    if e == 2:
                        rstd(st[:, u], m_var, m_rstd, t)
                if prv:
                    t = 2 * prv[0] + prv[1]
                    if e == 0:
                        rstd(st2[:, 0], t_var, t_rstd, 2 * t)
                    if e == 1:
                        rstd(st2[:, 1], t_var, t_rstd, 2 * t + 1)
                    if e == 2:
                        pool.wait_ge(*t_fs.done(t + 1))
                        nc.gpsimd.tensor_copy(tile(XN, t), t_fsb).then_inc(t_kept.s, 1)
                if e == 3 and nxt and not (isinstance(nxt[0], int) and 2 * nxt[0] + nxt[1] == T - 1):
                    stage_m(later(nxt, 1), adds)
                if g and there(later(g, 2)):
                    fill(0, later(g, 2), ring2)
            experts(pool, m_slot)
            pool.drain().then_inc(phase, 1)
            pool.wait_ge(*ended(4))
            pool.wait_ge(*t_st.done(T))
            left_out(1)
            with pool.Fori(0, G1 // 2 + 1) as h:
                for b in range(2):
                    fill(1, (h, b), ring)

            def e_step(now, nxt, gs, a, b, c, adds):
                if a:
                    rstd(st2[:, a[1]], f_var, f_rstd, 2 * a[0] + a[1])
                if nxt:
                    rstd(st[:, nxt[1]], e_var, e_rstd, 2 * nxt[0] + nxt[1])
                for g in gs:
                    if there(later(g, 2)):
                        fill(1, later(g, 2), ring)
            mixed(pool, e_step)

            pool.drain().then_inc(phase, 1)
            pool.wait_ge(*ended(8))
            pool.wait_ge(*g_w.done(10))

            def bias_h(j, u):
                t = 2 * j + u
                nc.gpsimd.tensor_tensor(tile(X, t), tile(X, t), rows[:, 0, :], ALU.add).then_inc(h_bx.s, 1)
            tiles(pool, bias_h)

        @block.tensor
        def _(pe):
            for s in (x_sum, a_p, k_T, k_L, g_agg[0], c_T[0], c_G[0], m_o, m_y, t_T, t_K, e_o, e_T, e_y, f_o,
                      f_tok, h_y):
                pe.sem_inc(s.s, s.credit)

            def mm(o, l, r, start=True, stop=True):
                return pe.matmul(o, l, r, start=start, stop=stop, skip_group_check=True)

            def tr(o, i):
                k = i.shape[0]
                return pe.transpose(o, i, ident[0:k, 0:k])

            def two(o, l, r):
                for c in range(C):
                    ins = mm(o, l[:, c, :], r[:, c, :], c == 0, c == C - 1)
                return ins

            def by_feature(b, s):
                for c in range(C):
                    ins = tr(bank(b, 128, TK, c * TK), s[:, c * 128:(c + 1) * 128])
                return ins

            def group(layer, h, b, ring=ring, at=None):
                g = 2 * h + b
                pe.wait_ge(*g_oh[layer].done(g + 1))
                pe.wait_ge(*(g_acc[layer].free(g) if at is None else g_acc[layer].done(g)))
                pe.wait_ge(*g_got[layer][b].done(h + 1))
                at = 6 + b if at is None else at
                for k in range(GK):
                    for c in range(C):
                        ins = mm(bank(at, 128, W, c * W), ring[b][k][:, c * 128:(c + 1) * 128],
                                 onehot[:, b, k, :], k == 0 and c == 0, k == GK - 1)
                ins.then_inc(g_agg[layer].s, 1)

            def left_out(layer):
                with pe.If(leftover(pe) > 0):
                    with pe.Fori(0, NG) as g:
                        pe.wait_ge(*x_got.done(g + (layer * NG + 1)))
                        pe.sem_inc(pe_passed, 1)
                        with pe.Fori(0, NW) as w:
                            n = g * NW + w + layer * NG * NW
                            pe.wait_ge(*x_oh.done(n + 1))
                            pe.wait_ge(*x_acc.done(n))
                            for k in range(GK):
                                for c in range(C):
                                    ins = mm(bank(7, 128, W, c * W), ring[0][k][:, c * 128:(c + 1) * 128],
                                             onehot[:, 0, k, :], k == 0 and c == 0, k == GK - 1)
                            ins.then_inc(x_sum.s, 1)

            pe.wait_ge(*s_const.done(6))
            pe.wait_ge(*s_rel.done(2))
            for a in range(3):
                for k in range(GK):
                    ins = tr(bank(a, TK, NG, k * NG), e_f[:, a, k, :])
                ins.then_inc(s_tT.s, 1)
            pe.wait_ge(*x_n.done(1))
            mm(bank(4, 1, 1), x_left[:, :], x_one[:, :]).then_inc(s_cnt.s, 1)
            tr(bank(3, 128, NV), vecs[0:NV, :])
            for c in range(C):
                tr(bank(3, 128, NE, 64 + c * NE), r_rt[:, c * 128:(c + 1) * 128])
            tr(bank(3, NM, 128, 256), mv).then_inc(s_vT.s, 1)
            pe.wait_ge(*s_vTc.done(3))
            pe.wait_ge(*s_tab.done(3))

            def a_step(a, b, c):
                if b:
                    t, u = 2 * b[0] + b[1], b[1]
                    pe.wait_ge(*a_xs.done(t + 1))
                    pe.wait_ge(*a_xT.free(t))
                    by_feature(u, a_s[u]).then_inc(a_T.s, 1)
                if c:
                    t, u = 2 * c[0] + c[1], c[1]
                    pe.wait_ge(*a_xT.done(t + 1))
                    pe.wait_ge(*a_pr.free(t))
                    two(bank(2 + u, TK, D), a_xTb[u], W0).then_inc(a_p.s, 1)
            staged(pe, a_step)
            pe.drain().then_inc(phase, 1)
            pe.wait_ge(*ended(0))
            left_out(0)

            def k_step(a, b, c):
                if b:
                    t, u = 2 * b[0] + b[1], b[1]
                    pe.wait_ge(*k_yT.done(t + 1))
                    pe.wait_ge(*k_sub.free(t))
                    pe.wait_ge(*k_k.free(t))
                    two(bank(2 + u, TK, 256), a_xTb[u], Wg[:, :, 0:256]).then_inc(k_L.s, 1)
                if a:
                    t, u = 2 * a[0] + a[1], a[1]
                    pe.wait_ge(*k_ys.done(t + 1))
                    pe.wait_ge(*k_yT.free(t))
                    by_feature(u, a_s[u]).then_inc(k_T.s, 1)
                if c:
                    group(0, *c)
                    t, u = 2 * c[0] + c[1], c[1]
                    pe.wait_ge(*k_k.done(t + 1))
                    pe.wait_ge(*k_KQ.free(t))
                    tr(bank(4 + u, 128, TK, 0), k_kb[u])
                    pe.wait_ge(*k_q.done(t + 1))
                    tr(bank(4 + u, 128, TK, TK), k_qb[u]).then_inc(k_KT.s, 1)
            staged(pe, k_step)
            pe.drain().then_inc(phase, 1)
            pe.wait_ge(*ended(1))

            def context(layer, nk, first):
                def step(g, start, h0):
                    for jj in range(nk):
                        n = g * nk + jj
                        pe.wait_ge(*c_es[layer].done(n + 1))
                        pe.wait_ge(*c_er[layer].free(n))
                        for i in range(BT):
                            ins = tr(bank(i // 4, TK, 128, (i % 4) * 128), c_esb[:, i * TK:(i + 1) * TK])
                        ins.then_inc(c_T[layer].s, 1)
                        for b in range(2) if nk == 1 else (jj,):
                            group(layer, *later((h0, first % 2), b))
                        pe.wait_ge(*c_er[layer].done(n + 1))
                        if layer == 1:
                            pe.wait_ge(*c_hh.done(g + 1))
                        for i in range(BT):
                            r = tile(XN, g * BT + i) if layer == 0 else c_hhb[:, i, :]
                            ins = mm(bank(4 + jj, 128, D), c_erb[:, i, :], r, start and i == 0, False)
                        ins.then_inc(c_G[layer].s, 1)
                step(0, True, first // 2)
                with pe.Fori(1, NB) as g:
                    step(g, False, g + first // 2)

            def fold(layer, nk, wv, wo):
                for jj in range(nk):
                    pe.wait_ge(*o_v[layer].done(3 * jj + 1))
                    for c in range(C):
                        ins = tr(bank(0, 128, 128, c * 128), o_gb[:, c * 128:(c + 1) * 128])
                    ins.then_inc(o_pe[layer].s, 1)
                    pe.wait_ge(*o_gTc[layer].done(jj + 1))
                    for c in range(C):
                        ins = mm(bank(1, 128, 128), wv(c, jj), o_gTb[:, c, :], c == 0, c == C - 1 and layer == 1)
                    if layer == 0:
                        pe.wait_ge(*o_mTc.done(1))
                        ins = mm(bank(1, 128, 128), mvT, mkT, False, True)
                    ins.then_inc(o_pe[layer].s, 1)
                    pe.wait_ge(*o_v[layer].done(3 * jj + 2))
                    mm(bank(2, 128, D), o_kvb, wo(jj)).then_inc(o_pe[layer].s, 1)

            context(0, 1, T)
            pe.drain().then_inc(phase, 1)
            pe.wait_ge(*ended(2))
            pe.wait_ge(*o_mem.done(1))
            tr(bank(3, NM, 128), o_mkb).then_inc(o_mT.s, 1)
            fold(0, 1, lambda c, jj: Wg[:, c, 256:384], lambda jj: wo0)
            pe.drain().then_inc(phase, 1)
            pe.wait_ge(*ended(3))

            pe.wait_ge(*s_w.done(18))
            pe.wait_ge(*w_blk.done(3))
            k = 0
            for r in (r_g1, r_g2, r_o):
                for c in range(C):
                    for a in range(C):
                        tr(bank(k // 4, 128, 128, (k % 4) * 128), r[:, a, c * 128:(c + 1) * 128])
                        k += 1
            for i in range(3):
                ins = tr(bank(3, 128, 128, i * 128), r_q[i])
            ins.then_inc(w_T.s, 1)
            pe.wait_ge(*w_Tc.done(4))
            pe.wait_ge(*w_b.done(1))
            for c in range(C):
                for m in range(C):
                    mm(bank(0, 128, D, c * D), r_g3[:, m, c * 128:(c + 1) * 128], r_g2T[:, m, :], m == 0, m == C - 1)
            two(bank(1, TK, D), r_b3b, r_g2T)
            for i in range(2):
                for c in range(C):
                    for a in range(C):
                        mm(bank(2 + c, 128, 128, i * D + a * 128), r_x[:, a, c * 128:(c + 1) * 128], r_qT[i])
                for a in range(C):
                    mm(bank(4, TK, 128, i * D + a * 128), r_xbb[:, a, :], r_qT[i])
            for c in range(C):
                for a in range(C):
                    mm(bank(5, 128, 128, c * D + a * 128), r_x[:, a, c * 128:(c + 1) * 128], r_qT[2])
            for a in range(C):
                ins = mm(bank(1, 128, 1, D + a), r_qT[2], r_xb[:, a:a + 1])
            ins.then_inc(w_P.s, 1)
            pe.wait_ge(*w_Pc.done(1))

            def m_up(t, u, e):
                pe.wait_ge(*m_g.free(NE * t + e))
                for a in range(C):
                    for c in range(C):
                        ins = mm(bank(e % 2, 128, TK, a * TK), w1[:, e, c, a * 128:(a + 1) * 128],
                                 m_xTb[u][:, c, :], c == 0, c == C - 1)
                ins.then_inc(m_h.s, 1)

            def m_slot(e, now, nxt, prv, g, adds):
                if nxt:
                    t, u = 2 * nxt[0] + nxt[1], nxt[1]
                    if e == 4:
                        pe.wait_ge(*m_xs.done(t + 1))
                        by_feature(4, m_sb[u]).then_inc(m_T.s, 1)
                    if e == 5:
                        pe.wait_ge(*m_xT.done(t + 1))
                        two(bank(4, TK, NE), m_xTb[u], rT).then_inc(m_r.s, 1)
                    if e == 7:
                        pe.wait_ge(*m_c.done(t + 1))
                        tr(bank(4, NE, TK), rt[:, u, 0:NE]).then_inc(m_cT.s, 1)
                if prv:
                    t = 2 * prv[0] + prv[1]
                    if e == 2:
                        pe.wait_ge(*t_fs.done(t + 1))
                        pe.wait_ge(*t_KQ.free(t))
                        by_feature(6, t_fsb).then_inc(t_T.s, 1)
                    if e == 3:
                        pe.wait_ge(*t_hh.done(t + 1))
                        by_feature(7, t_hhb).then_inc(t_T.s, 1)
                        pe.wait_ge(*t_Tc.done(2 * t + 1))
                        two(bank(6, TK, 2 * D), t_fT, WA).then_inc(t_A.s, 1)
                    if e == 4:
                        pe.wait_ge(*t_Tc.done(2 * t + 2))
                        two(bank(7, TK, 2 * D), t_hT, WB).then_inc(t_B.s, 1)
                    if e == 7:
                        pe.wait_ge(*t_q.done(t + 1))
                        for i in range(4):
                            a = (i + 2) % 4
                            ins = tr(bank(6, 128, TK, i * TK), t_qkb[:, a * 128:(a + 1) * 128])
                        ins.then_inc(t_K.s, 1)
                if g:
                    group(0, *g, ring2, at=5)
                if now and e + 1 < NE:
                    m_up(2 * now[0] + now[1], now[1], e + 1)
                if nxt and e == 0:
                    t = 2 * nxt[0] + nxt[1]
                    pe.wait_ge(*m_hs.done(t + 1))
                    pe.wait_ge(*m_x.free(t))
                    mm(bank(4, TK, D), m_qsb, M[:, 0, :])
                    for c in range(C):
                        ins = tr(bank(4, TK, 128, D + c * 128), m_hsb[:, c, :])
                    ins.then_inc(m_o.s, 1)
                if nxt and e + 1 == NE:
                    m_up(2 * nxt[0] + nxt[1], nxt[1], 0)
                if now:
                    n = NE * (2 * now[0] + now[1]) + e
                    pe.wait_ge(*m_g.done(n + 1))
                    pe.wait_ge(*m_acc.free(n))
                    two(bank(2 + e % 2, TK, D), m_gb[e % 2], w2[:, e]).then_inc(m_y.s, 1)
                if nxt and e == 7:
                    pe.wait_ge(*m_cTc.done(2 * nxt[0] + nxt[1] + 1))
                    mm(bank(4, TK, D), cT[:, :], b2row[:, :]).then_inc(m_b.s, 1)
            pe.wait_ge(*s_w12.done(2))
            experts(pe, m_slot)
            pe.drain().then_inc(phase, 1)
            pe.wait_ge(*ended(4))

            left_out(1)
            for i in range(2):
                pe.wait_ge(*l_raw.done(i + 1))
                for k in range(NHID):
                    pe.wait_ge(*l_ev.free(i * NHID + k))
                    for c in range(C):
                        a = k * D + c * 128 if i == 0 else c * NHID * 128 + k * 128
                        ins = tr(bank(k % 4, 128, 128, c * 128), l_rawb[:, a:a + 128])
                    ins.then_inc(l_T.s, 1)
            pe.wait_ge(*f_w.done(5))
            for a in range(4):
                for c in range(C):
                    ins = tr(bank(4 + a // 2, 128, 128, (a % 2) * 256 + c * 128), f_wx[:, c, a * 128:(a + 1) * 128])
            ins.then_inc(f_T.s, 1)
            pe.wait_ge(*f_blk.done(1))
            pe.wait_ge(*f_Tc.done(2))
            for a in range(4):
                for c in range(C):
                    mm(bank(6 + c, 128, 128, a * 128), f_wxT[:, a, c * 128:(c + 1) * 128], f_blkb)
                ins = mm(bank(4, TK, 128, a * 128), f_bxb[:, a, :], f_blkb)
            ins.then_inc(f_P.s, 1)
            pe.wait_ge(*f_ready.done(1))
            pe.drain().then_inc(phase, 1)
            pe.wait_ge(*ended(5))
            context(1, C, 0)
            pe.drain().then_inc(phase, 1)
            pe.wait_ge(*ended(6))
            fold(1, C, lambda c, jj: WV[:, c, jj * 128:(jj + 1) * 128], lambda jj: WoT[:, jj, :])
            pe.drain().then_inc(phase, 1)
            pe.wait_ge(*ended(7))

            def e_up(t, u, pairs):
                for a in range(2 * pairs[0], 2 * pairs[-1] + 2):
                    if a % 2 == 0:
                        pe.wait_ge(*e_g.free(4 * t + a // 2))
                    for c in range(C):
                        ins = mm(bank(2 + (a // 2) % 2, 128, TK, (a % 2) * TK), w1T[:, c, a * 128:(a + 1) * 128],
                                 e_yTb[u][:, c, :], c == 0, c == C - 1)
                    if a % 2:
                        ins.then_inc(e_H.s, 1)

            def f_a(j, u):
                t = 2 * j + u
                pe.wait_ge(*f_hs.done(t + 1))
                pe.wait_ge(*f_x.free(t))
                pe.wait_ge(*f_lg.free(t))
                pe.wait_ge(*f_sT.free(t))
                for i in range(C):
                    ins = tr(bank(1, TK, 128, i * 128), f_hsb[u][:, i, :])
                ins.then_inc(f_o.s, 1)

            def f_bx(a, j, u):
                t = 2 * j + u
                pe.wait_ge(*f_xs.done(t + 1))
                if a:
                    pe.wait_ge(*f_x.done(2 * a[0] + a[1] + 1))
                pe.wait_ge(*f_sT.free(t + 1))
                pe.wait_ge(*f_lg.free(t + 1))
                by_feature(1, f_xsb[u]).then_inc(f_tT.s, 1)

            def f_bl(j, u):
                pe.wait_ge(*f_xT.done(2 * j + u + 1))
                two(bank(1, TK, INNER), f_xTb, f_wxs).then_inc(f_L.s, 1)

            def f_cs(b, j, u):
                t = 2 * j + u
                if b:
                    pe.wait_ge(*f_lg.done(2 * b[0] + b[1] + 1))
                pe.wait_ge(*f_sT.done(t))
                pe.wait_ge(*f_sw.done(t + 1))
                for i in range(4):
                    ins = tr(bank(1, 128, TK, i * TK), f_lgb[u][:, i * 128:(i + 1) * 128])
                ins.then_inc(f_S.s, 1)

            def f_ct(j, u):
                start = isinstance(j, int) and (j, u) == (0, 0)
                for i in range(4):
                    ins = mm(bank(6 + i // 2, 128, D, (i % 2) * D), f_lgb[u][:, i * 128:(i + 1) * 128], f_xsb[u],
                             start and i % 2 == 0, False)
                ins.then_inc(f_tok.s, 1)

            def e_step(now, nxt, gs, a, b, c, adds):
                if now:
                    j, u = now
                    t = 2 * j + u
                    pe.wait_ge(*e_yT.done(t + 1))
                    e_up(t, u, (0, 1))
                if a:
                    f_a(*a)
                if nxt:
                    n, w = 2 * nxt[0] + nxt[1], nxt[1]
                    pe.wait_ge(*e_qs.done(n + 1))
                    pe.wait_ge(*e_h.free(n))
                    pe.wait_ge(*e_yT.free(n))
                    two(bank(0, TK, D), e_qsb[w], M).then_inc(e_o.s, 1)
                if now:
                    group(1, *gs[0], at=5)
                if b:
                    f_bx(a, *b)
                if now:
                    e_up(t, u, (2, 3))
                if b:
                    f_bl(*b)
                if now:
                    group(1, *gs[1], at=5)
                if nxt:
                    pe.wait_ge(*e_yh.done(n + 1))
                    by_feature(0, e_yb[w]).then_inc(e_T.s, 1)
                if c:
                    f_cs(b, *c)
                if now:
                    pe.wait_ge(*e_g.done(4 * t + 4))
                    pe.wait_ge(*e_x.free(t))
                    for i in range(NHID):
                        ins = mm(bank(4, TK, D), e_gb[:, i, :], w2T[:, i, :], i == 0, i == NHID - 1)
                    ins.then_inc(e_y.s, 1)
                if c:
                    f_ct(*c)
                if now:
                    group(1, *gs[2], at=5)
            mixed(pe, e_step)
            pe.drain().then_inc(phase, 1)
            pe.wait_ge(*ended(8))

            pe.wait_ge(*g_s.done(4))
            for a in range(4):
                for c in range(C):
                    tr(bank(a // 2, 128, 128, (a % 2) * 256 + c * 128), s_s[:, a, c * 128:(c + 1) * 128])
                ins = tr(bank(2, 1, 128, a * 128), s_s[:, a, D:PITCH])
            ins.then_inc(g_T.s, 1)
            pe.wait_ge(*g_Tc.done(3))
            pe.wait_ge(*g_w.done(10))
            pe.wait_ge(*g_blk.done(1))
            for a in range(4):
                o = bank(3, 128, 128, a * 128)
                for c in range(C):
                    mm(o, g_wfx[:, c, a * 128:(a + 1) * 128], s_sT[:, a, c, :], c == 0, False)
                ins = mm(o, g_bfx[:, a * 128:(a + 1) * 128], s_nr[:, a * 128:(a + 1) * 128], False, True)
            ins.then_inc(g_tok.s, 1)
            pe.wait_ge(*g_tokc.done(4))
            for a in range(4):
                mm(bank(4, 128, 128, a * 128), g_blkb[:, 0, :], s_tb[:, a, :])
                mm(bank(5, 128, 64, a * 64), g_blkb[:, 1, :], s_tc[:, a, :])
                ins = mm(bank(6, 128, 128, a * 128), g_blkb[:, 2, :], s_tb[:, a, :])
            ins.then_inc(g_qkv.s, 1)
            pe.wait_ge(*g_qkvc.done(2))
            pe.wait_ge(*g_kc.done(1))
            for a in range(4):
                mm(bank(7, 128, 64, a * 64), s_q[:, a, :], s_k[:, a, :])
                ins = mm(bank(a // 2, 128, D, (a % 2) * D), s_v[:, a, :], g_wout[:, a, :])
            ins.then_inc(g_sc.s, 1)
            pe.wait_ge(*g_at.done(2))
            for a in range(4):
                ins = tr(bank(2, 128, 128, a * 128), s_at[:, a, :])
            ins.then_inc(g_aT.s, 1)
            pe.wait_ge(*g_aTc.done(1))
            pe.wait_ge(*g_vw.done(2))
            for a in range(4):
                ins = mm(bank(3 + a // 2, 128, D, (a % 2) * D), s_aT[:, a, :], s_vw[:, a, :])
            ins.then_inc(g_M.s, 1)
            pe.wait_ge(*g_Mc.done(2))

            def h_tile(j, u):
                t = 2 * j + u
                pe.wait_ge(*h_ss.done(t + 1))
                pe.wait_ge(*h_ob.free(t))
                for a in range(4):
                    ins = mm(bank(5 + u, TK, D), h_ssb[u][:, a, :], M2[:, a, :], a == 0, a == 3)
                ins.then_inc(h_y.s, 1)
            tiles(pe, h_tile)

        @block.scalar
        def _(act):
            for s in (a_xT, a_sq, a_pr, k_yT, k_k, k_KQ, m_g, t_KQ, l_ev, e_yT, e_g, f_xT, f_sT):
                act.sem_inc(s.s, s.credit)

            def copy(o, i):
                return nc.scalar.activation(o, i, ACT.Copy)

            def blocks(b, p, n):
                return bank(b, p, C * n).rearrange("p (c n) -> p c n", c=C)

            def a_step(a, b, c):
                if b:
                    t, u = 2 * b[0] + b[1], b[1]
                    act.wait_ge(*a_xs.done(t + 1))
                    copy(tile(XN, t), a_s[u])
                    act.wait_ge(*a_T.done(t + 1))
                    act.wait_ge(*a_p.free(t))
                    copy(a_xTb[u], blocks(u, 128, TK)).then_inc(a_xT.s, 1)
                    act.wait_ge(*a_sq.done(t))
                    nc.scalar.activation(a_sqb, a_s[u], ACT.Square, accum_out=rr[:, one(t)]).then_inc(a_sq.s, 1)
                if c:
                    t, u = 2 * c[0] + c[1], c[1]
                    act.wait_ge(*a_p.done(t + 1))
                    act.wait_ge(*a_st[u].free(c[0]))
                    copy(a_prb[u], bank(2 + u, TK, D)).then_inc(a_pr.s, 1)
            staged(act, a_step)
            act.drain().then_inc(phase, 1)
            act.wait_ge(*ended(0))

            act.wait_ge(*a_rr.done(2))
            act.wait_ge(*a_st[0].done(T // 2 + 1))
            act.wait_ge(*a_st[1].done(T // 2))

            def k_step(a, b, c):
                if a:
                    t, u = 2 * a[0] + a[1], a[1]
                    act.wait_ge(*k_T.free(t))
                    nc.scalar.activation(a_s[u], tile(XN, t), ACT.Copy, scale=rr[:, one(t)]).then_inc(k_ys.s, 1)
                if b:
                    t, u = 2 * b[0] + b[1], b[1]
                    act.wait_ge(*k_sub.done(t + 1))
                    copy(k_kb[u], bank(2 + u, TK, 128, 128)).then_inc(k_k.s, 1)
                    nc.scalar.activation(k_qb[u], k_qb[u], ACT.Exp).then_inc(k_exp.s, 1)
                if a:
                    t, u = 2 * a[0] + a[1], a[1]
                    act.wait_ge(*k_T.done(t + 1))
                    act.wait_ge(*k_L.free(t))
                    copy(a_xTb[u], blocks(u, 128, TK)).then_inc(k_yT.s, 1)
                if c:
                    t, u = 2 * c[0] + c[1], c[1]
                    act.wait_ge(*k_KT.done(t + 1))
                    copy(KQ[:, 0:2, cols(t)], blocks(4 + u, 128, TK)).then_inc(k_KQ.s, 1)
            staged(act, k_step)
            act.drain().then_inc(phase, 1)
            act.wait_ge(*ended(1))

            def context(layer, nk):
                act.wait_ge(*c_max[layer].done(1))

                def step(g):
                    for jj in range(nk):
                        act.wait_ge(*c_T[layer].free(g * nk + jj))
                        nc.scalar.activation(c_esb, KQ[:, jj, bass.ds(g * BT * TK, BT * TK)], ACT.Exp,
                                             bias=nmax[:, jj:jj + 1], accum_out=ksum[:, jj, one(g)])\
                            .then_inc(c_es[layer].s, 1)
                with act.Fori(0, NB) as g:
                    step(g)

            context(0, 1)
            nc.scalar.activation(mk, mk, ACT.Exp, bias=nmax[:, 0:1], accum_out=msum)
            act.drain().then_inc(phase, 1)
            act.wait_ge(*ended(2))

            def fold(layer, nk):
                for jj in range(nk):
                    act.wait_ge(*o_pe[layer].done(3 * jj + 1))
                    copy(o_gTb, blocks(0, 128, 128)).then_inc(o_gTc[layer].s, 1)
            act.wait_ge(*o_mT.done(1))
            copy(mkT, bank(3, NM, 128)).then_inc(o_mTc.s, 1)
            fold(0, 1)
            act.drain().then_inc(phase, 1)
            act.wait_ge(*ended(3))

            act.wait_ge(*w_T.done(1))
            for o, b in ((WA[:, :, 0:D], 0), (r_g2T, 1), (WoT[:, :, :], 2)):
                copy(o, blocks(b, 128, D)).then_inc(w_Tc.s, 1)
            for i in range(3):
                ins = copy(r_qT[i], bank(3, 128, 128, i * 128))
            ins.then_inc(w_Tc.s, 1)
            act.wait_ge(*w_P.done(1))
            copy(WA[:, :, D:2 * D], blocks(0, 128, D))
            copy(rows[:, 3, :], bank(1, TK, D))
            copy(bvc[:, :], bank(1, 128, C, D))
            copy(bqk[:, :], bank(4, TK, 2 * D))
            for c in range(C):
                g = vT[:, V_LN1W + c:V_LN1W + c + 1]
                nc.scalar.activation(WB[:, c, :], bank(2 + c, 128, 2 * D), ACT.Copy, scale=g)
                ins = nc.scalar.activation(WV[:, c, :], bank(5, 128, D, c * D), ACT.Copy, scale=g)
            ins.then_inc(w_Pc.s, 1)

            def m_slot(e, now, nxt, prv, g, adds):
                if now:
                    n = NE * (2 * now[0] + now[1]) + e
                    act.wait_ge(*m_h.done(n + 1))
                    act.wait_ge(*m_y.free(n))
                    for a in range(C):
                        b = V_B1 + e * C + a
                        ins = nc.scalar.activation(m_gb[e % 2][:, a, :], bank(e % 2, 128, TK, a * TK), ACT.Gelu,
                                                   bias=vT[:, b:b + 1])
                    ins.then_inc(m_g.s, 1)
                if nxt and e == 1:
                    t, u = 2 * nxt[0] + nxt[1], nxt[1]
                    act.wait_ge(*m_bo.done(t + 1))
                    nc.scalar.activation(m_sb[u], m_ob, ACT.Square, accum_out=rt[:, u, 40:41]).then_inc(m_ss.s, 1)
                if prv:
                    t = 2 * prv[0] + prv[1]
                    if e == 2:
                        act.wait_ge(*t_T.done(2 * t + 1))
                        copy(t_fT, blocks(6, 128, TK)).then_inc(t_Tc.s, 1)
                    if e == 3:
                        act.wait_ge(*t_T.done(2 * t + 2))
                        copy(t_hT, blocks(7, 128, TK)).then_inc(t_Tc.s, 1)
                    if e == 5:
                        act.wait_ge(*t_sub.done(t + 1))
                        nc.scalar.activation(t_qkb[:, 0:D], t_qkb[:, 0:D], ACT.Exp).then_inc(t_exp.s, 1)
                if nxt:
                    t, u = 2 * nxt[0] + nxt[1], nxt[1]
                    if e == 4:
                        act.wait_ge(*m_T.done(t + 1))
                        copy(m_xTb[u], blocks(4, 128, TK)).then_inc(m_xT.s, 1)
                    if e == 5:
                        act.wait_ge(*m_mx.done(t + 1))
                        nc.scalar.activation(rt[:, u, 8:8 + NE], bank(4, TK, NE), ACT.Exp, bias=rt[:, u, 41:42],
                                             accum_out=rt[:, u, 42:43]).then_inc(m_ex.s, 1)
                    if e == 7:
                        act.wait_ge(*m_cT.done(t + 1))
                        copy(cT[:, :], bank(4, NE, TK)).then_inc(m_cTc.s, 1)
                if prv and e == 7:
                    t = 2 * prv[0] + prv[1]
                    act.wait_ge(*t_K.done(t + 1))
                    copy(KQ[:, :, cols(t)], bank(6, 128, 4 * TK).rearrange("p (c n) -> p c n", c=4))\
                        .then_inc(t_KQ.s, 1)
            experts(act, m_slot)
            act.drain().then_inc(phase, 1)
            act.wait_ge(*ended(4))

            for k in range(NHID):
                act.wait_ge(*l_T.done(k + 1))
                for c in range(C):
                    ins = nc.scalar.activation(w1T[:, c, k * 128:(k + 1) * 128], bank(k % 4, 128, 128, c * 128),
                                               ACT.Copy, scale=vT[:, V_LN2W + c:V_LN2W + c + 1])
                ins.then_inc(l_ev.s, 1)
            for k in range(NHID):
                act.wait_ge(*l_T.done(NHID + k + 1))
                copy(w2T[:, k, :], bank(k % 4, 128, D)).then_inc(l_ev.s, 1)
            act.wait_ge(*f_T.done(1))
            for i in range(2):
                copy(f_wxT[:, 2 * i:2 * i + 2, :], blocks(4 + i, 128, D)).then_inc(f_Tc.s, 1)
            act.drain().then_inc(phase, 1)
            act.wait_ge(*ended(5))
            context(1, C)
            act.drain().then_inc(phase, 1)
            act.wait_ge(*ended(6))
            fold(1, C)
            act.drain().then_inc(phase, 1)
            act.wait_ge(*ended(7))

            def stage_e(j, u):
                t = 2 * j + u
                act.wait_ge(*e_o.free(t))
                copy(e_qsb[u], KQ[:, C:2 * C, cols(t)]).then_inc(e_qs.s, 1)

            def e_gelu(t, pairs):
                for a in range(2 * pairs[0], 2 * pairs[-1] + 2):
                    if a % 2 == 0:
                        act.wait_ge(*e_H.done(4 * t + a // 2 + 1))
                    ins = nc.scalar.activation(e_gb[:, a, :], bank(2 + (a // 2) % 2, 128, TK, (a % 2) * TK),
                                               ACT.Gelu, bias=bm[:, a:a + 1])
                    if a % 2:
                        ins.then_inc(e_g.s, 1)

            def e_step(now, nxt, gs, a, b, c, adds):
                if a:
                    n, u = 2 * a[0] + a[1], a[1]
                    act.wait_ge(*f_o.free(n))
                    act.wait_ge(*g_acc[1].done(adds))
                    copy(f_hsb[u], HT[:, :, cols(n)]).then_inc(f_hs.s, 1)
                if nxt:
                    stage_e(*nxt)
                if now:
                    t = 2 * now[0] + now[1]
                    act.wait_ge(*e_y.free(t))
                    e_gelu(t, (0, 1))
                if b:
                    act.wait_ge(*f_tT.done(2 * b[0] + b[1] + 1))
                    copy(f_xTb, blocks(1, 128, TK)).then_inc(f_xT.s, 1)
                if now:
                    e_gelu(t, (2, 3))
                if c:
                    n = 2 * c[0] + c[1]
                    act.wait_ge(*f_S.done(n + 1))
                    for i in range(4):
                        ins = nc.scalar.activation(KQ[:, i, cols(n)], bank(1, 128, TK, i * TK), ACT.Copy,
                                                   accum_out=f_nrm[:, i, one(n)])
                    ins.then_inc(f_sT.s, 1)
                if nxt:
                    n, w = 2 * nxt[0] + nxt[1], nxt[1]
                    act.wait_ge(*e_T.done(n + 1))
                    copy(e_yTb[w], blocks(0, 128, TK)).then_inc(e_yT.s, 1)
                if b:
                    act.wait_ge(*f_sub.done(2 * b[0] + b[1] + 1))
                    nc.scalar.activation(f_lgb[b[1]], f_lgb[b[1]], ACT.Exp).then_inc(f_exp.s, 1)
            mixed(act, e_step)
            act.drain().then_inc(phase, 1)
            act.wait_ge(*ended(8))

            act.wait_ge(*g_T.done(1))
            for i in range(2):
                copy(s_sT[:, 2 * i:2 * i + 2].rearrange("p a c n -> p (a c n)"), bank(i, 128, 512))\
                    .then_inc(g_Tc.s, 1)
            copy(s_nr, bank(2, 1, INNER)).then_inc(g_Tc.s, 1)
            act.wait_ge(*g_qkv.done(1))
            copy(s_q.rearrange("p a n -> p (a n)"), bank(4, 128, 512)).then_inc(g_qkvc.s, 1)
            copy(s_v.rearrange("p a n -> p (a n)"), bank(6, 128, 512)).then_inc(g_qkvc.s, 1)
            act.wait_ge(*g_sc.done(1))
            for i in range(2):
                copy(s_vw[:, 2 * i:2 * i + 2, :], blocks(i, 128, D)).then_inc(g_vw.s, 1)
            act.wait_ge(*g_mx.done(2))
            for a in range(4):
                ins = nc.scalar.activation(s_ec[:, a, :], bank(7, 128, 64, a * 64), ACT.Exp, scale=64 ** -0.5,
                                           bias=small[:, 36 + a:37 + a], accum_out=small[:, 40 + a:41 + a])
            ins.then_inc(g_ex.s, 1)

            def stage_h(j, u):
                t = 2 * j + u
                act.wait_ge(*h_y.free(t))
                copy(h_ssb[u], KQ[:, :, cols(t)]).then_inc(h_ss.s, 1)
            tiles(act, stage_h)

        @block.vector
        def _(dve):
            v = nc.vector
            for s in (x_off, x_acc, g_acc[0], c_er[0], k_sub, m_x, m_acc, e_h, e_x, f_x, f_lg, h_ob):
                dve.sem_inc(s.s, s.credit)
            v.memset(HT[:, :, :], 0.0)
            v.memset(rt[:, :, :], -1.0)

            once = Steps(dve, dve_steps, 0, passed)
            once.tile(0)

            def plainly(*waits):
                for s, n in waits:
                    dve.wait_ge(s, n)
                dve.sem_inc(passed, 1)

            def moments(st_, i, done, var):
                done(v.bn_stats(st_[:, 0:6], i), plain=True)
                done(v.bn_aggr(st_[:, 6:8], st_[:, 0:6]))
                v.tensor_scalar(st_[:, 7:8], st_[:, 7:8], EPS, None, ALU.add).then_inc(var.s, 1)

            def scaled(st_, o, i, rstd, n):
                dve.wait_ge(*rstd.done(n + 1))
                return v.tensor_scalar(o, i, st_[:, 6:7], st_[:, 8:9], ALU.subtract, ALU.mult)

            def wide(a, n, w):
                return a.rearrange("p (n b) -> p n b", b=1).to_broadcast([a.shape[0], n, w])

            def heads(a, w):
                return a.rearrange("p (h w) -> p h w", w=w)

            def one_hots(layer, h, b):
                g = 2 * h + b
                dve.wait_ge(*g_agg[layer].free(g))
                for k in range(GK):
                    c = g * GK + k
                    if layer == 0:
                        ins = v.tensor_scalar(onehot[:, b, k, :], iota[:, :], dst_r[:, one(c)], w_e[:, one(c)],
                                              ALU.is_equal, ALU.mult)
                    else:
                        ins = v.tensor_scalar(onehot[:, b, k, :], iota[:, :], dst_r[:, one(c)], None, ALU.is_equal)
                ins.then_inc(g_oh[layer].s, 1)

            def add(layer, h, b, at=None):
                g = 2 * h + b
                r = dve.value_load(base[0:1, one(g)], min_val=0, max_val=N - 1)
                dve.wait_ge(*g_agg[layer].done(g + 1))
                dve.wait_ge(*g_acc[layer].done(g))
                o = HT[:, :, bass.ds(r, W)]
                i = bank(6 + b if at is None else at, 128, C * W).rearrange("p (c n) -> p c n", c=C)
                v.tensor_tensor(o, o, i, ALU.add)\
                    .then_inc(g_acc[layer].s, 1)

            def left_out(layer):
                with dve.If(leftover(dve) > 0):
                    with dve.Fori(0, NG) as g:
                        dve.wait_ge(*x_off.done(g * (NW + 1) + layer * NG * (NW + 1)))
                        v.tensor_scalar(x_d[:, :], dst_r[:, bass.ds(g * GK, GK)], FAR, None, ALU.subtract)\
                            .then_inc(x_off.s, 1)
                        with dve.Fori(0, NW) as w:
                            n = g * NW + w + layer * NG * NW
                            dve.wait_ge(*x_off.done(g * (NW + 1) + w + (layer * NG * (NW + 1) + 1)))
                            dve.wait_ge(*x_sum.done(n))
                            for k in range(GK):
                                o, d = onehot[:, 0, k, :], x_d[:, k:k + 1]
                                if layer == 0:
                                    ins = v.tensor_scalar(o, iota[:, :], d, w_e[:, one(g * GK + k)],
                                                          ALU.is_equal, ALU.mult)
                                else:
                                    ins = v.tensor_scalar(o, iota[:, :], d, None, ALU.is_equal)
                            ins.then_inc(x_oh.s, 1)
                            dve.wait_ge(*x_oh.done(n + 1))
                            v.tensor_scalar(x_d[:, :], x_d[:, :], float(W), None, ALU.subtract).then_inc(x_off.s, 1)
                            dve.wait_ge(*x_sum.done(n + 1))
                            dve.wait_ge(*x_acc.done(n))
                            o = HT[:, :, bass.ds(w * W, W)]
                            v.tensor_tensor(o, o, bank(7, 128, C * W).rearrange("p (c n) -> p c n", c=C), ALU.add)\
                                .then_inc(x_acc.s, 1)
                    dve.wait_ge(*x_acc.done((layer + 1) * NG * NW))
                    dve.wait_ge(*x_off.done((layer + 1) * NG * (NW + 1)))

            def next_and(gs, i):
                if there(later(gs[i], 1)):
                    one_hots(1, *later(gs[i], 1))
                add(1, *gs[i], at=5)

            dve.wait_ge(*s_in.done(22))
            v.tensor_copy(e_f[:, 0:2], e_i).then_inc(s_rel.s, 1)
            dve.wait_ge(*s_rel.done(1))
            dve.wait_ge(*s_const.done(6))
            d, d0 = e_f[:, 1], x_low[:, :]
            once.done(v.tensor_tensor(base[:, :], base[:, :], x_lowr, ALU.max))
            once.done(v.tensor_tensor(d0, d0, e_f[:, 1, 0, 0:1], ALU.max))
            v.tensor_scalar(small[0:NG, 56:57], d0, FAR, None, ALU.add)
            once.done(v.tensor_scalar(e_rel, d, d0, None, ALU.subtract))
            once.done(v.tensor_scalar(e_bad, e_rel, 0.0, None, ALU.is_lt))
            once.done(v.scalar_tensor_tensor(out=e_bad, in0=e_rel, scalar=float(W), in1=e_bad, op0=ALU.is_ge,
                                             op1=ALU.max))
            v.scalar_tensor_tensor(out=d, in0=e_bad, scalar=small[0:NG, 56:57], in1=e_rel, op0=ALU.mult, op1=ALU.add)\
                .then_inc(s_rel.s, 1)
            v.tensor_reduce(x_left[:, :], e_bad.rearrange("g k e -> g (k e)"), AX, ALU.add).then_inc(x_n.s, 1)
            for a, o in enumerate((src_i, dst_r, w_e)):
                dve.wait_ge(*s_tT.done(a + 1))
                v.tensor_copy(o[:, :].rearrange("e (g k) -> e g k", k=GK),
                              bank(a, TK, NCH).rearrange("e (k g) -> e g k", k=GK)).then_inc(s_tab.s, 1)
            dve.wait_ge(*s_cnt.done(1))
            v.tensor_copy(x_cnt[:, :], bank(4, 1, 1)).then_inc(s_left.s, 1)
            dve.wait_ge(*s_vT.done(1))
            v.tensor_copy(vT[:, 0:NV], bank(3, 128, NV)).then_inc(s_vTc.s, 1)
            v.tensor_copy(rT[:, :, :], bank(3, 128, C * NE, 64).rearrange("p (c n) -> p c n", c=C))\
                .then_inc(s_vTc.s, 1)
            v.tensor_copy(mvT, bank(3, NM, 128, 256)).then_inc(s_vTc.s, 1)
            dve.wait_ge(*s_vTc.done(1))
            for c in range(C):
                v.tensor_scalar(Wg[:, c, :], Wg[:, c, :], vT[:, V_GPRE + c:V_GPRE + c + 1], float(D) ** 0.5,
                                ALU.mult, ALU.mult)
            v.tensor_scalar(rows[:, 2, :], rows[:, 2, :], float(D) ** 0.5, None, ALU.mult)

            sa = Steps(dve, a_dve, 2, passed)

            def a_step(a, b, c):
                if a:
                    t, u = 2 * a[0] + a[1], a[1]
                    sa.tile(t)
                    moments(st[:, u], tile(X, t), sa.done, a_var)
                    sa.end()
                if b:
                    t, u = 2 * b[0] + b[1], b[1]
                    dve.wait_ge(*a_xT.free(t))
                    dve.wait_ge(*a_sq.free(t))
                    dve.wait_ge(*a_kept.free(t))
                    scaled(st[:, u], a_s[u], tile(X, t), a_rstd, t).then_inc(a_xs.s, 1)
            dve.wait_ge(*s_x.done(NB))
            staged(dve, a_step)
            dve.drain().then_inc(phase, 1)
            dve.wait_ge(*ended(0))
            dve.wait_ge(*a_rr.done(2))

            left_out(0)
            sk, km = Steps(dve, k_dve, 2, passed), Steps(dve, k_mdve, 1, passed)
            one_hots(0, 0, 0)
            dve.wait_ge(*a_st[0].done(T // 2 + 1))
            dve.wait_ge(*a_st[1].done(T // 2))

            def k_step(a, b, c):
                if c:
                    t, u = 2 * c[0] + c[1], c[1]
                    q = heads(k_qb[u], 32)
                    sk.tile(t)
                    dve.wait_ge(*k_exp.done(t + 1))
                    sk.done(v.tensor_reduce(qst[:, u, 4:8], q, AX, ALU.add))
                    sk.done(v.reciprocal(qst[:, u, 8:12], qst[:, u, 4:8]))
                    v.tensor_tensor(q, q, wide(qst[:, u, 8:12], 4, 32), ALU.mult).then_inc(k_q.s, 1)
                    sk.end()
                if b:
                    t, u = 2 * b[0] + b[1], b[1]
                    dve.wait_ge(*k_L.done(t + 1))
                    L = heads(bank(2 + u, TK, 128), 32)
                    km.tile(t)
                    km.done(v.tensor_reduce(qst[:, u, 0:4], L, AX, ALU.max))
                    dve.wait_ge(*k_KQ.free(t))
                    v.tensor_tensor(heads(k_qb[u], 32), L, wide(qst[:, u, 0:4], 4, 32), ALU.subtract)\
                        .then_inc(k_sub.s, 1)
                if c:
                    one_hots(0, *later(c, 1))
                    add(0, *c)
            staged(dve, k_step)
            dve.drain().then_inc(phase, 1)
            dve.wait_ge(*ended(1))

            def context(layer, nk, first):
                for jj in range(nk):
                    once.done(v.tensor_reduce(kmax[:, jj:jj + 1], KQ[:, jj, :], AX, ALU.max))
                if layer == 0:
                    once.done(v.tensor_reduce(small[:, 11:12], mk, AX, ALU.max))
                    once.done(v.tensor_tensor(kmax[:, 0:1], kmax[:, 0:1], small[:, 11:12], ALU.max))
                v.tensor_scalar(nmax[:, 0:nk], kmax[:, 0:nk], -1.0, None, ALU.mult).then_inc(c_max[layer].s, 1)

                def step(g, h0):
                    if layer == 1:
                        dve.wait_ge(*c_G[layer].free(g * nk))
                        for i in range(BT):
                            n = g * BT + i
                            ins = v.tensor_scalar(c_hhb[:, i, :], tile(XN, n), tile(MV, n)[:, 0:1], tile(MV, n)[:, 1:2],
                                                  ALU.subtract, ALU.mult)
                        ins.then_inc(c_hh.s, 1)
                    for jj in range(nk):
                        n = g * nk + jj
                        dve.wait_ge(*c_T[layer].done(n + 1))
                        dve.wait_ge(*c_G[layer].free(n))
                        for b, a, k in ((0, 0, 4), (1, 4, 1)):
                            i = bank(b, TK, k * 128).rearrange("p (a n) -> p a n", n=128)
                            if layer == 0:
                                ins = v.tensor_tensor(c_erb[:, a:a + k, :], i,
                                                      wide(rr[:, bass.ds(g * BT + a, k)], k, 128), ALU.mult)
                            else:
                                ins = v.tensor_copy(c_erb[:, a:a + k, :], i)
                        ins.then_inc(c_er[layer].s, 1)
                        for b in range(2) if nk == 1 else (jj,):
                            q = later((h0, first % 2), b)
                            one_hots(layer, *later(q, 1))
                            add(layer, *q)
                with dve.Fori(0, NB) as g:
                    step(g, g + first // 2)

            context(0, 1, T)
            dve.drain().then_inc(phase, 1)
            dve.wait_ge(*ended(2))

            def fold(layer, nk, scale):
                for jj in range(nk):
                    once.done(v.tensor_reduce(den[:, jj:jj + 1], ksum[:, jj, :], AX, ALU.add))
                    if layer == 0:
                        once.done(v.tensor_tensor(den[:, 0:1], den[:, 0:1], msum, ALU.add))
                    once.done(v.reciprocal(small[:, 24 + jj:25 + jj], den[:, jj:jj + 1]))
                if layer == 0:
                    v.tensor_scalar(o_mkb, mk, small[:, 24:25], None, ALU.mult).then_inc(o_mem.s, 1)
                for jj in range(nk):
                    v.tensor_scalar(o_gb, bank(4 + jj, 128, D), small[:, 24 + jj:25 + jj], None, ALU.mult)\
                        .then_inc(o_v[layer].s, 1)
                    dve.wait_ge(*o_pe[layer].done(3 * jj + 2))
                    if layer == 0:
                        ins = v.tensor_tensor(o_kvb, bank(1, 128, 128), mask32[:, :], ALU.mult)
                    else:
                        ins = v.scalar_tensor_tensor(out=o_kvb, in0=bank(1, 128, 128), scalar=bvc[:, jj:jj + 1],
                                                     in1=mask32[:, :], op0=ALU.add, op1=ALU.mult)
                    ins.then_inc(o_v[layer].s, 1)
                    dve.wait_ge(*o_pe[layer].done(3 * jj + 3))
                    v.tensor_scalar(M[:, jj, :], bank(2, 128, D), scale, None, ALU.mult).then_inc(o_v[layer].s, 1)
            fold(0, 1, 32 ** -0.5)
            dve.drain().then_inc(phase, 1)
            dve.wait_ge(*ended(3))

            dve.wait_ge(*s_w.done(18))
            for i in range(3):
                v.tensor_tensor(heads(r_q[i], 32), heads(mask32[:, :], 32),
                                r_q32[i].rearrange("p (a n) -> p a n", a=1).to_broadcast([128, 4, 32]), ALU.mult)\
                    .then_inc(w_blk.s, 1)
            for a in range(C):
                ins = v.tensor_tensor_reduce(r_jk, r_x[:, a, :], r_b, 1.0, 0.0, ALU.mult, ALU.add,
                                             r_xb0[:, a:a + 1])
                once.done(ins)
            once.done(v.tensor_tensor(r_xb, r_xb0, vT[:, V_BX:V_BX + C], ALU.add))
            v.tensor_copy(r_xbb, wide(r_xb, C, TK))
            v.tensor_copy(r_b3b, wide(vT[:, V_B3:V_B3 + C], C, TK)).then_inc(w_b.s, 1)

            sm, stl = Steps(dve, m_dve, 15, passed), Steps(dve, t_dve, 8, passed)

            def m_early(e, j, u):
                t = 2 * j + u
                n, r, Xt = sm.done, rt[:, u], tile(X, t)
                if e == 1:
                    dve.wait_ge(*m_ss.done(t + 1))
                    v.tensor_scalar(r[:, 40:41], r[:, 40:41], 1e-24, None, ALU.max).then_inc(m_sq.s, 1)
                if e == 0:
                    sm.tile(t)
                    dve.wait_ge(*m_o.done(t + 1))
                    v.tensor_tensor(m_ob, bank(4, TK, D), rows[:, 1, :], ALU.add).then_inc(m_bo.s, 1)
                    v.tensor_tensor(m_gnb, bank(4, TK, D, D), rows[:, 0, :], ALU.add)
                if e == 2:
                    dve.wait_ge(*m_rn.done(t + 1))
                    n(v.scalar_tensor_tensor(out=m_ob, in0=m_ob, scalar=r[:, 43:44], in1=rows[:, 2, :],
                                             op0=ALU.mult, op1=ALU.mult))
                    n(v.scalar_tensor_tensor(out=m_gnb, in0=m_gnb, scalar=0.0, in1=m_ob, op0=ALU.max, op1=ALU.add))
                    n(v.tensor_tensor(Xt, Xt, m_gnb, ALU.add), plain=True)
                    moments(st[:, u], Xt, n, m_var)
                if e == 3:
                    scaled(st[:, u], m_sb[u], Xt, m_rstd, t).then_inc(m_xs.s, 1)
                    dve.wait_ge(*m_xs.done(t + 1))
                    n(v.tensor_tensor(Xt, Xt, m_sb[u], ALU.add))
                if e == 5:
                    dve.wait_ge(*m_r.done(t + 1))
                    v.tensor_reduce(r[:, 41:42], bank(4, TK, NE), AX, ALU.max, negate=True).then_inc(m_mx.s, 1)
                if e == 6:
                    dve.wait_ge(*m_ex.done(t + 1))
                    n(v.reciprocal(r[:, 44:45], r[:, 42:43]))
                    n(v.tensor_scalar(r[:, 8:8 + NE], r[:, 8:8 + NE], r[:, 44:45], None, ALU.mult), plain=True)
                    n(v.max(r[:, 24:32], r[:, 8:8 + NE]))
                    n(v.tensor_copy(r[:, 32:34], r[:, 24:26]))
                    n(v.tensor_tensor(r[:, 45:46], r[:, 24:25], r[:, 25:26], ALU.add))
                    n(v.tensor_scalar(r[:, 45:46], r[:, 45:46], 1e-12, None, ALU.max), plain=True)
                    n(v.match_replace(out=rt2[:, :], in_to_replace=r[:, 32:40], in_values=r[:, 8:22], imm_value=0.0))
                    n(v.reciprocal(r[:, 46:47], r[:, 45:46]))
                    n(v.tensor_tensor(r[:, 0:NE], r[:, 8:8 + NE], rt2[:, 0:NE], ALU.subtract))
                    v.tensor_scalar(r[:, 0:NE], r[:, 0:NE], r[:, 46:47], None, ALU.mult).then_inc(m_c.s, 1)
                    sm.end()

            def m_tail(e, j, u):
                t = 2 * j + u
                n, Xt = stl.done, tile(X, t)
                if e == 0:
                    stl.tile(t)
                    plainly(m_acc.done(NE * t + NE))
                    moments(st2[:, 0], Xt, n, t_var)
                if e == 1:
                    dve.wait_ge(*t_kept.free(t))
                    dve.wait_ge(*t_T.free(2 * t))
                    scaled(st2[:, 0], t_fsb, Xt, t_rstd, 2 * t).then_inc(t_fs.s, 1)
                    plainly(t_fs.done(t + 1))
                    moments(st2[:, 1], t_fsb, n, t_var)
                if e == 2:
                    dve.wait_ge(*t_T.free(2 * t + 1))
                    scaled(st2[:, 1], t_hhb, t_fsb, t_rstd, 2 * t + 1).then_inc(t_hh.s, 1)
                    v.tensor_copy(tile(MV, t), st2[:, 1, 6:9:2])
                if e == 4:
                    dve.wait_ge(*t_A.done(t + 1))
                    dve.wait_ge(*t_st.free(t))
                    v.tensor_tensor(t_prb, bank(6, TK, D, D), rows[:, 3, :], ALU.add).then_inc(t_pr.s, 1)
                    v.tensor_tensor(Xt, Xt, bank(6, TK, D), ALU.add)
                q, qs = heads(t_qkb[:, 0:D], 32), qst[:, u]
                if e == 5:
                    dve.wait_ge(*t_B.done(t + 1))
                    dve.wait_ge(*t_K.free(t))
                    n(v.tensor_tensor(t_qkb, bank(7, TK, 2 * D), bqk[:, :], ALU.add))
                    n(v.tensor_reduce(qs[:, 0:H1], q, AX, ALU.max))
                    v.tensor_tensor(q, q, wide(qs[:, 0:H1], H1, 32), ALU.subtract).then_inc(t_sub.s, 1)
                if e == 6:
                    dve.wait_ge(*t_exp.done(t + 1))
                    n(v.tensor_reduce(qs[:, H1:2 * H1], q, AX, ALU.add))
                    n(v.reciprocal(qs[:, 2 * H1:3 * H1], qs[:, H1:2 * H1]))
                    v.tensor_tensor(q, q, wide(qs[:, 2 * H1:3 * H1], H1, 32), ALU.mult).then_inc(t_q.s, 1)
                    stl.end()

            def m_slot(e, now, nxt, prv, g, adds):
                if prv:
                    m_tail(e, *prv)
                if nxt and e:
                    m_early(e, *nxt)
                if g:
                    if there(later(g, 1)):
                        one_hots(0, *later(g, 1))
                    add(0, *g, at=5)
                if now:
                    t, u = 2 * now[0] + now[1], now[1]
                    Xt = tile(X, t)
                    dve.wait_ge(*m_y.done(NE * t + e + 1))
                    dve.wait_ge(*(m_acc.done(NE * t + e) if e else m_x.done(t + 1)))
                    v.scalar_tensor_tensor(out=Xt, in0=bank(2 + e % 2, TK, D), scalar=rt[:, u, e:e + 1], in1=Xt,
                                           op0=ALU.mult, op1=ALU.add).then_inc(m_acc.s, 1)
                if nxt and e == 0:
                    m_early(e, *nxt)
                if nxt and e == 7:
                    Xt = tile(X, 2 * nxt[0] + nxt[1])
                    dve.wait_ge(*m_b.done(2 * nxt[0] + nxt[1] + 1))
                    v.tensor_tensor(Xt, Xt, bank(4, TK, D), ALU.add).then_inc(m_x.s, 1)
            experts(dve, m_slot)
            dve.drain().then_inc(phase, 1)
            dve.wait_ge(*ended(4))

            once.done(v.memset(HT[:, :, :], 0.0))
            left_out(1)
            dve.wait_ge(*l_row.done(3))
            dve.wait_ge(*l_raw.done(1))
            for k in range(NHID):
                if k:
                    dve.wait_ge(*l_b.done(k))
                v.tensor_tensor_reduce(l_jk, l_rawb[:, k * D:(k + 1) * D], l_bb, 1.0, 0.0, ALU.mult, ALU.add,
                                       bm[:, k:k + 1]).then_inc(l_b.s, 1)
            dve.wait_ge(*l_b.done(NHID))
            v.tensor_tensor(bm, bm, vT[:, V_BM1:V_BM1 + NHID], ALU.add)
            dve.wait_ge(*f_w.done(5))
            once.done(v.memset(f_blkb, 0.0))
            v.tensor_copy(f_blkb[0:64, 0:64], f_raw[0:64])
            v.tensor_copy(f_bxb, wide(vT[:, V_BSX:V_BSX + 4], 4, TK))
            v.tensor_copy(f_blkb[64:128, 64:128], f_raw[64:128]).then_inc(f_blk.s, 1)
            once.done(v.tensor_scalar(f_temp, f_temp, 0.1, 5.0, ALU.max, ALU.min))
            once.done(v.reciprocal(small[:, 44:52], f_temp))
            dve.wait_ge(*f_P.done(1))
            for c in range(C):
                v.tensor_tensor(heads(f_wxs[:, c, :], 64), heads(bank(6 + c, 128, INNER), 64),
                                wide(small[:, 44:52], HS, 64), ALU.mult)
            once.done(v.tensor_tensor(heads(f_bxs[:, :], 64), heads(bank(4, TK, INNER), 64),
                                    f_bsl.rearrange("p (a n) -> p a n", a=1).to_broadcast([TK, HS, 64]), ALU.add))
            once.done(v.tensor_tensor(heads(f_bxs[:, :], 64), heads(f_bxs[:, :], 64),
                                      wide(small[0:TK, 44:52], HS, 64), ALU.mult))
            dve.drain().then_inc(f_ready.s, 1)
            one_hots(1, 0, 0)
            dve.drain().then_inc(phase, 1)
            dve.wait_ge(*ended(5))
            context(1, C, 0)
            dve.drain().then_inc(phase, 1)
            dve.wait_ge(*ended(6))
            fold(1, C, 1.0)
            dve.drain().then_inc(phase, 1)
            dve.wait_ge(*ended(7))

            se = Steps(dve, e_dve, 4, passed)

            sf, sg, sl = Steps(dve, f_dve, 2, passed), Steps(dve, f_sdve, 2, passed), Steps(dve, f_mdve, 1, passed)

            def e_step(now, nxt, gs, a, b, c, adds):
                if a:
                    n, u = 2 * a[0] + a[1], a[1]
                    sf.tile(n)
                    Xt = tile(X, n)
                    dve.wait_ge(*f_o.done(n + 1))
                    v.tensor_tensor(Xt, Xt, bank(1, TK, D), ALU.add).then_inc(f_x.s, 1)
                    plainly(f_x.done(n + 1))
                    moments(st2[:, u], Xt, sf.done, f_var)
                    sf.end()
                if nxt:
                    n, w = 2 * nxt[0] + nxt[1], nxt[1]
                    se.tile(n)
                    dve.wait_ge(*e_o.done(n + 1))
                    se.done(v.tensor_tensor(e_hb[w], bank(0, TK, D), rows[:, 0, :], ALU.add))
                    v.tensor_tensor(e_hb[w], e_hb[w], tile(XN, n), ALU.add).then_inc(e_h.s, 1)
                    plainly(e_h.done(n + 1))
                    moments(st[:, w], e_hb[w], se.done, e_var)
                if now:
                    next_and(gs, 0)
                if c:
                    n, u = 2 * c[0] + c[1], c[1]
                    sg.tile(n)
                    L, q = heads(f_lgb[u], 64), qst[:, u]
                    dve.wait_ge(*f_exp.done(n + 1))
                    sg.done(v.tensor_reduce(q[:, HS:2 * HS], L, AX, ALU.add))
                    sg.done(v.reciprocal(q[:, 2 * HS:3 * HS], q[:, HS:2 * HS]))
                    v.tensor_tensor(L, L, wide(q[:, 2 * HS:3 * HS], HS, 64), ALU.mult).then_inc(f_sw.s, 1)
                    sg.end()
                if nxt:
                    n, w = 2 * nxt[0] + nxt[1], nxt[1]
                    dve.wait_ge(*e_T.free(n))
                    scaled(st[:, w], e_yb[w], e_hb[w], e_rstd, n).then_inc(e_yh.s, 1)
                    se.done(v.tensor_tensor(e_hb[w], e_hb[w], rows[:, 1, :], ALU.add))
                    se.end()
                if b:
                    n, u = 2 * b[0] + b[1], b[1]
                    L, q = heads(f_lgb[u], 64), qst[:, u]
                    dve.wait_ge(*f_L.done(n + 1))
                    dve.wait_ge(*f_tok.free(n))
                    v.tensor_tensor(f_lgb[u], bank(1, TK, INNER), f_bxs[:, :], ALU.add).then_inc(f_lg.s, 1)
                    dve.wait_ge(*f_lg.done(n + 1))
                    sl.tile(n)
                    sl.done(v.tensor_reduce(q[:, 0:HS], L, AX, ALU.max))
                    v.tensor_tensor(L, L, wide(q[:, 0:HS], HS, 64), ALU.subtract).then_inc(f_sub.s, 1)
                if now:
                    t, u = 2 * now[0] + now[1], now[1]
                    next_and(gs, 1)
                    Xt = tile(X, t)
                    v.tensor_tensor(Xt, Xt, e_hb[u], ALU.add).then_inc(e_hx.s, 1)
                    dve.wait_ge(*e_y.done(t + 1))
                    dve.wait_ge(*e_hx.done(t + 1))
                    v.tensor_tensor(Xt, Xt, bank(4, TK, D), ALU.add).then_inc(e_x.s, 1)
                if a:
                    n, u = 2 * a[0] + a[1], a[1]
                    dve.wait_ge(*f_tok.free(n))
                    scaled(st2[:, u], f_xsb[u], tile(X, n), f_rstd, n).then_inc(f_xs.s, 1)
                if now:
                    next_and(gs, 2)
            mixed(dve, e_step)
            dve.drain().then_inc(phase, 1)
            dve.wait_ge(*ended(8))

            once.done(v.tensor_reduce(small[:, 60:64], f_nrm, AX, ALU.add))
            once.done(v.tensor_scalar(small[:, 32:36], small[:, 60:64], 1e-5, None, ALU.add))
            once.done(v.reciprocal(small[:, 52:56], small[:, 32:36]))
            for a in range(4):
                v.tensor_tensor(s_s[:, a, D:PITCH], small[:, 60 + a:61 + a], small[:, 52 + a:53 + a], ALU.mult)
                v.tensor_scalar(s_s[:, a, 0:D], bank(6 + a // 2, 128, D, (a % 2) * D), small[:, 52 + a:53 + a], None,
                                ALU.mult).then_inc(g_s.s, 1)
            once.done(v.memset(g_blkb, 0.0))
            dve.wait_ge(*g_w.done(10))
            v.tensor_copy(g_blkb[0:64, :, 0:64], g_raw[0:64])
            v.tensor_copy(g_blkb[64:128, :, 64:128], g_raw[64:128]).then_inc(g_blk.s, 1)
            once.done(v.memset(s_tb, 0.0))
            once.done(v.memset(s_at, 0.0))
            dve.wait_ge(*g_tok.done(1))
            P3 = bank(3, 128, 512).rearrange("p (a n) -> p a n", a=4)
            for lo in (0, 64):
                for o in (s_tc[lo:lo + 64], s_tb[lo:lo + 64, :, lo:lo + 64]):
                    v.tensor_copy(o, P3[lo:lo + 64, :, lo:lo + 64]).then_inc(g_tokc.s, 1)
            dve.wait_ge(*g_qkv.done(1))
            v.tensor_copy(s_k.rearrange("p a n -> p (a n)"), bank(5, 128, 256)).then_inc(g_kc.s, 1)
            dve.wait_ge(*g_sc.done(1))
            v.tensor_reduce(small[:, 32:36], bank(7, 128, 256).rearrange("p (a n) -> p a n", a=4), AX, ALU.max)\
                .then_inc(g_mx.s, 1)
            dve.wait_ge(*g_mx.done(1))
            v.tensor_scalar(small[:, 36:40], small[:, 32:36], -(64 ** -0.5), None, ALU.mult).then_inc(g_mx.s, 1)
            dve.wait_ge(*g_ex.done(1))
            once.done(v.reciprocal(small[:, 52:56], small[:, 40:44]))
            for lo in (0, 64):
                v.tensor_tensor(s_at[lo:lo + 64, :, lo:lo + 64], s_ec[lo:lo + 64],
                                wide(small[lo:lo + 64, 52:56], 4, 64), ALU.mult).then_inc(g_at.s, 1)
            dve.wait_ge(*g_aT.done(1))
            v.tensor_copy(s_aT.rearrange("p a n -> p (a n)"), bank(2, 128, 512)).then_inc(g_aTc.s, 1)
            dve.wait_ge(*g_M.done(1))
            for i in range(2):
                v.tensor_copy(M2[:, 2 * i:2 * i + 2, :], bank(3 + i, 128, 512).rearrange("p (a n) -> p a n", a=2))\
                    .then_inc(g_Mc.s, 1)

            def h_tile(j, u):
                t = 2 * j + u
                dve.wait_ge(*h_bx.done(t + 1))
                dve.wait_ge(*h_y.done(t + 1))
                dve.wait_ge(*h_st[u].free(j))
                v.tensor_tensor(h_obb[u], tile(X, t), bank(5 + u, TK, D), ALU.add).then_inc(h_ob.s, 1)
            tiles(dve, h_tile)


_INS = ['x', 'src', 'dst', 'edge_weight', 'L0_gnn_W', 'L0_gnn_b', 'L0_mix_w_qkv', 'L0_mix_mem_kv',
        'L0_mix_w_out', 'L0_mix_b_out', 'L0_mix_g_out', 'L0_mix_g_pre', 'L0_ffn_router_w', 'L0_ffn_w1',
        'L0_ffn_b1', 'L0_ffn_w2', 'L0_ffn_b2', 'L1_gnn_w1', 'L1_gnn_w2', 'L1_gnn_w3', 'L1_gnn_b3',
        'L1_mix_ln1_w', 'L1_mix_ln1_b', 'L1_mix_Wx', 'L1_mix_bx', 'L1_mix_Wq', 'L1_mix_Wk', 'L1_mix_Wv',
        'L1_mix_Wo', 'L1_mix_bo', 'L1_mix_ln2_w', 'L1_mix_ln2_b', 'L1_mix_W1', 'L1_mix_b1', 'L1_mix_W2',
        'L1_mix_b2', 'L1_ffn_W_fx', 'L1_ffn_b_fx', 'L1_ffn_W_x', 'L1_ffn_b_x', 'L1_ffn_W_slice',
        'L1_ffn_b_slice', 'L1_ffn_W_q', 'L1_ffn_W_k', 'L1_ffn_W_v', 'L1_ffn_W_out', 'L1_ffn_b_out',
        'L1_ffn_temperature']
_OUTS = [((N, D), 'float32')]


def kernel(**inputs):
    import numpy as _np
    import concourse.bacc as _bacc
    from concourse import mybir as _mybir
    from concourse.bass_utils import run_bass_kernel_spmd as _run

    nc = _bacc.Bacc("TRN2", target_bir_lowering=False, num_devices=1)
    arrays, args = {}, []
    for name in _INS:
        a = _np.ascontiguousarray(inputs[name])
        arrays[f"in_{name}_dram"] = a
        args.append(nc.dram_tensor(f"in_{name}_dram", a.shape, _mybir.dt.from_np(a.dtype), kind="ExternalInput").ap())
    for i, (shape, dtype) in enumerate(_OUTS):
        dt = _mybir.dt.from_np(_np.dtype(dtype))
        args.append(nc.dram_tensor(f"out_{i}_dram", shape, dt, kind="ExternalOutput").ap())
    build(nc, *args)
    r = _run(nc, [arrays], core_ids=[0])
    return r.results[0]["out_0_dram"]
```
